# Optimizing a Trainium2 kernel written in Bass

```python
import numpy as np
import jax
import jax.numpy as jnp

def _softmax(x, axis=-1):
    return jax.nn.softmax(x, axis=axis)

def _gelu(x):
    return jax.nn.gelu(x, approximate=True)

def _silu(x):
    return jax.nn.silu(x)

def _sigmoid(x):
    return jax.nn.sigmoid(x)

def _layernorm(x, axis=-1, eps=1e-05):
    m = jnp.mean(x, axis=axis, keepdims=True)
    v = jnp.var(x, axis=axis, keepdims=True)
    return (x - m) / jnp.sqrt(v + eps)

def _scatter_add(tgt, idx, src, axis=0):
    return tgt.at[idx].add(src)

def _segment_sum(src, seg, n):
    return jax.ops.segment_sum(src, seg, n)
kernel_name = 'mk_flamingo_gated_d2_seqx_r8_8b44d5'

def setup_inputs(seed: int=0):
    np.random.seed(seed)
    _w = jnp.asarray

    def _rec_inputs():
        import jax
        import jax.numpy as jnp
        _rk = jax.random.key(seed)
        x = 0.0003765 + 1 * jax.random.normal(jax.random.fold_in(_rk, 1), (8, 128, 256), jnp.float32)
        _lenS = 128 - jax.random.randint(jax.random.fold_in(_rk, 7), (8,), 0, max(1, 128 // 4) + 1, jnp.int32)
        _lenS2 = 128 - jax.random.randint(jax.random.fold_in(_rk, 8), (8,), 0, max(1, 128 // 4) + 1, jnp.int32)
        _ctx_2048P = jax.random.normal(jax.random.fold_in(_rk, 11), (8, 16, 256), jnp.float32)
        _ctx_2048c = jax.random.dirichlet(jax.random.fold_in(_rk, 511), 0.3 * jnp.ones((16,), jnp.float32), (8, 128))
        _ctx_2048t = jnp.einsum('bsk,bkd->bsd', _ctx_2048c, _ctx_2048P)
        _ctx_2048t = _ctx_2048t * jax.lax.rsqrt(jnp.mean(jnp.square(_ctx_2048t)) + 1e-12) * 0.953939
        ctx_2048 = -0.000292821 + 1.00034 * (_ctx_2048t + 0.3 * jax.random.normal(jax.random.fold_in(_rk, 611), (8, 128, 256), jnp.float32))
        _g = jax.random.normal(jax.random.fold_in(_rk, 9001), (2, 2), jnp.float32)
        _g = jnp.sign(_g) * jnp.maximum(jnp.abs(_g), 1.0) + (_g == 0) * 1.0
        g_xattn = _g[0]
        g_ffn = _g[1]
        return (x, ctx_2048, g_xattn, g_ffn)
    x, ctx_2048, g_xattn, g_ffn = _rec_inputs()

    def _L0_xattn_setup():
        import jax, jax.numpy as jnp
        import numpy as np
        key = jax.random.key(seed)
        k1, k2, k3, k4, k5 = jax.random.split(key, 5)
        B, D_MODEL, L = (2, 128, 256)
        HEAD_DIM = 8
        H = D_MODEL // HEAD_DIM
        return {'k': jax.random.normal(k1, (B, D_MODEL, L), dtype=jnp.float32), 'v': jax.random.normal(k2, (B, D_MODEL, L), dtype=jnp.float32), 'q': jax.random.normal(k3, (B, D_MODEL, L), dtype=jnp.float32), 'ssm_kernel': jax.random.normal(k4, (H, L), dtype=jnp.float32), 'D': jax.random.normal(k5, (H,), dtype=jnp.float32), 'head_dim': HEAD_DIM}
    _L0_xattn_all = _L0_xattn_setup()
    _L0_xattn_in = {k: v for k, v in _L0_xattn_all.items() if k in ('ssm_kernel', 'D')}
    del _L0_xattn_all

    def _L0_ffn_setup():
        import jax, jax.numpy as jnp
        import numpy as np
        B, S, H = (1, 128, 256)
        I = 176
        E = 32
        K = 6
        G = 8
        TG = 3
        NSH = 2
        SCALE = 16.0
        C = 48

        def _moe_forward(x3, gate_w, w_gate_up, w_down, ws_gate_up, ws_down):
            b, s, h = x3.shape
            x = x3.reshape(-1, h)
            T = x.shape[0]
            logits = x @ gate_w.T
            grouped = logits.reshape(T, G, E // G)
            group_scores = jnp.max(grouped, axis=-1)
            _, group_idx = jax.lax.top_k(group_scores, TG)
            group_keep = jnp.zeros((T, G), bool).at[jnp.arange(T)[:, None], group_idx].set(True)
            masked = jnp.where(group_keep[..., None], grouped, 0.0)
            scores = masked.reshape(T, E)
            probs = jax.nn.softmax(scores.astype(jnp.float32), axis=-1)
            topk_w, topk_idx = jax.lax.top_k(probs, K)
            topk_w = topk_w * SCALE
            flat_e = topk_idx.reshape(-1)
            tok_idx = jnp.repeat(jnp.arange(T), K)
            oh = jax.nn.one_hot(flat_e, E, dtype=jnp.int32)
            pos = jnp.take_along_axis(jnp.cumsum(oh, axis=0) - 1, flat_e[:, None], axis=1)[:, 0]
            valid = pos < C
            slot = jnp.where(valid, flat_e * C + pos, E * C)
            buf = jnp.zeros((E * C + 1, h), x.dtype).at[slot].set(x[tok_idx])
            xb = buf[:E * C].reshape(E, C, h)
            gu = jnp.einsum('ech,ehf->ecf', xb, w_gate_up)
            g, u = jnp.split(gu, 2, axis=-1)
            act = jax.nn.silu(g) * u
            yb = jnp.einsum('eci,eih->ech', act, w_down)
            yflat = jnp.concatenate([yb.reshape(E * C, h), jnp.zeros((1, h), yb.dtype)], axis=0)
            y_pairs = yflat[slot].reshape(T, K, h)
            out = jnp.einsum('tk,tkh->th', topk_w.astype(x.dtype), y_pairs)
            gu_s = x @ ws_gate_up
            gs, us = jnp.split(gu_s, 2, axis=-1)
            out = out + jax.nn.silu(gs) * us @ ws_down
            return out.reshape(b, s, h)
        key = jax.random.key(seed)
        ks = jax.random.split(key, 6)
        s = 0.02
        return {'hidden_states': jax.random.normal(ks[0], (B, S, H), jnp.float32), 'gate_w': jax.random.normal(ks[1], (E, H), jnp.float32) * s, 'w_gate_up': jax.random.normal(ks[2], (E, H, 2 * I), jnp.float32) * s, 'w_down': jax.random.normal(ks[3], (E, I, H), jnp.float32) * s, 'ws_gate_up': jax.random.normal(ks[4], (H, 2 * I * NSH), jnp.float32) * s, 'ws_down': jax.random.normal(ks[5], (I * NSH, H), jnp.float32) * s}
    _L0_ffn_all = _L0_ffn_setup()
    _L0_ffn_in = {k: v for k, v in _L0_ffn_all.items() if k in ('gate_w', 'w_gate_up', 'w_down', 'ws_gate_up', 'ws_down')}
    del _L0_ffn_all

    def _L1_xattn_setup():
        import jax, jax.numpy as jnp
        import numpy as np
        B, D, N, H = (4, 128, 256, 16)
        HD = D // H

        def rotate_half(x):
            x1 = x[..., 0::2]
            x2 = x[..., 1::2]
            return jnp.stack((-x2, x1), axis=-1).reshape(x.shape)

        def apply_cached_rotary_emb(freqs, t):
            return t * freqs[0] + rotate_half(t) * freqs[1]
        key = jax.random.key(seed)
        ks = jax.random.split(key, 13)
        s = 1.0 / np.sqrt(D)
        inp = {'query': jax.random.normal(ks[0], (B, D, N), jnp.float32), 'key': jax.random.normal(ks[1], (B, D, N), jnp.float32), 'value': jax.random.normal(ks[2], (B, D, N), jnp.float32), 'encoding': jax.random.normal(ks[3], (2, 1, 1, N, HD), jnp.float32), 'Wq': jax.random.normal(ks[4], (D, D), jnp.float32) * s, 'bq': jax.random.normal(ks[5], (D,), jnp.float32) * s, 'Wk': jax.random.normal(ks[6], (D, D), jnp.float32) * s, 'bk': jax.random.normal(ks[7], (D,), jnp.float32) * s, 'Wv': jax.random.normal(ks[8], (D, D), jnp.float32) * s, 'bv': jax.random.normal(ks[9], (D,), jnp.float32) * s, 'Wm': jax.random.normal(ks[10], (D, D), jnp.float32) * s, 'bm': jax.random.normal(ks[11], (D,), jnp.float32) * s}
        return inp
    _L1_xattn_all = _L1_xattn_setup()
    _L1_xattn_in = {k: v for k, v in _L1_xattn_all.items() if k in ('encoding', 'Wq', 'bq', 'Wk', 'bk', 'Wv', 'bv', 'Wm', 'bm')}
    del _L1_xattn_all

    def _L1_ffn_setup():
        import jax, jax.numpy as jnp
        import numpy as np
        IN_F, OUT_F = (256, 256)
        N_EXPERTS, RANK, TOP_K = (8, 128, 2)
        key = jax.random.key(seed)
        k_x, k_r, k_a, k_b = jax.random.split(key, 4)
        hidden_states = jax.random.normal(k_x, (4, 512, IN_F), dtype=jnp.float32)
        router_w = jax.random.normal(k_r, (IN_F, N_EXPERTS), dtype=jnp.float32) * IN_F ** (-0.5)
        Wa = jax.random.normal(k_a, (N_EXPERTS, IN_F, RANK), dtype=jnp.float32) * IN_F ** (-0.5)
        Wb = jax.random.normal(k_b, (N_EXPERTS, RANK, OUT_F), dtype=jnp.float32) * RANK ** (-0.5)
        return {'hidden_states': hidden_states, 'router_w': router_w, 'Wa': Wa, 'Wb': Wb}
    _L1_ffn_all = _L1_ffn_setup()
    _L1_ffn_in = {k: v for k, v in _L1_ffn_all.items() if k in ('router_w', 'Wa', 'Wb')}
    del _L1_ffn_all
    return {'x': x, 'ctx_2048': ctx_2048, 'g_xattn': g_xattn, 'g_ffn': g_ffn, 'L0_xattn_ssm_kernel': _L0_xattn_in['ssm_kernel'], 'L0_xattn_D': _L0_xattn_in['D'], 'L0_ffn_gate_w': _L0_ffn_in['gate_w'], 'L0_ffn_w_gate_up': _L0_ffn_in['w_gate_up'], 'L0_ffn_w_down': _L0_ffn_in['w_down'], 'L0_ffn_ws_gate_up': _L0_ffn_in['ws_gate_up'], 'L0_ffn_ws_down': _L0_ffn_in['ws_down'], 'L1_xattn_encoding': _L1_xattn_in['encoding'], 'L1_xattn_Wq': _L1_xattn_in['Wq'], 'L1_xattn_bq': _L1_xattn_in['bq'], 'L1_xattn_Wk': _L1_xattn_in['Wk'], 'L1_xattn_bk': _L1_xattn_in['bk'], 'L1_xattn_Wv': _L1_xattn_in['Wv'], 'L1_xattn_bv': _L1_xattn_in['bv'], 'L1_xattn_Wm': _L1_xattn_in['Wm'], 'L1_xattn_bm': _L1_xattn_in['bm'], 'L1_ffn_router_w': _L1_ffn_in['router_w'], 'L1_ffn_Wa': _L1_ffn_in['Wa'], 'L1_ffn_Wb': _L1_ffn_in['Wb']}

def reference(x, ctx_2048, g_xattn, g_ffn, L0_xattn_ssm_kernel, L0_xattn_D, L0_ffn_gate_w, L0_ffn_w_gate_up, L0_ffn_w_down, L0_ffn_ws_gate_up, L0_ffn_ws_down, L1_xattn_encoding, L1_xattn_Wq, L1_xattn_bq, L1_xattn_Wk, L1_xattn_bk, L1_xattn_Wv, L1_xattn_bv, L1_xattn_Wm, L1_xattn_bm, L1_ffn_router_w, L1_ffn_Wa, L1_ffn_Wb):
    import jax
    import jax.numpy as jnp

    def _L0_xattn_ref(k, v, q, ssm_kernel, D, head_dim):
        import jax, jax.numpy as jnp
        import numpy as np
        B, HD, L = k.shape
        H = HD // head_dim
        fft_size = 2 * L
        k_ = k.reshape(B, H, head_dim, L)
        v_ = v.reshape(B, H, head_dim, L)
        q_ = q.reshape(B, H, head_dim, L)
        kv = jnp.einsum('bhil,bhjl->bijhl', k_, v_)
        kv_f = jnp.fft.rfft(kv, n=fft_size)
        kernel_f = jnp.fft.rfft(ssm_kernel, n=fft_size)
        y = jnp.fft.irfft(kv_f * kernel_f, n=fft_size)[..., :L]
        out = y + kv * D[None, None, None, :, None]
        out = jnp.einsum('bijhl,bhil->bjhl', out, q_)
        out = jnp.transpose(out, (0, 2, 1, 3)).reshape(B, H * head_dim, L)
        return out.astype(k.dtype)

    def _L0_ffn_ref(hidden_states, gate_w, w_gate_up, w_down, ws_gate_up, ws_down):
        import jax, jax.numpy as jnp
        import numpy as np
        B, S, H = (1, 128, 256)
        I = 176
        E = 32
        K = 6
        G = 8
        TG = 3
        NSH = 2
        SCALE = 16.0
        C = 48

        def _moe_forward(x3, gate_w, w_gate_up, w_down, ws_gate_up, ws_down):
            b, s, h = x3.shape
            x = x3.reshape(-1, h)
            T = x.shape[0]
            logits = x @ gate_w.T
            grouped = logits.reshape(T, G, E // G)
            group_scores = jnp.max(grouped, axis=-1)
            _, group_idx = jax.lax.top_k(group_scores, TG)
            group_keep = jnp.zeros((T, G), bool).at[jnp.arange(T)[:, None], group_idx].set(True)
            masked = jnp.where(group_keep[..., None], grouped, 0.0)
            scores = masked.reshape(T, E)
            probs = jax.nn.softmax(scores.astype(jnp.float32), axis=-1)
            topk_w, topk_idx = jax.lax.top_k(probs, K)
            topk_w = topk_w * SCALE
            flat_e = topk_idx.reshape(-1)
            tok_idx = jnp.repeat(jnp.arange(T), K)
            oh = jax.nn.one_hot(flat_e, E, dtype=jnp.int32)
            pos = jnp.take_along_axis(jnp.cumsum(oh, axis=0) - 1, flat_e[:, None], axis=1)[:, 0]
            valid = pos < C
            slot = jnp.where(valid, flat_e * C + pos, E * C)
            buf = jnp.zeros((E * C + 1, h), x.dtype).at[slot].set(x[tok_idx])
            xb = buf[:E * C].reshape(E, C, h)
            gu = jnp.einsum('ech,ehf->ecf', xb, w_gate_up)
            g, u = jnp.split(gu, 2, axis=-1)
            act = jax.nn.silu(g) * u
            yb = jnp.einsum('eci,eih->ech', act, w_down)
            yflat = jnp.concatenate([yb.reshape(E * C, h), jnp.zeros((1, h), yb.dtype)], axis=0)
            y_pairs = yflat[slot].reshape(T, K, h)
            out = jnp.einsum('tk,tkh->th', topk_w.astype(x.dtype), y_pairs)
            gu_s = x @ ws_gate_up
            gs, us = jnp.split(gu_s, 2, axis=-1)
            out = out + jax.nn.silu(gs) * us @ ws_down
            return out.reshape(b, s, h)
        return _moe_forward(hidden_states, gate_w, w_gate_up, w_down, ws_gate_up, ws_down)

    def _L1_xattn_ref(query, key, value, encoding, Wq, bq, Wk, bk, Wv, bv, Wm, bm):
        import jax, jax.numpy as jnp
        import numpy as np
        B, D, N, H = (4, 128, 256, 16)
        HD = D // H

        def rotate_half(x):
            x1 = x[..., 0::2]
            x2 = x[..., 1::2]
            return jnp.stack((-x2, x1), axis=-1).reshape(x.shape)

        def apply_cached_rotary_emb(freqs, t):
            return t * freqs[0] + rotate_half(t) * freqs[1]
        b, d_model, n = query.shape

        def proj(W, bias, x):
            return jnp.einsum('oi,bin->bon', W, x) + bias[None, :, None]
        q = proj(Wq, bq, query).reshape(b, HD, H, n)
        k = proj(Wk, bk, key).reshape(b, HD, H, n)
        v = proj(Wv, bv, value).reshape(b, HD, H, n)
        q = jnp.transpose(apply_cached_rotary_emb(encoding, jnp.transpose(q, (0, 2, 3, 1))), (0, 3, 1, 2))
        k = jnp.transpose(apply_cached_rotary_emb(encoding, jnp.transpose(k, (0, 2, 3, 1))), (0, 3, 1, 2))
        scores = jnp.einsum('bdhn,bdhm->bhnm', q, k) / np.float32(np.sqrt(HD))
        prob = jax.nn.softmax(scores, axis=-1)
        x = jnp.einsum('bhnm,bdhm->bdhn', prob, v)
        out = jnp.einsum('oi,bin->bon', Wm, x.reshape(b, d_model, n)) + bm[None, :, None]
        return out

    def _L1_ffn_ref(hidden_states, router_w, Wa, Wb):
        import jax, jax.numpy as jnp
        import numpy as np
        IN_F, OUT_F = (256, 256)
        N_EXPERTS, RANK, TOP_K = (8, 128, 2)
        B, S, D = hidden_states.shape
        x = hidden_states.reshape(-1, D)
        norm = jnp.maximum(jnp.linalg.norm(x, axis=-1, keepdims=True), 1e-12)
        router_logits = x / norm @ router_w
        routing_weights = jax.nn.softmax(router_logits.astype(jnp.float32), axis=-1)
        rw, selected_experts = jax.lax.top_k(routing_weights, TOP_K)
        rw = rw / jnp.sum(rw, axis=-1, keepdims=True)
        rw = rw.astype(hidden_states.dtype)
        combine = jnp.sum(jax.nn.one_hot(selected_experts, N_EXPERTS, dtype=rw.dtype) * rw[..., None], axis=1)
        out = jnp.zeros((x.shape[0], OUT_F), dtype=hidden_states.dtype)
        for e in range(N_EXPERTS):
            out = out + combine[:, e, None] * (x @ Wa[e] @ Wb[e])
        return out.reshape(B, S, OUT_F)
    x = x + jnp.tanh(g_xattn[0]) * _L0_xattn_ref(ctx_2048, ctx_2048, _layernorm(x, axis=-1), L0_xattn_ssm_kernel, L0_xattn_D, 8)
    x = x + jnp.tanh(g_ffn[0]) * _L0_ffn_ref(_layernorm(x, axis=-1), L0_ffn_gate_w, L0_ffn_w_gate_up, L0_ffn_w_down, L0_ffn_ws_gate_up, L0_ffn_ws_down)
    x = x + jnp.tanh(g_xattn[1]) * _L1_xattn_ref(_layernorm(x, axis=-1), ctx_2048, ctx_2048, L1_xattn_encoding, L1_xattn_Wq, L1_xattn_bq, L1_xattn_Wk, L1_xattn_bk, L1_xattn_Wv, L1_xattn_bv, L1_xattn_Wm, L1_xattn_bm)
    x = x + jnp.tanh(g_ffn[1]) * _L1_ffn_ref(_layernorm(x, axis=-1), L1_ffn_router_w, L1_ffn_Wa, L1_ffn_Wb)
    return x

_drawn_inputs = setup_inputs


def setup_inputs(seed=0):
    import zlib

    import numpy as np

    out = dict(_drawn_inputs(seed))
    spreads = {'g_ffn': (-1.0, 0.6)}
    factors = {'L0_ffn_gate_w': 8.0,
     'L0_ffn_w_gate_up': 8.0,
     'L0_ffn_w_down': 8.0,
     'L0_ffn_ws_gate_up': 8.0,
     'L0_ffn_ws_down': 8.0,
     'L1_xattn_encoding': 3.138,
     'L1_xattn_Wq': 3.273,
     'L1_xattn_bq': 8.0,
     'L1_xattn_Wk': 3.188,
     'L1_xattn_bk': 8.0,
     'L1_xattn_Wv': 2.882,
     'L1_xattn_bv': 8.0,
     'L1_xattn_Wm': 2.983,
     'L1_xattn_bm': 29.549,
     'L1_ffn_router_w': 3.147,
     'L1_ffn_Wa': 2.734,
     'L1_ffn_Wb': 2.737}
    for name, (base, spread) in spreads.items():
        noise = np.random.default_rng([zlib.crc32(name.encode()), seed]).standard_normal(out[name].shape)
        drawn = base * np.exp(spread * noise) if base else spread * noise
        out[name] = jnp.asarray(drawn.astype(out[name].dtype))
    for name, factor in factors.items():
        out[name] = (out[name] * factor).astype(out[name].dtype)
    return out
```

```python
from contextlib import ExitStack

import concourse.bass as bass
from concourse import mybir

F32 = mybir.dt.float32
BF16 = mybir.dt.bfloat16
I32 = mybir.dt.int32
ALU = mybir.AluOpType
ACT = mybir.ActivationFunctionType
AX = mybir.AxisListType.X

B, S, L = 8, 128, 256
P = 128
LB = L // P
T = B * S
NH, HD = 16, 8
PAIRS = HD * HD
E0, TOPK0, CAP, NG, TG, INTER = 32, 6, 48, 8, 3, 176
GE = E0 // NG
SCALE0 = 16.0
HI = INTER // 2
SLOTC = 64
KT0 = E0 * SLOTC // P
SH = 2 * INTER
SHF = [(0, 128), (128, 128), (256, 96)]
NRING = 6
E1, RANK, TOPK1 = 8, 128, 2
EPS = 1e-5
TERMS = [(0, 0), (0, 1), (1, 0), (0, 2), (2, 0), (1, 1)]
NT = len(TERMS) * HD
SROWS = NT + 3


def build(nc, x, ctx_in, g_xattn, g_ffn, ssm, dskip, gate_w, wgu, wdn, wsgu, wsdn, enc,
          wq, bq, wk, bk, wv, bv, wm, bm, rw, wa, wb, out):
    es = ExitStack()
    with es:
        def sb(name, shape, dt=F32):
            return es.enter_context(nc.sbuf_tensor(name, shape, dt))

        def sem(name):
            return es.enter_context(nc.semaphore(name))

        kpad_d = nc.dram_tensor("kpad_d", [NH, P + L], F32, kind="Internal")
        rows_d = nc.dram_tensor("rows_d", [T + 1, L], F32, kind="Internal")
        kparts_d = nc.dram_tensor("kparts_d", [3, P, T * 2], BF16, kind="Internal")
        qparts_d = nc.dram_tensor("qparts_d", [3, P, T * 2], BF16, kind="Internal")

        X = sb("X", [P, B, L])
        XN = sb("XN", [P, B, L])
        CTX = sb("CTX", [P, B, L])
        XNT = CTX[:, :, :].rearrange("p b l -> p (b l)").rearrange("p (k t) -> p k t", k=LB)
        R1 = sb("R1", [P, 8192])
        R2 = sb("R2", [P, 16384])
        V9 = sb("V9", [P, LB, B, NH, HD + 1])
        FQ = sb("FQ", [P, 2, L])
        SHW = sb("SHW", [P, LB, 2 * SH])
        SHD = sb("SHD", [P, 3, L])
        SA = sb("SA", [P, 3, T])
        WG = sb("WG", [P, NRING, LB, 2 * INTER])
        WD = sb("WD", [HI, NRING, 2, L])
        IDF = sb("IDF", [P, P])
        IDB = sb("IDB", [P, P], BF16)
        UPB = sb("UPB", [P, P], BF16)
        ONB = sb("ONB", [P, P], BF16)
        WST = R1[:, 0:512].rearrange("p (w n) -> p w n", w=4)
        WT = sb("WT", [P, 4, P])
        PWT = sb("PWT", [P, 2, P])
        BST = R1[0:6, 512:640]
        BT = sb("BT", [P, 6])
        BVB = sb("BVB", [P, P])
        GW = sb("GW", [E0, L])
        GT = sb("GT", [P, LB, E0])
        RW = sb("RW", [P, LB, E1])
        GR = sb("GR", [P, 4])
        TGT = sb("TGT", [P, 4])
        STT = sb("STT", [P, B, 6])
        MV = sb("MV", [P, B, 2])
        RS = sb("RS", [P, B])
        RSA = sb("RSA", [P, B])
        RSB = sb("RSB", [P, B])
        MH = sb("MH", [P, B])
        KPAD = R1[0:NH, 640:640 + P + L]
        DSK = sb("DSK", [NH, 1])
        ZROW = sb("ZROW", [1, L])
        ENC = sb("ENC", [P, LB, 2, HD])
        IOT = sb("IOT", [P, CAP], F32)
        RM = sb("RM", [P, B, E0])
        LTG = sb("LTG", [P, NG, NG])

        PS = es.enter_context(nc.psum_tensor("PS", [P, 8, 512], F32))

        def r2(a, n, pat=None, **kw):
            v = R2[:, a:a + n]
            return v.rearrange(pat, **kw) if pat else v

        KT = r2(0, 2048, "p (k c) -> p k c", k=LB * B)
        QT = r2(2048, 2048, "p (k c) -> p k c", k=LB * B)
        TT = r2(4096, 4096, "p (h l) -> p h l", h=NH)
        KV = r2(8192, 4096, "p (s n) -> p s n", s=4)
        Z = r2(12288, 2048, "p (s n) -> p s n", s=2)
        CR = r2(12288, 2048, "p (b k n) -> p b k n", b=B, k=LB)
        OL = r2(14336, 2048, "p (k c) -> p k c", k=LB * B)
        def rope_views(base):
            return dict(a=base[:, 0:512], b=base[:, 512:1024],
                        parts=base[:, 1024:1792].bitcast(BF16).rearrange("p (s n) -> p s n", s=3))
        KR = rope_views(SA[:, :, :].rearrange("p s n -> p (s n)")[:, 0:1024 + 768])
        EB = SA[:, 2, 0:512].rearrange("p (k f c) -> p k f c", k=LB, f=2)

        OH = R1[:, :].bitcast(BF16).rearrange("p (b e c) -> p b e c", b=B, e=E0)
        OHT = r2(0, 8192).bitcast(BF16).rearrange("p (k t) -> p k t", k=KT0)
        Y = r2(8192, 6144).bitcast(BF16).rearrange("p (k s n) -> p k s n", k=KT0, s=3)
        XG = r2(14336, 1024, "p (s n) -> p s n", s=4)
        XB = r2(15360, 512, "p (s k n) -> p s k n", s=2, k=LB)
        base = [0]

        def small(n, *dims):
            a = base[0]
            base[0] += n
            v = r2(a, n)
            return v
        LG = small(256).rearrange("p (b e) -> p b e", b=B)
        GS = small(64).rearrange("p (b g) -> p b g", b=B)
        C1 = small(512).rearrange("p (b g k) -> p b g k", b=B, g=NG)
        C2 = small(512).rearrange("p (b g k) -> p b g k", b=B, g=NG)
        RK = small(64).rearrange("p (b g) -> p b g", b=B)
        SC = small(256).rearrange("p (b e) -> p b e", b=B)
        M8 = small(64).rearrange("p (b k) -> p b k", b=B)
        SS = small(256).rearrange("p (b e) -> p b e", b=B)
        EX = small(256).rearrange("p (b e) -> p b e", b=B)
        GTR = small(256).rearrange("p (b e) -> p b e", b=B)
        EQ = small(256).rearrange("p (b e) -> p b e", b=B)
        PF = small(256).rearrange("p (b e) -> p b e", b=B)
        CNT = small(8)
        SE = small(8)
        SEL = small(256).rearrange("p (b e) -> p b e", b=B)
        VL = small(256).rearrange("p (b e) -> p b e", b=B)
        PK = sb("PK", [P, B, E0])
        SELB = sb("SELB", [P, B, E0], BF16)
        RH = sb("RH", [P, B, KT0, 8], BF16)
        IX = sb("IX", [P, KT0], I32)
        WS = sb("WS", [P, KT0])
        TH = sb("TH", [P, 2, 256])
        A1 = sb("A1", [P, 512])
        AT = sb("AT", [HI, 2, 2, 2, SLOTC])
        YR = sb("YR", [P, L])
        THS = R2[:, 8192:8192 + 1024].rearrange("p (s n) -> p s n", s=2)
        A1S = R2[:, 9216:9216 + 512]

        KST = R1[:, 0:4096].bitcast(BF16).rearrange("p (s h n) -> p s h n", s=2, h=NH)
        QST = R1[:, 4096:8192].bitcast(BF16).rearrange("p (s h n) -> p s h n", s=2, h=NH)
        QR = rope_views(R2[:, 0:1792])
        PE_ = r2(2048, 2048, "p (s h m n) -> p s h m n", s=2, h=2, m=LB)
        MX = r2(4096, 32, "p (h m) -> p h m", h=NH)
        MXR = r2(4128, 32)
        MS = r2(4160, 48).bitcast(BF16).rearrange("p (s n) -> p s n", s=3)
        MR = r2(4224, 64).bitcast(BF16)
        RO = r2(4288, 32, "p (m h) -> p m h", m=LB)
        ON = r2(4352, 256, "p (m d h) -> p m d h", m=LB, d=HD)
        OT = r2(4608, 256)
        TMP = r2(4864, 256)

        WA = r2(8192, 2048, "p (e k r) -> p e k r", e=E1, k=LB)
        WB = r2(10240, 2048, "p (e n) -> p e n", e=E1)
        CB = r2(12288, 1024, "p (s n) -> p s n", s=2)
        AE = r2(13312, 1024, "p (s n) -> p s n", s=2)
        SQ = r2(14336, 256)
        b4 = [14592]

        def small4(n):
            a = b4[0]
            b4[0] += n
            return r2(a, n)
        NQ = small4(8)
        LG4 = small4(64).rearrange("p (b e) -> p b e", b=B)
        M84 = small4(64).rearrange("p (b e) -> p b e", b=B)
        GT4 = small4(64).rearrange("p (b e) -> p b e", b=B)
        EQ4 = small4(64).rearrange("p (b e) -> p b e", b=B)
        PF4 = small4(64).rearrange("p (b e) -> p b e", b=B)
        EX4 = small4(64).rearrange("p (b e) -> p b e", b=B)
        C4 = small4(8)
        S4 = small4(8)
        RM4 = sb("RM4", [P, B, E1])
        CP = sb("CP", [P, B, 3, E1], BF16)
        CPT = sb("CPT", [3 * E1, T], BF16)
        SELE = sb("SELE", [3 * E1, E1, P], BF16)

        ld_ctx, ld_x, ld_ssm, ld_w, ld_enc, ld_g, ld_sh = (sem(n) for n in (
            "ld_ctx", "ld_x", "ld_ssm", "ld_w", "ld_enc", "ld_g", "ld_sh"))
        ld_exp = [sem(f"ld_exp{i}") for i in range(NRING)]
        kpad_out, ld_tt, const_ok, kpad_ok = (sem(n) for n in ("kpad_out", "ld_tt", "const_ok", "kpad_ok"))
        cr_ok = sem("cr_ok")
        dve_step, act_step, pool_step = sem("dve_step"), sem("act_step"), sem("pool_step")
        job_pe, job_act = sem("job_pe"), sem("job_act")
        kv_ready, conv_done, z_done, ol_done = sem("kv_ready"), sem("conv_done"), sem("z_done"), sem("ol_done")
        kp_pe, kp_free, kp_parts, kp_out = sem("kp_pe"), sem("kp_free"), sem("kp_parts"), sem("kp_out")
        cast_in, cast_out = sem("cast_in"), sem("cast_out")
        enc_ok, f_ok = sem("enc_ok"), sem("f_ok")
        ln_var, ln_pow, ln_ok = sem("ln_var"), sem("ln_pow"), sem("ln_ok")
        ot_pe, ot_x = sem("ot_pe"), sem("ot_x")
        rows_out, zrow_out = sem("rows_out"), sem("zrow_out")
        xt_pe, xt_act = sem("xt_pe"), sem("xt_act")
        lg_pe, ss_ok, ex_ok, selb_ok, pos_pe = (sem(n) for n in ("lg_pe", "ss_ok", "ex_ok", "selb_ok", "pos_pe"))
        sh_pe, sh_th, sh_act = sem("sh_pe"), sem("sh_th"), sem("sh_act")
        oh_ok, oht_pe, oht_ok, ix_pe, ix_ok = (sem(n) for n in ("oh_ok", "oht_pe", "oht_ok", "ix_pe", "ix_ok"))
        xg_in = [sem(f"xg_in{i}") for i in range(4)]
        xb_pe, xb_act, gu_pe, th_ok, at_ok, y_pe, y_ok = (sem(n) for n in (
            "xb_pe", "xb_act", "gu_pe", "th_ok", "at_ok", "y_pe", "y_ok"))
        mo_pe, mo_x = sem("mo_pe"), sem("mo_x")
        qp_pe, qp_free, qp_parts = sem("qp_pe"), sem("qp_free"), sem("qp_parts")
        qp_out = [sem(f"qp_out{c}") for c in range(B // 2)]
        st_in = [sem(f"st_in{s}") for s in range(2)]
        kst_one = sem("kst_one")
        s_pe, s_max, ms_ok, mt_pe, mr_ok = (sem(n) for n in ("s_pe", "s_max", "ms_ok", "mt_pe", "mr_ok"))
        mrow_in, st_pe, p_ok, pv_pe = (sem(n) for n in ("mrow_in", "st_pe", "p_ok", "pv_pe"))
        on_ok, ont_pe, ot_ok, wm_pe, x3_ok = (sem(n) for n in ("on_ok", "ont_pe", "ot_ok", "wm_pe", "x3_ok"))
        ld_ab, c_ok, ct_pe, ct_ok, sele_ok = (sem(n) for n in ("ld_ab", "c_ok", "ct_pe", "ct_ok", "sele_ok"))
        ss4_ok, ex4_ok = sem("ss4_ok"), sem("ex4_ok")
        cb_pe, cb_ok, a_pe, ae_ok, o_pe, o_ok, out_dma = (sem(n) for n in (
            "cb_pe", "cb_ok", "a_pe", "ae_ok", "o_pe", "o_ok", "out_dma"))

        QC = B // 2
        NJ = 16

        block = es.enter_context(nc.Block())

        @block.sync
        def _(sp):
            sp.dma_start(CTX[:, :, :], ctx_in.rearrange("b s l -> s b l")).then_inc(ld_ctx, 16)
            sp.dma_start(KPAD[:, P:P + L], ssm).then_inc(ld_ssm, 16)
            sp.dma_start(DSK[:, :], dskip.rearrange("(h a) -> h a", a=1)).then_inc(ld_ssm, 16)
            sp.dma_start(X[:, :, :], x.rearrange("b s l -> s b l")).then_inc(ld_x, 16)
            sp.wait_ge(kpad_ok, 1)
            sp.dma_start(kpad_d.ap(), KPAD).then_inc(kpad_out, 16)
            sp.wait_ge(kpad_out, 16)
            tap = bass.AP(tensor=kpad_d, offset=1, ap=[[1, P], [P + L, NH], [1, L]])
            sp.dma_start(TT, tap).then_inc(ld_tt, 16)
            for e in range(NRING):
                sp.dma_start(WG[:, e, :, :], wgu[e].rearrange("(k p) f -> p k f", p=P)).then_inc(ld_exp[e], 16)
                sp.dma_start(WD[:, e, :, :], wdn[e].rearrange("(k p) n -> p k n", p=HI)).then_inc(ld_exp[e], 16)
            for c in range(QC):
                sp.wait_ge(kp_parts, c + 1)
                sp.dma_start(kparts_d.ap().rearrange("s p n -> p s n")[:, :, c * 512:c * 512 + 512],
                             KR["parts"]).then_inc(kp_out, 16)
            sp.wait_ge(ln_ok, 2)
            sp.dma_start(rows_d.ap()[1:T + 1, :].rearrange("(b s) l -> s b l", b=B), XN[:, :, :])\
              .then_inc(rows_out, 16)
            for e in range(NRING, E0):
                sp.wait_ge(y_pe, (e - NRING) // 2 + 1)
                sp.dma_start(WG[:, e % NRING, :, :], wgu[e].rearrange("(k p) f -> p k f", p=P))\
                  .then_inc(ld_exp[e % NRING], 16)
                sp.dma_start(WD[:, e % NRING, :, :], wdn[e].rearrange("(k p) n -> p k n", p=HI))\
                  .then_inc(ld_exp[e % NRING], 16)
            sp.wait_ge(mo_x, 4)
            sp.dma_start(WA, wa.rearrange("e (k p) r -> p e k r", p=P)).then_inc(ld_ab, 16)
            sp.dma_start(WB, wb.rearrange("e p n -> p e n")).then_inc(ld_ab, 16)
            sp.wait_ge(kst_one, 1)

            def stack(b):
                if b >= 2:
                    sp.wait_ge(pv_pe, 8 * (b - 1))
                for r, (qp, kp) in enumerate(TERMS):
                    rows = slice(r * HD, r * HD + HD)
                    for dst, src, part in ((KST, kparts_d, kp), (QST, qparts_d, qp)):
                        sp.dma_start(dst[rows, b % 2, :, :],
                                     src.ap()[part].rearrange("(d h) (b n) -> d h b n", h=NH, b=B)[:, :, b, :])\
                          .then_inc(st_in[b % 2], 16)

            def maxrow(b):
                sp.wait_ge(mr_ok, b + 1)
                for s in range(3):
                    sp.dma_start(QST[NT + s:NT + s + 1, b % 2, :, :].rearrange("p h (m n) -> p (h m) n", m=LB),
                                 MR[32 * s:32 * s + 32, :]).then_inc(mrow_in, 16)

            for c in range(QC):
                sp.wait_ge(qp_parts, c + 1)
                sp.dma_start(qparts_d.ap().rearrange("s p n -> p s n")[:, :, c * 512:c * 512 + 512],
                             QR["parts"]).then_inc(qp_out[c], 16)
                if c == 0:
                    sp.wait_ge(kp_out, 16 * QC)
                    sp.wait_ge(qp_out[0], 16)
                    stack(0)
                    stack(1)
            maxrow(0)
            for b in range(B):
                if b + 1 < B:
                    maxrow(b + 1)
                if b + 2 < B:
                    sp.wait_ge(qp_out[(b + 2) // 2], 16)
                    stack(b + 2)
            for c in range(2):
                sp.wait_ge(o_ok, 2 * c + 2)
                sp.dma_start(out.rearrange("b s l -> s b l")[:, 4 * c:4 * c + 4, :], X[:, 4 * c:4 * c + 4, :])\
                  .then_inc(out_dma, 16)
            sp.wait_ge(out_dma, 32)
            sp.wait_ge(zrow_out, 16)

        @block.gpsimd
        def _(pool):
            n = [0]

            def done(ins):
                n[0] += 1
                ins.then_inc(pool_step, 1)
                pool.wait_ge(pool_step, n[0])

            done(pool.memset(IDF[:, :], 0.0))
            done(pool.affine_select(out=IDF[:, :], in_=IDF[:, :], compare_op=ALU.not_equal, fill=1.0,
                                    base=0, pattern=[[-1, P]], channel_multiplier=1))
            pool.tensor_copy(IDB[:, :], IDF[:, :]).then_inc(const_ok, 1)
            for i, w in enumerate((wk, wv, wq, wm)):
                pool.dma_start(WST[:, i, :], w).then_inc(ld_w, 16)
            half = "(a t s) -> a t s"
            for i, v in enumerate((bk, bq)):
                pool.dma_start(BST[2 * i:2 * i + 1, :], v.rearrange("(a n) -> a n", a=1)).then_inc(ld_w, 16)
                src = v.rearrange(half, t=2, s=NH)
                dst = BST[2 * i + 1:2 * i + 2, :].rearrange("p (a t s) -> p a t s", t=2, s=NH)
                for t in range(2):
                    pool.dma_start(dst[:, :, t, :], src[:, 1 - t, :].rearrange("(o a) s -> o a s", o=1))\
                        .then_inc(ld_w, 16)
            pool.dma_start(BST[4:5, :], bv.rearrange("(a n) -> a n", a=1)).then_inc(ld_w, 16)
            pool.dma_start(BST[5:6, :], bm.rearrange("(a n) -> a n", a=1)).then_inc(ld_w, 16)
            pool.dma_start(BVB[:, :], bv.partition_broadcast(P)).then_inc(ld_w, 16)
            pool.dma_start(GW[:, :], gate_w).then_inc(ld_w, 16)
            pool.dma_start(RW[:, :, :], rw.rearrange("(k p) e -> p k e", p=P)).then_inc(ld_w, 16)
            for f in range(2):
                pool.dma_start(ENC[:, :, f, :], enc[f, 0, 0].rearrange("(k p) d -> p k d", p=P)).then_inc(ld_enc, 16)
            pool.dma_start(GR[:, 0:2], g_xattn.partition_broadcast(P)).then_inc(ld_g, 16)
            pool.dma_start(GR[:, 2:4], g_ffn.partition_broadcast(P)).then_inc(ld_g, 16)
            pool.dma_start(SHW[:, :, :], wsgu.rearrange("(k p) f -> p k f", p=P)).then_inc(ld_sh, 16)
            pool.dma_start(SHD[:, 0:2, :], wsdn[0:256, :].rearrange("(k p) n -> p k n", p=P)).then_inc(ld_sh, 16)
            pool.dma_start(SHD[0:96, 2, :], wsdn[256:352, :]).then_inc(ld_sh, 16)
            pool.memset(MH[:, :], -0.5).then_inc(const_ok, 1)

            def root():
                root.k += 1
                pool.wait_ge(ln_var, root.k)
                pool.tensor_tensor(RSB[:, :], RSA[:, :], MH[:, :], ALU.pow).then_inc(ln_pow, 1)
            root.k = 0
            root()
            pool.wait_ge(job_act, 4)
            for h in range(NH):
                if h >= 4:
                    pool.wait_ge(conv_done, h - 3)
                head = KT[:, :, h * HD:h * HD + HD]
                pool.tensor_tensor(KV[:, h % 4, :].rearrange("p (k j i) -> p k j i", j=HD, i=HD),
                                   head.unsqueeze(3).to_broadcast([P, LB * B, HD, HD]),
                                   head.unsqueeze(2).to_broadcast([P, LB * B, HD, HD]),
                                   ALU.mult).then_inc(kv_ready, 1)
                if h == 3:
                    done(pool.memset(UPB[:, :], 0.0))
                    done(pool.affine_select(out=UPB[:, :], in_=UPB[:, :], compare_op=ALU.is_ge, fill=1.0,
                                            base=0, pattern=[[-1, P]], channel_multiplier=1))
                    pool.memset(ONB[:, :], 1.0).then_inc(const_ok, 1)
                    pool.iota(IOT[:, :], [[1, CAP]], base=0, channel_multiplier=0,
                              allow_small_or_imprecise_dtypes=True).then_inc(const_ok, 1)
                if h == 5:
                    done(pool.memset(RM[:, :, :], 1.0))
                    pool.memset(RM[:, :, 0:1], 0.0).then_inc(const_ok, 1)
                    done(pool.memset(RM4[:, :, :], 1.0))
                    pool.memset(RM4[:, :, 0:1], 0.0).then_inc(const_ok, 1)
                    done(pool.memset(LTG[:, :, :], 0.0))
                    pool.affine_select(out=LTG[:, :, :], in_=LTG[:, :, :], compare_op=ALU.is_ge, fill=1.0,
                                       base=0, pattern=[[-1, NG], [1, NG]], channel_multiplier=0)\
                        .then_inc(const_ok, 1)
                if h == 7:
                    pool.iota(RH[:, :, :, 0], [[P, B], [0, KT0]], base=0, channel_multiplier=0,
                              allow_small_or_imprecise_dtypes=True).then_inc(const_ok, 1)
                    pool.iota(RH[:, :, :, 1], [[0, B], [0, KT0]], base=1, channel_multiplier=1,
                              allow_small_or_imprecise_dtypes=True).then_inc(const_ok, 1)
                    done(pool.memset(SELE[:, :, :], 0.0))
                    for s in range(3):
                        done(pool.affine_select(out=SELE[:, :, :], in_=SELE[:, :, :], compare_op=ALU.not_equal,
                                                fill=1.0, base=-s * E1, pattern=[[-1, E1], [0, P]],
                                                channel_multiplier=1))
                    pool.memset(V9[:, :, :, :, HD:HD + 1], 1.0).then_inc(const_ok, 1)
                if h == 9:
                    pool.memset(OH[:, :, :, CAP:SLOTC], 0.0).then_inc(const_ok, 1)
                    done(pool.memset(ZROW[:, :], 0.0))
                    pool.dma_start(rows_d.ap()[0:1, :], ZROW[:, :]).then_inc(zrow_out, 16)
            root()
            pool.wait_ge(ix_ok, 1)
            pool.wait_ge(rows_out, 16)
            pool.wait_ge(zrow_out, 16)
            for k in range(KT0):
                if k >= 4:
                    pool.wait_ge(xb_pe, k - 3)
                pool.indirect_dma_start(XG[:, k % 4, :], None, rows_d.ap(),
                                        bass.IndirectOffsetOnAxis(ap=IX[:, k:k + 1], axis=0))\
                    .then_inc(xg_in[k % 4], 16)
            root()
            pool.wait_ge(oht_pe, KT0)
            pool.wait_ge(ix_pe, 1)
            pool.memset(KST[0:64, :, :, :], 1.0).then_inc(kst_one, 1)
            root()
            root()

        @block.scalar
        def _(act):
            act.wait_ge(ld_g, 32)
            act.activation(TGT[:, :], GR[:, :], ACT.Tanh).then_inc(act_step, 1)
            jn = [0]

            def job(dst, src):
                act.wait_ge(job_pe, jn[0] + 1)
                act.activation(dst, src, ACT.Copy).then_inc(job_act, 1)
                jn[0] += 1

            def bank(i, w=512):
                return PS[:, i, 0:w]

            def casts(parts, a, k, sem_in):
                for s in range(2):
                    act.wait_ge(cast_in, 2 * k + s + 1)
                    act.activation(parts[:, s, :], a, ACT.Copy).then_inc(cast_out, 1)

            for g in range(4):
                job(KT[:, 4 * g:4 * g + 4, :].rearrange("p k c -> p (k c)"), bank(g % 2))
            for g in range(4):
                job(QT[:, 4 * g:4 * g + 4, :].rearrange("p k c -> p (k c)"), bank(g % 2))
            job(WT[:, :, :].rearrange("p k c -> p (k c)"), bank(0))
            job(FQ[:, :, :].rearrange("p f (k n) -> p k f n", k=LB),
                PS[:, 1, :].rearrange("p (k f n) -> p k f n", k=LB, f=2))
            job(BT[:, :], PS[:, 0, 0:6])
            job(GT[:, :, :].rearrange("p k e -> p (k e)"), PS[:, 1, 0:2 * E0])
            act.wait_ge(job_act, 12)
            for i, w in enumerate((0, 2)):
                src = WT[:, w, :].rearrange("p (a t s) -> p a t s", t=2, s=NH)
                dst = PWT[:, i, :].rearrange("p (a t s) -> p a t s", t=2, s=NH)
                for t in range(2):
                    act.activation(dst[:, :, t, :], src[:, :, 1 - t, :], ACT.Copy).then_inc(f_ok, 1)
            for c in range(QC):
                casts(KR["parts"], KR["a"], c, None)
            def turn_in(base):
                for g in range(4):
                    act.wait_ge(xt_pe, base + g + 1)
                    act.activation(XNT[:, g // 2, (g % 2) * 512:(g % 2) * 512 + 512], bank(6 + g % 2), ACT.Copy)\
                        .then_inc(xt_act, 1)
            turn_in(0)

            def shared(u):
                act.wait_ge(sh_pe, u + 1)
                if u >= 2:
                    act.wait_ge(sh_act, u - 1)
                m = SHF[u % 3][1]
                act.activation(THS[0:m, u % 2, :], PS[0:m, 2 + 2 * (u % 2), :], ACT.Tanh, scale=0.5)\
                    .then_inc(sh_th, 1)

            act.wait_ge(ss_ok, 1)
            act.activation(EX, SS, ACT.Exp).then_inc(ex_ok, 1)
            for u in range(6):
                shared(u)
            for k in range(KT0):
                act.wait_ge(xb_pe, k + 1)
                if k >= 2:
                    act.wait_ge(gu_pe, k - 1)
                act.activation(XB[:, k % 2, :, :], PS[:, 1, 0:256], ACT.Copy).then_inc(xb_act, 1)
                act.wait_ge(oht_pe, k + 1)
                act.activation(OHT[:, k, :], PS[:, 6 + k % 2, :].bitcast(BF16), ACT.Copy).then_inc(oht_ok, 1)
                act.wait_ge(gu_pe, k + 1)
                if k >= 2:
                    act.wait_ge(at_ok, k - 1)
                act.activation(TH[0:HI, k % 2, :], PS[0:HI, 2 + k % 2, 0:256], ACT.Tanh, scale=0.5)\
                    .then_inc(th_ok, 1)
            for c in range(QC):
                casts(QR["parts"], QR["a"], QC + c, None)
            sc = 1.0 / float(HD) ** 0.5
            for b in range(B):
                for g in range(NH // 2):
                    G = b * (NH // 2) + g
                    act.wait_ge(st_pe, G + 1)
                    if G >= 2:
                        act.wait_ge(pv_pe, G - 1)
                    act.activation(PE_[:, G % 2].rearrange("p h m n -> p (h m n)"),
                                   PS[:, 2 * (G % 2):2 * (G % 2) + 2, :].rearrange("p a n -> p (a n)"),
                                   ACT.Exp, scale=sc).then_inc(p_ok, 1)
            turn_in(4)
            act.wait_ge(ss4_ok, 1)
            act.activation(EX4, LG4, ACT.Exp).then_inc(ex4_ok, 1)
            act.wait_ge(ct_pe, 1)
            act.activation(CPT[:, :], PS[0:24, 3, :].bitcast(BF16), ACT.Copy).then_inc(ct_ok, 1)
            for u in range(2 * E1):
                act.wait_ge(cb_pe, u + 1)
                if u >= 2:
                    act.wait_ge(ae_ok, u - 1)
                act.activation(CB[:, u % 2, :], bank(6 + u % 2), ACT.Copy).then_inc(cb_ok, 1)

        @block.tensor
        def _(pe):
            def f32r(v):
                return v
            pe.wait_ge(const_ok, 1)
            jn = [0]

            def job(parts, waits=()):
                if jn[0] >= 2:
                    pe.wait_ge(job_act, jn[0] - 1)
                last = None
                for f in parts:
                    last = f(jn[0] % 2)
                last.then_inc(job_pe, 1)
                jn[0] += 1

            def turn(src, off, idn=IDF, m=P):
                w = src.shape[0]
                return lambda bk_: pe.transpose(PS[0:m, bk_, off:off + w], src, idn[0:w, 0:w])

            pe.wait_ge(cr_ok, 1)
            for g in range(4):
                lb, b0 = divmod(4 * g, B)
                job([turn(CR[:, b0 + i, lb, :], i * P) for i in range(4)])
            pe.wait_ge(ln_ok, 1)
            for g in range(4):
                lb, b0 = divmod(4 * g, B)
                job([turn(XN[:, b0 + i, lb * P:lb * P + P], i * P) for i in range(4)])
            pe.wait_ge(ld_w, 16 * 15)
            job([turn(WST[:, i, :], i * P) for i in range(4)])
            pe.wait_ge(enc_ok, 1)
            job([turn(EB[:, k, f, :], (k * 2 + f) * P) for k in range(LB) for f in range(2)])
            job([turn(BST, 0)])
            job([turn(GW[:, k * P:k * P + P], k * E0) for k in range(LB)])

            def conv(h):
                pe.wait_ge(kv_ready, h + 1)
                if h == 0:
                    pe.wait_ge(ld_tt, 16)
                if h >= 2:
                    pe.wait_ge(z_done, h - 1)
                b0 = 2 + 2 * (h % 2)
                pe.matmul(PS[:, b0, :], TT[:, h, 0:P], KV[:, h % 4, 0:512], start=True, stop=True)
                pe.matmul(PS[:, b0 + 1, :], TT[:, h, P:L], KV[:, h % 4, 0:512], start=True, stop=False)
                pe.matmul(PS[:, b0 + 1, :], TT[:, h, 0:P], KV[:, h % 4, 512:1024], start=False, stop=True)\
                    .then_inc(conv_done, 1)

            def rope_mm(c, w, src, k0, sem_pe, sem_free, b0):
                if c >= 1:
                    pe.wait_ge(sem_free, c)
                rhs = src[:, 2 * c:2 * c + 2, :].rearrange("p b n -> p (b n)")
                pe.matmul(PS[:, b0, :], WT[:, w, :], rhs, start=True, stop=True)
                pe.matmul(PS[:, b0 + 1, :], PWT[:, w // 2, :], rhs, start=True, stop=True).then_inc(sem_pe, 1)

            vj = [0]

            def vproj(g):
                lb, b0 = divmod(4 * g, B)
                fs = []
                for i in range(4):
                    fs.append(lambda bk_, i=i: pe.matmul(PS[:, bk_, i * P:i * P + P],
                                                         CTX[:, b0 + i, lb * P:lb * P + P], WT[:, 1, :],
                                                         start=True, stop=True))
                job(fs)

            for h in range(NH):
                conv(h)
                if h == 1:
                    pe.wait_ge(f_ok, 4)
                if 1 <= h and h % 3 == 1 and h // 3 < QC:
                    rope_mm(h // 3, 0, CTX, 0, kp_pe, kp_free, 6)
                if h >= 1 and h % 3 == 2 and h // 3 < 4:
                    vproj(h // 3)
            pe.wait_ge(ol_done, NH)
            for g in range(4):
                pe.wait_ge(z_done, NH)
                for i in range(4):
                    b, lb = 2 * g + i // 2, i % 2
                    last = pe.transpose(PS[:, 2 + g, i * P:i * P + P], OL[:, lb * B + b, :], IDF[:, :])
                last.then_inc(ot_pe, 1)

            def turn_in(base, wait_free):
                for g in range(4):
                    if g >= 2:
                        pe.wait_ge(xt_act, base + g - 1)
                    for i in range(4):
                        t = (g % 2) * 4 + i
                        last = pe.transpose(PS[:, 6 + g % 2, i * P:i * P + P],
                                            XN[:, t, (g // 2) * P:(g // 2) * P + P], IDF[:, :])
                    last.then_inc(xt_pe, 1)

            pe.wait_ge(ln_ok, 2)
            pe.wait_ge(kp_free, QC)
            turn_in(0, None)
            pe.wait_ge(xt_act, 4)
            pe.wait_ge(job_act, NJ)
            for b in range(B):
                for k in range(LB):
                    last = pe.matmul(PS[:, 0, b * E0:b * E0 + E0], XNT[:, k, b * P:b * P + P], GT[:, k, :],
                                     start=(k == 0), stop=(k == 1))
            last.then_inc(lg_pe, 1)
            pe.wait_ge(ld_sh, 48)
            pe.wait_ge(ot_x, 4)

            def shared(u):
                n2, f = divmod(u, 3)
                f0, m = SHF[f]
                if u >= 2:
                    pe.wait_ge(sh_act, u - 1)
                for half in range(2):
                    for k in range(LB):
                        last = pe.matmul(PS[0:m, 2 + 2 * (u % 2) + half, :],
                                         SHW[:, k, half * SH + f0:half * SH + f0 + m],
                                         XNT[:, k, n2 * 512:n2 * 512 + 512], start=(k == 0), stop=(k == 1))
                last.then_inc(sh_pe, 1)

            shared(0)
            shared(1)
            pe.wait_ge(selb_ok, 1)
            pe.wait_ge(const_ok, 3)
            flat = SELB[:, :, :].rearrange("p b e -> p (b e)")
            pe.matmul(PS[:, 1, 0:256], UPB[:, :], flat, start=True, stop=True)
            for k in range(1, B):
                last = pe.matmul(PS[:, 1, k * E0:256], ONB[:, :], flat[:, 0:(B - k) * E0], start=False,
                                 stop=True, skip_group_check=True)
            last.then_inc(pos_pe, 1)
            for u in range(2, 6):
                shared(u)
            pe.wait_ge(oh_ok, B)
            for k in range(KT0):
                for b in range(B):
                    last = pe.matmul(PS[:, 0, k * 8:k * 8 + 8], OH[:, b, 2 * k:2 * k + 2, :].rearrange("p e c -> p (e c)"),
                                     RH[:, b, k, :], start=(b == 0), stop=(b == B - 1))
            last.then_inc(ix_pe, 1)

            def oh_turn(k):
                if k >= 2:
                    pe.wait_ge(oht_ok, k - 1)
                dst = PS[:, 6 + k % 2, :].bitcast(BF16)
                for b in range(B):
                    last = pe.transpose(dst[:, b * P:b * P + P],
                                        OH[:, b, 2 * k:2 * k + 2, :].rearrange("p e c -> p (e c)"), IDB[:, :])
                last.then_inc(oht_pe, 1)

            def xb_turn(k):
                pe.wait_ge(xg_in[k % 4], 16 * (k // 4 + 1))
                if k >= 1:
                    pe.wait_ge(xb_act, k)
                for j in range(LB):
                    last = pe.transpose(PS[:, 1, j * P:j * P + P], XG[:, k % 4, j * P:j * P + P], IDF[:, :])
                last.then_inc(xb_pe, 1)

            def up(k):
                pe.wait_ge(xb_act, k + 1)
                if k >= 2:
                    pe.wait_ge(at_ok, k - 1)
                for eo in range(2):
                    e = 2 * k + eo
                    pe.wait_ge(ld_exp[e % NRING], 32 * (e // NRING + 1))
                    for f in range(4):
                        for j in range(LB):
                            c = f * 128 + eo * SLOTC
                            last = pe.matmul(PS[0:HI, 2 + k % 2, c:c + SLOTC],
                                             WG[:, e % NRING, j, f * HI:f * HI + HI],
                                             XB[:, k % 2, j, eo * SLOTC:eo * SLOTC + SLOTC],
                                             start=(j == 0), stop=(j == 1))
                last.then_inc(gu_pe, 1)

            def down(k):
                pe.wait_ge(at_ok, k + 1)
                if k >= 2:
                    pe.wait_ge(y_ok, k - 1)
                for eo in range(2):
                    e = 2 * k + eo
                    for f in range(2):
                        last = pe.matmul(PS[eo * 64:eo * 64 + 64, 4 + k % 2, 0:256], AT[:, k % 2, f, eo, :],
                                         WD[:, e % NRING, f, :], start=(f == 0), stop=(f == 1))
                last.then_inc(y_pe, 1)

            pe.wait_ge(sh_act, 6)
            oh_turn(0)
            oh_turn(1)
            xb_turn(0)
            for k in range(KT0):
                up(k)
                if k + 1 < KT0:
                    xb_turn(k + 1)
                if k >= 1:
                    down(k - 1)
                if k + 2 < KT0:
                    oh_turn(k + 2)
            down(KT0 - 1)
            pe.wait_ge(oht_ok, KT0)
            pe.wait_ge(th_ok, KT0)
            for b in range(B):
                o = PS[:, b // 2, (b % 2) * L:(b % 2) * L + L]
                for f, (f0, m) in enumerate(SHF):
                    pe.matmul(o, SA[0:m, f, b * P:b * P + P], SHD[0:m, f, :], start=(f == 0), stop=False)
                for k in range(KT0):
                    if b == 0:
                        pe.wait_ge(y_ok, k + 1)
                    for s in range(3):
                        last = pe.matmul(o, OHT[:, k, b * P:b * P + P], Y[:, k, s, :], start=False,
                                         stop=(k == KT0 - 1 and s == 2))
                if b % 2 == 1:
                    last.then_inc(mo_pe, 1)

            pe.wait_ge(ln_ok, 3)
            for c in range(QC):
                rope_mm(c, 2, XN, QC, qp_pe, qp_free, 6)
            pe.wait_ge(qp_free, QC)

            def smax(H):
                b, h = divmod(H, NH)
                if h == 0:
                    pe.wait_ge(st_in[b % 2], 16 * 2 * len(TERMS) * (b // 2 + 1))
                if H >= 2:
                    pe.wait_ge(s_max, H - 1)
                for m in range(LB):
                    last = pe.matmul(PS[:, 4 + H % 2, m * L:m * L + L], QST[0:NT, b % 2, h, m * P:m * P + P],
                                     KST[0:NT, b % 2, h, :], start=True, stop=True)
                last.then_inc(s_pe, 1)

            def maxturn(b):
                pe.wait_ge(ms_ok, b + 1)
                pe.transpose(PS[0:96, 7, 0:64].bitcast(BF16), MS.rearrange("p s n -> p (s n)"), IDB[:, :])\
                    .then_inc(mt_pe, 1)

            def scores(G):
                b, g = divmod(G, NH // 2)
                if g == 0:
                    pe.wait_ge(mrow_in, 48 * (b + 1))
                if G >= 2:
                    pe.wait_ge(p_ok, G - 1)
                for hh in range(2):
                    for m in range(LB):
                        last = pe.matmul(PS[:, 2 * (G % 2) + hh, m * L:m * L + L],
                                         KST[0:SROWS, b % 2, 2 * g + hh, m * P:m * P + P],
                                         QST[0:SROWS, b % 2, 2 * g + hh, :], start=True, stop=True)
                last.then_inc(st_pe, 1)

            def values(G):
                b, g = divmod(G, NH // 2)
                pe.wait_ge(p_ok, G + 1)
                if g == 0 and b >= 1:
                    pe.wait_ge(on_ok, b)
                for hh in range(2):
                    h = 2 * g + hh
                    for n in range(LB):
                        for m in range(LB):
                            c = (n * NH + h) * (HD + 1)
                            last = pe.matmul(PS[:, 6, c:c + HD + 1], PE_[:, G % 2, hh, m, n * P:n * P + P],
                                             V9[:, m, b, h, :], start=(m == 0), stop=(m == 1))
                last.then_inc(pv_pe, 1)

            def outturn(b):
                pe.wait_ge(on_ok, b + 1)
                pe.wait_ge(mr_ok, min(b + 2, B))
                if b >= 1:
                    pe.wait_ge(x3_ok, b)
                for n in range(LB):
                    last = pe.transpose(PS[:, 7, n * P:n * P + P], ON[:, n].rearrange("p d h -> p (d h)"), IDF[:, :])
                last.then_inc(ont_pe, 1)

            def project(b):
                pe.wait_ge(ot_ok, b + 1)
                pe.matmul(PS[:, 7, 256:512], WT[:, 3, :], OT, start=True, stop=True).then_inc(wm_pe, 1)

            for h in range(NH):
                smax(h)
            maxturn(0)
            for b in range(B):
                nxt = b + 1 < B
                q = [(b + 1) * NH + h for h in range(NH)] if nxt else []
                for g in range(NH // 2):
                    G = b * (NH // 2) + g
                    scores(G)
                    for _ in range(3):
                        if q:
                            smax(q.pop(0))
                    if g == 1 and b >= 1:
                        outturn(b - 1)
                    if g >= 1:
                        values(G - 1)
                    if g == 2 and b >= 1:
                        project(b - 1)
                    if g == 6 and nxt:
                        if b >= 1:
                            pe.wait_ge(x3_ok, b)
                        maxturn(b + 1)
                values(b * (NH // 2) + NH // 2 - 1)
            outturn(B - 1)
            project(B - 1)

            pe.wait_ge(ln_ok, 4)
            pe.wait_ge(x3_ok, B)
            turn_in(4, None)
            pe.wait_ge(xt_act, 8)
            for b in range(B):
                for k in range(LB):
                    last = pe.matmul(PS[:, 2, b * E1:b * E1 + E1], XNT[:, k, b * P:b * P + P], RW[:, k, :],
                                     start=(k == 0), stop=(k == 1))
            last.then_inc(lg_pe, 1)
            pe.wait_ge(ld_ab, 32)

            def inner(u):
                c, e = divmod(u, E1)
                if u >= 2:
                    pe.wait_ge(ae_ok, u - 1)
                for k in range(LB):
                    last = pe.matmul(PS[:, 4 + u % 2, :], WA[:, e, k, :], XNT[:, k, c * 512:c * 512 + 512],
                                     start=(k == 0), stop=(k == 1))
                last.then_inc(a_pe, 1)

            def weights(u):
                c, e = divmod(u, E1)
                if u >= 2:
                    pe.wait_ge(cb_ok, u - 1)
                pe.matmul(PS[:, 6 + u % 2, :], SELE[:, e, :], CPT[:, c * 512:c * 512 + 512], start=True,
                          stop=True).then_inc(cb_pe, 1)

            inner(0)
            inner(1)
            pe.wait_ge(c_ok, 1)
            dst = PS[0:3 * E1, 3, :].bitcast(BF16)
            for b in range(B):
                last = pe.transpose(dst[:, b * P:b * P + P], CP[:, b].rearrange("p s e -> p (s e)"), IDB[:, :])
            last.then_inc(ct_pe, 1)
            pe.wait_ge(ct_ok, 1)
            weights(0)
            weights(1)
            for u in range(2 * E1):
                c, e = divmod(u, E1)
                pe.wait_ge(ae_ok, u + 1)
                for t in range(4):
                    last = pe.matmul(PS[:, 2 * c + t // 2, (t % 2) * L:(t % 2) * L + L],
                                     AE[:, u % 2, t * P:t * P + P], WB[:, e, :],
                                     start=(e == 0 and t % 2 == 0), stop=True, skip_group_check=True)
                last.then_inc(o_pe, 1)
                if u + 2 < 2 * E1:
                    inner(u + 2)
                    weights(u + 2)

        @block.vector
        def _(dve):
            n = [0]

            def done(ins):
                n[0] += 1
                ins.then_inc(dve_step, 1)
                dve.wait_ge(dve_step, n[0])

            def bc(v, shape, axis):
                return v.unsqueeze(axis).to_broadcast(shape)

            def layernorm(k):
                for b in range(B):
                    ins = dve.bn_stats(STT[:, b, :], X[:, b, :])
                done(ins)
                for b in range(B):
                    ins = dve.bn_aggr(MV[:, b, :], STT[:, b, :])
                done(ins)
                dve.tensor_scalar(RSA[:, :], MV[:, :, 1], EPS, None, ALU.add).then_inc(ln_var, 1)
                dve.wait_ge(ln_pow, k)
                done(dve.tensor_tensor(RS[:, :], RSB[:, :], RSB[:, :], ALU.mult))
                done(dve.tensor_tensor(RS[:, :], RS[:, :], RSA[:, :], ALU.mult))
                done(dve.tensor_scalar(RS[:, :], RS[:, :], -0.5, 1.5, ALU.mult, ALU.add))
                done(dve.tensor_tensor(RS[:, :], RS[:, :], RSB[:, :], ALU.mult))
                for b in range(B):
                    ins = dve.tensor_scalar(XN[:, b, :], X[:, b, :], MV[:, b, 0:1], RS[:, b:b + 1],
                                            ALU.subtract, ALU.mult)
                ins.then_inc(ln_ok, 1)

            dve.wait_ge(ld_ctx, 16)
            dve.tensor_copy(CR, CTX[:, :, :].rearrange("p b (k n) -> p b k n", k=LB)[:, :, :, ::-1]).then_inc(cr_ok, 1)
            done(dve.memset(KPAD[:, 0:P], 0.0))
            dve.wait_ge(ld_ssm, 32)
            dve.tensor_tensor(KPAD[:, P:P + 1], KPAD[:, P:P + 1], DSK[:, :], ALU.add).then_inc(kpad_ok, 1)
            dve.wait_ge(ld_x, 16)
            dve.wait_ge(const_ok, 2)
            layernorm(1)
            dve.wait_ge(ld_enc, 32)
            even = ENC[:, :, 1, :].rearrange("p k (a t) -> p k a t", t=2)[:, :, :, 0]
            done(dve.tensor_scalar(even, even, -1.0, None, ALU.mult))
            for k in range(LB):
                ins = dve.tensor_copy(EB[:, k].rearrange("p f (d h) -> p f d h", h=NH),
                                      bc(ENC[:, k], [P, 2, HD, NH], 3))
            ins.then_inc(enc_ok, 1)

            def two(v):
                return v.rearrange("p (b n) -> p b n", b=2)

            def rope(c, R, bias, sem_pe, sem_free, sem_parts, out_wait, cast0, b0):
                dve.wait_ge(sem_pe, c + 1)
                if out_wait:
                    out_wait()
                dve.scalar_tensor_tensor(out=two(R["a"]), in0=two(PS[:, b0, :]), scalar=BT[:, bias:bias + 1],
                                         in1=bc(FQ[:, 0, :], [P, 2, L], 1), op0=ALU.add, op1=ALU.mult)
                dve.scalar_tensor_tensor(out=two(R["b"]), in0=two(PS[:, b0 + 1, :]), scalar=BT[:, bias + 1:bias + 2],
                                         in1=bc(FQ[:, 1, :], [P, 2, L], 1), op0=ALU.add, op1=ALU.mult)\
                    .then_inc(sem_free, 1)
                dve.wait_ge(sem_free, c + 1)
                dve.tensor_tensor(R["a"], R["a"], R["b"], ALU.add).then_inc(cast_in, 1)
                dve.wait_ge(cast_out, 2 * cast0 + 1)
                dve.tensor_tensor(R["a"], R["a"], R["parts"][:, 0, :], ALU.subtract).then_inc(cast_in, 1)
                dve.wait_ge(cast_out, 2 * cast0 + 2)
                dve.tensor_tensor(R["parts"][:, 2, :], R["a"], R["parts"][:, 1, :], ALU.subtract)\
                    .then_inc(sem_parts, 1)

            def krope(c):
                if c == 0:
                    dve.wait_ge(job_act, 12)

                def w():
                    if c >= 1:
                        dve.wait_ge(kp_out, 16 * c)
                rope(c, KR, 0, kp_pe, kp_free, kp_parts, w, c, 6)

            def vout(g):
                lb, b0 = divmod(4 * g, B)
                dve.wait_ge(job_pe, 12 + g + 1)
                src = PS[:, g % 2, :].rearrange("p (b c) -> p b c", b=4)
                for i in range(4):
                    ins = dve.tensor_tensor(V9[:, lb, b0 + i, :, 0:HD].rearrange("p h d -> p d h"),
                                            src[:, i, :].rearrange("p (d h) -> p d h", h=NH),
                                            BVB[:, :].rearrange("p (d h) -> p d h", h=NH), ALU.add)
                ins.then_inc(job_act, 1)

            def zmul(h):
                dve.wait_ge(conv_done, h + 1)
                b0 = 2 + 2 * (h % 2)
                zz = Z[:, h % 2, :].rearrange("p (k j i) -> p k j i", j=HD, i=HD)
                yy = PS[:, b0:b0 + 2, :].rearrange("p a n -> p (a n)").rearrange("p (k j i) -> p k j i", j=HD, i=HD)
                dve.tensor_tensor(zz, yy, bc(QT[:, :, h * HD:h * HD + HD], [P, LB * B, HD, HD], 2), ALU.mult)\
                    .then_inc(z_done, 1)
                dve.wait_ge(z_done, h + 1)
                dve.tensor_reduce(OL[:, :, h * HD:h * HD + HD], zz, AX, ALU.add).then_inc(ol_done, 1)

            dve.wait_ge(job_act, 8)
            for h in range(NH):
                zmul(h)
                if 1 <= h and h % 3 == 1 and h // 3 < QC:
                    krope(h // 3)
                if h >= 1 and h % 3 == 2 and h // 3 < 4:
                    vout(h // 3)
            dve.wait_ge(act_step, 1)
            for g in range(4):
                dve.wait_ge(ot_pe, g + 1)
                v = X[:, 2 * g:2 * g + 2, :].rearrange("p b l -> p (b l)")
                ins = dve.scalar_tensor_tensor(out=v, in0=PS[:, 2 + g, :], scalar=TGT[:, 0:1], in1=v,
                                               op0=ALU.mult, op1=ALU.add)
                ins.then_inc(ot_x, 1)
            dve.wait_ge(ot_x, 4)
            layernorm(2)

            dve.wait_ge(lg_pe, 1)
            dve.wait_ge(const_ok, 10)
            done(dve.tensor_copy(LG.rearrange("p b e -> p (b e)"), PS[:, 0, 0:256]))
            done(dve.tensor_reduce(GS, LG.rearrange("p b (g k) -> p b g k", g=NG), AX, ALU.max))
            sh4 = [P, B, NG, NG]
            dve.tensor_tensor(C1, bc(GS, sh4, 2), bc(GS, sh4, 3), ALU.is_gt)
            done(dve.tensor_tensor(C2, bc(GS, sh4, 2), bc(GS, sh4, 3), ALU.is_equal))
            done(dve.tensor_tensor(C2, C2, bc(LTG[:, :, :], sh4, 1), ALU.mult))
            done(dve.tensor_tensor(C1, C1, C2, ALU.add))
            done(dve.tensor_reduce(RK, C1, AX, ALU.add))
            done(dve.tensor_scalar(RK, RK, float(TG), None, ALU.is_lt))
            g4 = "p b (g k) -> p (b g) k"
            done(dve.tensor_tensor(SC.rearrange(g4, k=GE), LG.rearrange(g4, k=GE),
                                   bc(RK.rearrange("p b g -> p (b g)"), [P, B * NG, GE], 2), ALU.mult))
            for b in range(B):
                ins = dve.max(M8[:, b, :], SC[:, b, :])
            done(ins)
            sh3 = [P, B, E0]
            dve.tensor_tensor(SS, SC, bc(M8[:, :, 0], sh3, 2), ALU.subtract).then_inc(ss_ok, 1)
            dve.tensor_tensor(EQ, SC, bc(M8[:, :, TOPK0 - 1], sh3, 2), ALU.is_equal)
            done(dve.tensor_tensor(GTR, SC, bc(M8[:, :, TOPK0 - 1], sh3, 2), ALU.is_gt))
            done(dve.tensor_reduce(CNT, GTR, AX, ALU.add))
            done(dve.tensor_scalar(CNT, CNT, -1.0, float(TOPK0), ALU.mult, ALU.add))
            fl = "p b e -> p (b e)"
            done(dve.tensor_tensor_scan(PF.rearrange(fl), RM[:, :, :].rearrange(fl), EQ.rearrange(fl), 0.0,
                                        ALU.mult, ALU.add))
            done(dve.tensor_tensor(PF, PF, bc(CNT, sh3, 2), ALU.is_le))
            done(dve.tensor_tensor(EQ, EQ, PF, ALU.mult))
            done(dve.tensor_tensor(SEL, GTR, EQ, ALU.add))
            dve.tensor_copy(SELB[:, :, :], SEL).then_inc(selb_ok, 1)
            dve.wait_ge(ex_ok, 1)
            done(dve.tensor_reduce(SE, EX, AX, ALU.add))
            done(dve.reciprocal(SE, SE))
            done(dve.tensor_tensor(EX, EX, bc(SE, sh3, 2), ALU.mult))

            def shared(u):
                n2, f = divmod(u, 3)
                m = SHF[f][1]
                b0 = 2 + 2 * (u % 2)
                dve.wait_ge(sh_th, u + 1)
                if u >= 1:
                    dve.wait_ge(sh_act, u)
                done(dve.scalar_tensor_tensor(out=A1S[0:m, :], in0=THS[0:m, u % 2, :], scalar=1.0,
                                              in1=PS[0:m, b0, :], op0=ALU.add, op1=ALU.mult))
                dve.scalar_tensor_tensor(out=SA[0:m, f, n2 * 512:n2 * 512 + 512], in0=A1S[0:m, :], scalar=0.5,
                                         in1=PS[0:m, b0 + 1, :], op0=ALU.mult, op1=ALU.mult).then_inc(sh_act, 1)

            dve.wait_ge(kp_out, 16 * QC)
            shared(0)
            dve.wait_ge(pos_pe, 1)
            pos = PS[:, 1, 0:256].rearrange("p (b e) -> p b e", b=B)
            done(dve.scalar_tensor_tensor(out=VL.rearrange(fl), in0=PS[:, 1, 0:256], scalar=float(CAP),
                                          in1=SEL.rearrange(fl), op0=ALU.is_lt, op1=ALU.mult))
            done(dve.scalar_tensor_tensor(out=PK[:, :, :].rearrange(fl), in0=PS[:, 1, 0:256], scalar=float(SLOTC),
                                          in1=VL.rearrange(fl), op0=ALU.subtract, op1=ALU.mult))
            done(dve.tensor_scalar(PK[:, :, :], PK[:, :, :], float(SLOTC), None, ALU.add))
            done(dve.scalar_tensor_tensor(out=EX.rearrange(fl), in0=EX.rearrange(fl), scalar=SCALE0,
                                          in1=VL.rearrange(fl), op0=ALU.mult, op1=ALU.mult))
            w4 = EX.rearrange("p b (k e) -> p (b k) e", e=2)

            def rh(s):
                return RH[:, :, :, 2 + 2 * s:4 + 2 * s].rearrange("p b k e -> p (b k) e")
            done(dve.tensor_copy(rh(0), w4))
            done(dve.tensor_tensor(w4, w4, rh(0), ALU.subtract))
            done(dve.tensor_copy(rh(1), w4))
            done(dve.tensor_tensor(rh(2), w4, rh(1), ALU.subtract))
            dve.wait_ge(const_ok, 11)
            for b in range(B):
                dve.tensor_tensor(OH[:, b, :, 0:CAP], bc(PK[:, b, :], [P, E0, CAP], 2),
                                  bc(IOT[:, :], [P, E0, CAP], 1), ALU.is_equal).then_inc(oh_ok, 1)
                if b < 5:
                    shared(b + 1)
            dve.wait_ge(ix_pe, 1)
            ixv = PS[:, 0, 0:KT0 * 8].rearrange("p (k c) -> p k c", c=8)
            done(dve.tensor_copy(WS[:, :], ixv[:, :, 0]))
            dve.tensor_tensor(IX[:, :], WS[:, :], ixv[:, :, 1], ALU.add).then_inc(ix_ok, 1)
            dve.wait_ge(ix_ok, 1)
            for eo in range(2):
                rows = slice(eo * 64, eo * 64 + 64)
                done(dve.tensor_reduce(WS[rows, :],
                                       ixv[rows, :, 2 + eo:8].rearrange("p k c -> p k c")[:, :, 0:5:2], AX, ALU.add))

            def silu(k):
                dve.wait_ge(th_ok, k + 1)
                if k >= 1:
                    dve.wait_ge(at_ok, k)
                if k >= 2:
                    dve.wait_ge(y_pe, k - 1)
                done(dve.scalar_tensor_tensor(out=A1[0:HI, 0:256], in0=TH[0:HI, k % 2, :], scalar=1.0,
                                              in1=PS[0:HI, 2 + k % 2, 0:256], op0=ALU.add, op1=ALU.mult))
                dve.scalar_tensor_tensor(out=AT[:, k % 2].rearrange("p f e c -> p (f e c)"), in0=A1[0:HI, 0:256],
                                         scalar=0.5, in1=PS[0:HI, 2 + k % 2, 256:512], op0=ALU.mult,
                                         op1=ALU.mult).then_inc(at_ok, 1)

            def yout(k):
                dve.wait_ge(y_pe, k + 1)
                if k >= 1:
                    dve.wait_ge(y_ok, k)
                yp = PS[:, 4 + k % 2, 0:256]
                done(dve.tensor_scalar(Y[:, k, 0, :], yp, WS[:, k:k + 1], None, ALU.mult))
                done(dve.scalar_tensor_tensor(out=YR[:, :], in0=yp, scalar=WS[:, k:k + 1], in1=Y[:, k, 0, :],
                                              op0=ALU.mult, op1=ALU.subtract))
                done(dve.tensor_copy(Y[:, k, 1, :], YR[:, :]))
                dve.tensor_tensor(Y[:, k, 2, :], YR[:, :], Y[:, k, 1, :], ALU.subtract).then_inc(y_ok, 1)

            for k in range(KT0):
                silu(k)
                if k >= 1:
                    yout(k - 1)
            yout(KT0 - 1)
            for g in range(4):
                dve.wait_ge(mo_pe, g + 1)
                v = X[:, 2 * g:2 * g + 2, :].rearrange("p b l -> p (b l)")
                dve.scalar_tensor_tensor(out=v, in0=PS[:, g, :], scalar=TGT[:, 2:3], in1=v,
                                         op0=ALU.mult, op1=ALU.add).then_inc(mo_x, 1)
            dve.wait_ge(mo_x, 4)
            dve.wait_ge(rows_out, 16)
            layernorm(3)

            for c in range(QC):
                def w():
                    if c >= 1:
                        dve.wait_ge(qp_out[c - 1], 16)
                rope(c, QR, 2, qp_pe, qp_free, qp_parts, w, QC + c, 6)

            def rowmax(H):
                dve.wait_ge(s_pe, H + 1)
                dve.tensor_reduce(MX[:, H % NH, :], PS[:, 4 + H % 2, :].rearrange("p (m n) -> p m n", m=LB),
                                  AX, ALU.max).then_inc(s_max, 1)

            def maxparts(b):
                dve.wait_ge(s_max, NH * (b + 1))
                if b >= 1:
                    dve.wait_ge(ms_ok, b)
                if b >= 1:
                    dve.wait_ge(mt_pe, b)
                m = MX.rearrange("p h m -> p (h m)")
                done(dve.tensor_scalar(MS[:, 0, :], m, -1.0, None, ALU.mult))
                done(dve.scalar_tensor_tensor(out=MXR, in0=m, scalar=-1.0, in1=MS[:, 0, :], op0=ALU.mult,
                                              op1=ALU.subtract))
                done(dve.tensor_copy(MS[:, 1, :], MXR))
                dve.tensor_tensor(MS[:, 2, :], MXR, MS[:, 1, :], ALU.subtract).then_inc(ms_ok, 1)
                dve.wait_ge(mt_pe, b + 1)
                if b >= 1:
                    dve.wait_ge(mrow_in, 48 * b)
                dve.tensor_copy(MR[0:96, :], PS[0:96, 7, 0:64].bitcast(BF16)).then_inc(mr_ok, 1)

            def normal(b):
                dve.wait_ge(pv_pe, (NH // 2) * (b + 1))
                if b >= 1:
                    dve.wait_ge(ont_pe, b)
                o = PS[:, 6, 0:LB * NH * (HD + 1)].rearrange("p (m h d) -> p m h d", m=LB, h=NH)
                done(dve.reciprocal(RO, o[:, :, :, HD]))
                for m in range(LB):
                    ins = dve.tensor_tensor(ON[:, m], o[:, m, :, 0:HD].rearrange("p h d -> p d h"),
                                            bc(RO[:, m, :], [P, HD, NH], 1), ALU.mult)
                ins.then_inc(on_ok, 1)

            def turned(b):
                dve.wait_ge(ont_pe, b + 1)
                if b >= 1:
                    dve.wait_ge(wm_pe, b)
                dve.tensor_copy(OT, PS[:, 7, 0:256]).then_inc(ot_ok, 1)

            def residual(b):
                dve.wait_ge(wm_pe, b + 1)
                if b >= 1:
                    dve.wait_ge(x3_ok, b)
                done(dve.tensor_scalar(TMP, PS[:, 7, 256:512], BT[:, 5:6], TGT[:, 1:2], ALU.add, ALU.mult))
                dve.tensor_tensor(X[:, b, :], X[:, b, :], TMP, ALU.add).then_inc(x3_ok, 1)

            for h in range(NH):
                rowmax(h)
            maxparts(0)
            for b in range(B):
                q = [(b + 1) * NH + h for h in range(NH)] if b + 1 < B else []
                for g in range(NH // 2):
                    for _ in range(3):
                        if q:
                            rowmax(q.pop(0))
                    if g == 0 and b >= 1:
                        normal(b - 1)
                    if g == 1 and b >= 1:
                        turned(b - 1)
                    if g == 2 and b >= 1:
                        residual(b - 1)
                    if g == 6 and b + 1 < B:
                        maxparts(b + 1)
            normal(B - 1)
            turned(B - 1)
            residual(B - 1)

            dve.wait_ge(x3_ok, B)
            layernorm(4)
            dve.wait_ge(ln_ok, 4)
            for b in range(B):
                done(dve.tensor_tensor_reduce(SQ, XN[:, b, :], XN[:, b, :], 1.0, 0.0, ALU.mult, ALU.add,
                                              NQ[:, b:b + 1]))
            done(dve.tensor_scalar(NQ, NQ, 1e-24, None, ALU.max))
            dve.tensor_copy(RSA[:, :], NQ).then_inc(ln_var, 1)
            dve.wait_ge(ln_pow, 5)
            done(dve.tensor_tensor(RS[:, :], RSB[:, :], RSB[:, :], ALU.mult))
            done(dve.tensor_tensor(RS[:, :], RS[:, :], NQ, ALU.mult))
            done(dve.tensor_scalar(RS[:, :], RS[:, :], -0.5, 1.5, ALU.mult, ALU.add))
            done(dve.tensor_tensor(RS[:, :], RS[:, :], RSB[:, :], ALU.mult))
            dve.wait_ge(lg_pe, 2)
            s8 = [P, B, E1]
            done(dve.tensor_tensor(LG4, PS[:, 2, 0:64].rearrange("p (b e) -> p b e", b=B),
                                   bc(RS[:, :], s8, 2), ALU.mult))
            for b in range(B):
                ins = dve.max(M84[:, b, :], LG4[:, b, :])
            done(ins)
            dve.tensor_tensor(EQ4, LG4, bc(M84[:, :, TOPK1 - 1], s8, 2), ALU.is_equal)
            done(dve.tensor_tensor(GT4, LG4, bc(M84[:, :, TOPK1 - 1], s8, 2), ALU.is_gt))
            dve.tensor_tensor(LG4, LG4, bc(M84[:, :, 0], s8, 2), ALU.subtract).then_inc(ss4_ok, 1)
            done(dve.tensor_reduce(C4, GT4, AX, ALU.add))
            done(dve.tensor_scalar(C4, C4, -1.0, float(TOPK1), ALU.mult, ALU.add))
            done(dve.tensor_tensor_scan(PF4.rearrange(fl), RM4[:, :, :].rearrange(fl), EQ4.rearrange(fl), 0.0,
                                        ALU.mult, ALU.add))
            done(dve.tensor_tensor(PF4, PF4, bc(C4, s8, 2), ALU.is_le))
            done(dve.tensor_tensor(EQ4, EQ4, PF4, ALU.mult))
            done(dve.tensor_tensor(GT4, GT4, EQ4, ALU.add))
            dve.wait_ge(ex4_ok, 1)
            done(dve.tensor_tensor(EX4, EX4, GT4, ALU.mult))
            done(dve.tensor_reduce(S4, EX4, AX, ALU.add))
            done(dve.reciprocal(S4, S4))
            done(dve.tensor_tensor(EX4, EX4, bc(S4, s8, 2), ALU.mult))
            done(dve.tensor_copy(CP[:, :, 0, :], EX4))
            done(dve.tensor_tensor(EX4, EX4, CP[:, :, 0, :], ALU.subtract))
            done(dve.tensor_copy(CP[:, :, 1, :], EX4))
            dve.tensor_tensor(CP[:, :, 2, :], EX4, CP[:, :, 1, :], ALU.subtract).then_inc(c_ok, 1)
            for u in range(2 * E1):
                dve.wait_ge(cb_ok, u + 1)
                dve.wait_ge(a_pe, u + 1)
                if u >= 2:
                    dve.wait_ge(o_pe, u - 1)
                dve.tensor_tensor(AE[:, u % 2, :], PS[:, 4 + u % 2, :], CB[:, u % 2, :], ALU.mult)\
                    .then_inc(ae_ok, 1)
                if u % E1 == E1 - 1:
                    c = u // E1
                    dve.wait_ge(o_pe, E1 * (c + 1))
                    for g in range(2):
                        v = X[:, 4 * c + 2 * g:4 * c + 2 * g + 2, :].rearrange("p b l -> p (b l)")
                        dve.scalar_tensor_tensor(out=v, in0=PS[:, 2 * c + g, :], scalar=TGT[:, 3:4], in1=v,
                                                 op0=ALU.mult, op1=ALU.add).then_inc(o_ok, 1)


_INS = ['x', 'ctx_2048', 'g_xattn', 'g_ffn', 'L0_xattn_ssm_kernel', 'L0_xattn_D', 'L0_ffn_gate_w',
        'L0_ffn_w_gate_up', 'L0_ffn_w_down', 'L0_ffn_ws_gate_up', 'L0_ffn_ws_down', 'L1_xattn_encoding',
        'L1_xattn_Wq', 'L1_xattn_bq', 'L1_xattn_Wk', 'L1_xattn_bk', 'L1_xattn_Wv', 'L1_xattn_bv',
        'L1_xattn_Wm', 'L1_xattn_bm', 'L1_ffn_router_w', 'L1_ffn_Wa', 'L1_ffn_Wb']
_OUTS = [((8, 128, 256), 'float32')]


def kernel(**inputs):
    import numpy as _np
    import concourse.bacc as _bacc
    from concourse import mybir as _mybir
    from concourse.bass_utils import run_bass_kernel_spmd as _run

    nc = _bacc.Bacc("TRN2", target_bir_lowering=False, num_devices=1)
    arrays, args = {}, []
    for name in _INS:
        a = _np.ascontiguousarray(inputs[name])
        arrays[f"in_{name}_dram"] = a
        args.append(nc.dram_tensor(f"in_{name}_dram", a.shape, _mybir.dt.from_np(a.dtype), kind="ExternalInput").ap())
    for i, (shape, dtype) in enumerate(_OUTS):
        dt = _mybir.dt.from_np(_np.dtype(dtype))
        args.append(nc.dram_tensor(f"out_{i}_dram", shape, dt, kind="ExternalOutput").ap())
    build(nc, *args)
    r = _run(nc, [arrays], core_ids=[0])
    return r.results[0]["out_0_dram"]
```

```python
from contextlib import ExitStack

import concourse.bass as bass
from concourse import mybir

F32 = mybir.dt.float32
BF16 = mybir.dt.bfloat16
I32 = mybir.dt.int32
ALU = mybir.AluOpType
ACT = mybir.ActivationFunctionType
AX = mybir.AxisListType.X

B, S, L = 8, 128, 256
P = 128
LB = L // P
T = B * S
NH, HD = 16, 8
PAIRS = HD * HD
E0, TOPK0, CAP, NG, TG, INTER = 32, 6, 48, 8, 3, 176
GE = E0 // NG
SCALE0 = 16.0
HI = INTER // 2
SLOTC = 64
KT0 = E0 * SLOTC // P
SH = 2 * INTER
SHF = [(0, 128), (128, 128), (256, 96)]
NRING = 6
E1, RANK, TOPK1 = 8, 128, 2
EPS = 1e-5
NT = 9 * HD
SROWS = NT + 3
UN = NH // 2
LEAD = 11


def build(nc, x, ctx_in, g_xattn, g_ffn, ssm, dskip, gate_w, wgu, wdn, wsgu, wsdn, enc,
          wq, bq, wk, bk, wv, bv, wm, bm, rw, wa, wb, out):
    es = ExitStack()
    with es:
        def sb(name, shape, dt=F32):
            return es.enter_context(nc.sbuf_tensor(name, shape, dt))

        def sem(name):
            return es.enter_context(nc.semaphore(name))

        kpad_d = nc.dram_tensor("kpad_d", [NH, P + L], F32, kind="Internal")
        rows_d = nc.dram_tensor("rows_d", [T + 1, L], F32, kind="Internal")
        kparts_d = nc.dram_tensor("kparts_d", [3, P, T * 2], BF16, kind="Internal")
        qparts_d = nc.dram_tensor("qparts_d", [5, P, T * 2], BF16, kind="Internal")

        X = sb("X", [P, B, L])
        XN = sb("XN", [P, B, L])
        CTX = sb("CTX", [P, B, L])
        XNT = CTX[:, :, :].rearrange("p b l -> p (b l)").rearrange("p (k t) -> p k t", k=LB)
        R1 = sb("R1", [P, 8192])
        R2 = sb("R2", [P, 16384])
        V9 = sb("V9", [P, LB, B, NH, HD + 1])
        FQ = sb("FQ", [P, 2, L])
        SHW = sb("SHW", [P, LB, 2 * SH])
        SHD = sb("SHD", [P, 3, L])
        SA = sb("SA", [P, 3, T])
        WG = sb("WG", [P, NRING, LB, 2 * INTER])
        WD = sb("WD", [HI, NRING, 2, L])
        IDF = sb("IDF", [P, P])
        IDB = sb("IDB", [P, P], BF16)
        UPB = sb("UPB", [P, P], BF16)
        ONB = sb("ONB", [P, P], BF16)
        WST = R1[:, 0:512].rearrange("p (w n) -> p w n", w=4)
        WT = sb("WT", [P, 4, P])
        PWT = sb("PWT", [P, 2, P])
        BST = R1[0:6, 512:640]
        BT = sb("BT", [P, 6])
        BVB = sb("BVB", [P, P])
        GW = sb("GW", [E0, L])
        GT = sb("GT", [P, LB, E0])
        RW = sb("RW", [P, LB, E1])
        GR = sb("GR", [P, 4])
        TGT = sb("TGT", [P, 4])
        STT = sb("STT", [P, B, 6])
        MV = sb("MV", [P, B, 2])
        RS = sb("RS", [P, B])
        RSA = sb("RSA", [P, B])
        RSB = sb("RSB", [P, B])
        MH = sb("MH", [P, B])
        NQ = sb("NQ", [P, B])
        BMG = sb("BMG", [P, 1])
        KPAD = R1[0:NH, 640:640 + P + L]
        DSK = sb("DSK", [NH, 1])
        ZROW = sb("ZROW", [1, L])
        ENC = sb("ENC", [P, LB, 2, HD])
        IOT = sb("IOT", [P, CAP], F32)
        RM = sb("RM", [P, B, E0])
        LTG = sb("LTG", [P, NG, NG])

        PS = es.enter_context(nc.psum_tensor("PS", [P, 8, 512], F32))

        def r2(a, n, pat=None, **kw):
            v = R2[:, a:a + n]
            return v.rearrange(pat, **kw) if pat else v

        KT = r2(0, 2048, "p (k c) -> p k c", k=LB * B)
        QT = r2(2048, 2048, "p (k c) -> p k c", k=LB * B)
        TT = r2(4096, 4096, "p (h l) -> p h l", h=NH)
        KV = r2(8192, 4096, "p (s n) -> p s n", s=4)
        Z = r2(12288, 2048, "p (s n) -> p s n", s=2)
        CR = r2(12288, 2048, "p (b k n) -> p b k n", b=B, k=LB)
        OL = r2(14336, 2048, "p (k c) -> p k c", k=LB * B)
        def rope_views(base):
            return dict(a=base[:, 0:512], b=base[:, 512:1024],
                        parts=base[:, 1024:1792].bitcast(BF16).rearrange("p (s n) -> p s n", s=3))
        KR = rope_views(SA[:, :, :].rearrange("p s n -> p (s n)")[:, 0:1024 + 768])
        EB = SA[:, 2, 0:512].rearrange("p (k f c) -> p k f c", k=LB, f=2)

        OH = R1[:, :].bitcast(BF16).rearrange("p (b e c) -> p b e c", b=B, e=E0)
        OHT = r2(0, 8192).bitcast(BF16).rearrange("p (k t) -> p k t", k=KT0)
        Y = r2(8192, 6144).bitcast(BF16).rearrange("p (k s n) -> p k s n", k=KT0, s=3)
        XG = r2(14336, 1024, "p (s n) -> p s n", s=4)
        XB = r2(15360, 512, "p (s k n) -> p s k n", s=2, k=LB)
        base = [0]

        def small(n, *dims):
            a = base[0]
            base[0] += n
            v = r2(a, n)
            return v
        LG = small(256).rearrange("p (b e) -> p b e", b=B)
        GS = small(64).rearrange("p (b g) -> p b g", b=B)
        C1 = small(512).rearrange("p (b g k) -> p b g k", b=B, g=NG)
        C2 = small(512).rearrange("p (b g k) -> p b g k", b=B, g=NG)
        RK = small(64).rearrange("p (b g) -> p b g", b=B)
        SC = small(256).rearrange("p (b e) -> p b e", b=B)
        M8 = small(64).rearrange("p (b k) -> p b k", b=B)
        SS = small(256).rearrange("p (b e) -> p b e", b=B)
        EX = small(256).rearrange("p (b e) -> p b e", b=B)
        GTR = small(256).rearrange("p (b e) -> p b e", b=B)
        EQ = small(256).rearrange("p (b e) -> p b e", b=B)
        PF = small(256).rearrange("p (b e) -> p b e", b=B)
        CNT = small(8)
        SE = small(8)
        SEL = small(256).rearrange("p (b e) -> p b e", b=B)
        VL = small(256).rearrange("p (b e) -> p b e", b=B)
        PK = sb("PK", [P, B, E0])
        SELB = sb("SELB", [P, B, E0], BF16)
        RH = sb("RH", [P, B, KT0, 8], BF16)
        IX = sb("IX", [P, KT0], I32)
        WS = sb("WS", [P, KT0])
        TH = sb("TH", [P, 2, 256])
        A1 = sb("A1", [P, 512])
        AT = sb("AT", [HI, 2, 2, 2, SLOTC])
        YR = sb("YR", [P, L])
        THS = R2[:, 8192:8192 + 1024].rearrange("p (s n) -> p s n", s=2)
        A1S = R2[:, 9216:9216 + 512]

        def stacks(r1, r2_):
            return [r1.bitcast(BF16)[:, i * 4096:i * 4096 + 4096].rearrange("p (h n) -> p h n", h=NH)
                    for i in range(2)] + [r2_.bitcast(BF16).rearrange("p (h n) -> p h n", h=NH)]
        KST = stacks(R1[:, 0:4096], r2(8192, 2048))
        QST = stacks(R1[:, 4096:8192], r2(10240, 2048))
        QR = rope_views(R2[:, 0:1792])
        PX = r2(2048, 4096, "p (s h m n) -> p s h m n", s=4, h=2, m=LB)
        MX = r2(6144, 32, "p (h m) -> p h m", h=NH)
        MXR = r2(6176, 32)
        MS = r2(6208, 48).bitcast(BF16).rearrange("p (s n) -> p s n", s=3)
        MR = r2(6272, 64).bitcast(BF16)
        RO = r2(6336, 32, "p (m h) -> p m h", m=LB)
        ON = r2(6400, 256, "p (m d h) -> p m d h", m=LB, d=HD)
        OT = r2(6656, 256)
        TMP = r2(6912, 256)
        SQ = r2(7168, 256)
        OTS = r2(12288, 2048, "p (s q n) -> p s q n", s=2, q=NH // 4)
        V32 = r2(14336, 2048, "p (s m h c) -> p s m h c", s=2, m=LB, h=NH)

        WGF = WG[:, :, :, :].rearrange("p s k f -> p (s k f)")
        WA = WGF[:, 0:2048].rearrange("p (e k r) -> p e k r", e=E1, k=LB)
        WB = WGF[:, 2048:4096].rearrange("p (e n) -> p e n", e=E1)
        CB = r2(12288, 1024, "p (s n) -> p s n", s=2)
        AE = r2(13312, 1024, "p (s n) -> p s n", s=2)
        b4 = [14592]

        def small4(n):
            a = b4[0]
            b4[0] += n
            return r2(a, n)
        LG4 = small4(64).rearrange("p (b e) -> p b e", b=B)
        M84 = small4(64).rearrange("p (b e) -> p b e", b=B)
        GT4 = small4(64).rearrange("p (b e) -> p b e", b=B)
        EQ4 = small4(64).rearrange("p (b e) -> p b e", b=B)
        PF4 = small4(64).rearrange("p (b e) -> p b e", b=B)
        EX4 = small4(64).rearrange("p (b e) -> p b e", b=B)
        C4 = small4(8)
        S4 = small4(8)
        RM4 = sb("RM4", [P, B, E1])
        CP = sb("CP", [P, B, 3, E1], BF16)
        CPT = sb("CPT", [3 * E1, T], BF16)
        SELE = sb("SELE", [3 * E1, E1, P], BF16)

        ld_ctx, ld_x, ld_ssm, ld_w, ld_enc, ld_g, ld_sh = (sem(n) for n in (
            "ld_ctx", "ld_x", "ld_ssm", "ld_w", "ld_enc", "ld_g", "ld_sh"))
        ld_exp = [sem(f"ld_exp{i}") for i in range(NRING)]
        kpad_out, ld_tt, const_ok, kpad_ok = (sem(n) for n in ("kpad_out", "ld_tt", "const_ok", "kpad_ok"))
        cr_ok = sem("cr_ok")
        dve_step, act_step, pool_step = sem("dve_step"), sem("act_step"), sem("pool_step")
        job_pe, job_act = sem("job_pe"), sem("job_act")
        kv_ready, conv_done, z_done, ol_done = sem("kv_ready"), sem("conv_done"), sem("z_done"), sem("ol_done")
        kp_pe, kp_free, kp_parts, kp_out = sem("kp_pe"), sem("kp_free"), sem("kp_parts"), sem("kp_out")
        cast_in, cast_out = sem("cast_in"), sem("cast_out")
        enc_ok, f_ok = sem("enc_ok"), sem("f_ok")
        ln_var, ln_pow, ln_ok = sem("ln_var"), sem("ln_pow"), sem("ln_ok")
        ot_pe, ot_x = sem("ot_pe"), sem("ot_x")
        rows_out, zrow_out = sem("rows_out"), sem("zrow_out")
        xt_pe, xt_act = sem("xt_pe"), sem("xt_act")
        lg_pe, ss_ok, ex_ok, selb_ok, pos_pe = (sem(n) for n in ("lg_pe", "ss_ok", "ex_ok", "selb_ok", "pos_pe"))
        sh_pe, sh_th, sh_act = sem("sh_pe"), sem("sh_th"), sem("sh_act")
        oh_ok, oht_pe, oht_ok, ix_pe, ix_ok = (sem(n) for n in ("oh_ok", "oht_pe", "oht_ok", "ix_pe", "ix_ok"))
        xg_in = [sem(f"xg_in{i}") for i in range(4)]
        xb_pe, xb_act, gu_pe, th_ok, at_ok, y_pe, y_ok = (sem(n) for n in (
            "xb_pe", "xb_act", "gu_pe", "th_ok", "at_ok", "y_pe", "y_ok"))
        mo_pe, mo_x = sem("mo_pe"), sem("mo_x")
        qp_pe, qp_free, qp_parts = sem("qp_pe"), sem("qp_free"), sem("qp_parts")
        qp_out = [sem(f"qp_out{c}") for c in range(B // 2)]
        st_in = [sem(f"st_in{s}") for s in range(3)]
        kst_one = sem("kst_one")
        s_pe, s_max, ms_ok, mt_pe, mr_ok = (sem(n) for n in ("s_pe", "s_max", "ms_ok", "mt_pe", "mr_ok"))
        mrow_in, st_pe, p_ok, pv_pe = (sem(n) for n in ("mrow_in", "st_pe", "p_ok", "pv_pe"))
        on_ok, ont_pe, ot_ok, wm_pe, x3_ok = (sem(n) for n in ("on_ok", "ont_pe", "ot_ok", "wm_pe", "x3_ok"))
        ots_ok, on_pe, tmp_ok, v32_ok, nq_ok, bmg_ok = (sem(n) for n in (
            "ots_ok", "on_pe", "tmp_ok", "v32_ok", "nq_ok", "bmg_ok"))
        ld_ab, c_ok, ct_pe, ct_ok, sele_ok = (sem(n) for n in ("ld_ab", "c_ok", "ct_pe", "ct_ok", "sele_ok"))
        ss4_ok, ex4_ok = sem("ss4_ok"), sem("ex4_ok")
        cb_pe, cb_ok, a_pe, ae_ok, o_pe, o_ok, out_dma = (sem(n) for n in (
            "cb_pe", "cb_ok", "a_pe", "ae_ok", "o_pe", "o_ok", "out_dma"))

        QC = B // 2
        QBANK = (6, 4, 0, 2)
        NJ = 16

        block = es.enter_context(nc.Block())

        @block.sync
        def _(sp):
            sp.dma_start(CTX[:, :, :], ctx_in.rearrange("b s l -> s b l")).then_inc(ld_ctx, 16)
            sp.dma_start(KPAD[:, P:P + L], ssm).then_inc(ld_ssm, 16)
            sp.dma_start(DSK[:, :], dskip.rearrange("(h a) -> h a", a=1)).then_inc(ld_ssm, 16)
            sp.dma_start(X[:, :, :], x.rearrange("b s l -> s b l")).then_inc(ld_x, 16)
            sp.wait_ge(kpad_ok, 1)
            sp.dma_start(kpad_d.ap(), KPAD).then_inc(kpad_out, 16)
            sp.wait_ge(kpad_out, 16)
            tap = bass.AP(tensor=kpad_d, offset=1, ap=[[1, P], [P + L, NH], [1, L]])
            sp.dma_start(TT, tap).then_inc(ld_tt, 16)
            for e in range(NRING):
                sp.dma_start(WG[:, e, :, :], wgu[e].rearrange("(k p) f -> p k f", p=P)).then_inc(ld_exp[e], 16)
                sp.dma_start(WD[:, e, :, :], wdn[e].rearrange("(k p) n -> p k n", p=HI)).then_inc(ld_exp[e], 16)
            for c in range(QC):
                sp.wait_ge(kp_parts, c + 1)
                sp.dma_start(kparts_d.ap().rearrange("s p n -> p s n")[:, :, c * 512:c * 512 + 512],
                             KR["parts"]).then_inc(kp_out, 16)
            sp.wait_ge(ln_ok, 2)
            sp.dma_start(rows_d.ap()[1:T + 1, :].rearrange("(b s) l -> s b l", b=B), XN[:, :, :])\
              .then_inc(rows_out, 16)
            for e in range(NRING, E0):
                sp.wait_ge(y_pe, (e - NRING) // 2 + 1)
                sp.dma_start(WG[:, e % NRING, :, :], wgu[e].rearrange("(k p) f -> p k f", p=P))\
                  .then_inc(ld_exp[e % NRING], 16)
                sp.dma_start(WD[:, e % NRING, :, :], wdn[e].rearrange("(k p) n -> p k n", p=HI))\
                  .then_inc(ld_exp[e % NRING], 16)
            sp.wait_ge(y_pe, KT0)
            sp.dma_start(WA, wa.rearrange("e (k p) r -> p e k r", p=P)).then_inc(ld_ab, 16)
            sp.dma_start(WB, wb.rearrange("e p n -> p e n")).then_inc(ld_ab, 16)
            def stack(b):
                if b >= 3:
                    sp.wait_ge(pv_pe, (NH // 4) * (b - 2))
                else:
                    sp.wait_ge(kst_one, b + 1)
                for r in range(3):
                    rows = slice(3 * HD * r, 3 * HD * r + 3 * HD)
                    for dst, src, part in ((KST, kparts_d, 0), (QST, qparts_d, r)):
                        sp.dma_start(dst[b % 3][rows, :, :],
                                     src.ap()[part:part + 3].rearrange("s (d h) (b n) -> (s d) h b n", h=NH, b=B)[:, :, b, :])\
                          .then_inc(st_in[b % 3], 16)

            def maxrow(b):
                sp.wait_ge(mr_ok, b + 1)
                for s in range(3):
                    sp.dma_start(QST[b % 3][NT + s:NT + s + 1, :, :].rearrange("p h (m n) -> p (h m) n", m=LB),
                                 MR[32 * s:32 * s + 32, :]).then_inc(mrow_in, 16)

            for c in range(QC):
                sp.wait_ge(qp_parts, c + 1)
                cols = slice(c * 512, c * 512 + 512)
                sp.dma_start(qparts_d.ap().rearrange("s p n -> p s n")[:, 0:3, cols], QR["parts"]).then_inc(qp_out[c], 16)
                sp.dma_start(qparts_d.ap().rearrange("s p n -> p s n")[:, 3:5, cols], QR["parts"][:, 0:2, :])\
                  .then_inc(qp_out[c], 16)
                if c == 0:
                    sp.wait_ge(kp_out, 16 * QC)
                if c < 2:
                    sp.wait_ge(qp_out[c], 32)
                    stack(2 * c)
                    if c == 0:
                        stack(1)
            maxrow(0)
            for b in range(B):
                if b + 1 < B:
                    maxrow(b + 1)
                if b + 3 < B:
                    sp.wait_ge(qp_out[(b + 3) // 2], 32)
                    stack(b + 3)
            for c in range(2):
                sp.wait_ge(o_ok, 2 * c + 2)
                sp.dma_start(out.rearrange("b s l -> s b l")[:, 4 * c:4 * c + 4, :], X[:, 4 * c:4 * c + 4, :])\
                  .then_inc(out_dma, 16)
            sp.wait_ge(out_dma, 32)
            sp.wait_ge(zrow_out, 16)

        @block.gpsimd
        def _(pool):
            n = [0]

            def done(ins):
                n[0] += 1
                ins.then_inc(pool_step, 1)
                pool.wait_ge(pool_step, n[0])

            done(pool.memset(IDF[:, :], 0.0))
            done(pool.affine_select(out=IDF[:, :], in_=IDF[:, :], compare_op=ALU.not_equal, fill=1.0,
                                    base=0, pattern=[[-1, P]], channel_multiplier=1))
            pool.tensor_copy(IDB[:, :], IDF[:, :]).then_inc(const_ok, 1)
            pool.memset(MH[:, :], -0.5).then_inc(const_ok, 1)
            pool.dma_start(SHW[:, :, :], wsgu.rearrange("(k p) f -> p k f", p=P)).then_inc(ld_sh, 16)
            pool.dma_start(SHD[:, 0:2, :], wsdn[0:256, :].rearrange("(k p) n -> p k n", p=P)).then_inc(ld_sh, 16)
            pool.dma_start(SHD[0:96, 2, :], wsdn[256:352, :]).then_inc(ld_sh, 16)

            rk = [0]

            def root(a, z):
                rk[0] += 1
                pool.wait_ge(ln_var, rk[0])
                pool.wait_ge(const_ok, 2)
                r, v, t = RSB[:, a:z], RSA[:, a:z], RS[:, a:z]
                done(pool.tensor_tensor(r, v, MH[:, a:z], ALU.pow))
                done(pool.tensor_tensor(t, r, r, ALU.mult))
                done(pool.tensor_tensor(t, t, v, ALU.mult))
                done(pool.tensor_scalar(t, t, -0.5, 1.5, ALU.mult, ALU.add))
                pool.tensor_tensor(t, t, r, ALU.mult).then_inc(ln_pow, 1)
                pool.wait_ge(ln_pow, rk[0])
            root(0, B)
            pool.wait_ge(job_act, 4)
            for h in range(NH):
                if h >= 4:
                    pool.wait_ge(conv_done, h - 3)
                head = KT[:, :, h * HD:h * HD + HD]
                pool.tensor_tensor(KV[:, h % 4, :].rearrange("p (k j i) -> p k j i", j=HD, i=HD),
                                   head.unsqueeze(3).to_broadcast([P, LB * B, HD, HD]),
                                   head.unsqueeze(2).to_broadcast([P, LB * B, HD, HD]),
                                   ALU.mult).then_inc(kv_ready, 1)
                if h == 3:
                    done(pool.memset(UPB[:, :], 0.0))
                    done(pool.affine_select(out=UPB[:, :], in_=UPB[:, :], compare_op=ALU.is_ge, fill=1.0,
                                            base=0, pattern=[[-1, P]], channel_multiplier=1))
                    pool.memset(ONB[:, :], 1.0).then_inc(const_ok, 1)
                    pool.iota(IOT[:, :], [[1, CAP]], base=0, channel_multiplier=0,
                              allow_small_or_imprecise_dtypes=True).then_inc(const_ok, 1)
                if h == 5:
                    done(pool.memset(RM[:, :, :], 1.0))
                    pool.memset(RM[:, :, 0:1], 0.0).then_inc(const_ok, 1)
                    done(pool.memset(RM4[:, :, :], 1.0))
                    pool.memset(RM4[:, :, 0:1], 0.0).then_inc(const_ok, 1)
                    done(pool.memset(LTG[:, :, :], 0.0))
                    pool.affine_select(out=LTG[:, :, :], in_=LTG[:, :, :], compare_op=ALU.is_ge, fill=1.0,
                                       base=0, pattern=[[-1, NG], [1, NG]], channel_multiplier=0)\
                        .then_inc(const_ok, 1)
                if h == 7:
                    pool.iota(RH[:, :, :, 0], [[P, B], [0, KT0]], base=0, channel_multiplier=0,
                              allow_small_or_imprecise_dtypes=True).then_inc(const_ok, 1)
                    pool.iota(RH[:, :, :, 1], [[0, B], [0, KT0]], base=1, channel_multiplier=1,
                              allow_small_or_imprecise_dtypes=True).then_inc(const_ok, 1)
                    done(pool.memset(SELE[:, :, :], 0.0))
                    for s in range(3):
                        done(pool.affine_select(out=SELE[:, :, :], in_=SELE[:, :, :], compare_op=ALU.not_equal,
                                                fill=1.0, base=-s * E1, pattern=[[-1, E1], [0, P]],
                                                channel_multiplier=1))
                    pool.memset(V9[:, :, :, :, HD:HD + 1], 1.0).then_inc(const_ok, 1)
                if h == 9:
                    pool.memset(OH[:, :, :, CAP:SLOTC], 0.0).then_inc(const_ok, 1)
                    done(pool.memset(ZROW[:, :], 0.0))
                    pool.dma_start(rows_d.ap()[0:1, :], ZROW[:, :]).then_inc(zrow_out, 16)
            root(0, B)
            pool.wait_ge(ix_ok, 1)
            pool.wait_ge(rows_out, 16)
            pool.wait_ge(zrow_out, 16)
            for k in range(KT0):
                if k >= 4:
                    pool.wait_ge(xb_pe, k - 3)
                pool.indirect_dma_start(XG[:, k % 4, :], None, rows_d.ap(),
                                        bass.IndirectOffsetOnAxis(ap=IX[:, k:k + 1], axis=0))\
                    .then_inc(xg_in[k % 4], 16)
            pool.wait_ge(oht_pe, KT0)
            pool.wait_ge(ix_pe, 1)
            for i in range(2):
                pool.memset(KST[i][64:96, :, :], 1.0).then_inc(kst_one, 1)
                pool.wait_ge(kst_one, i + 1)
            for c in range(QC):
                root(2 * c, 2 * c + 2)
                if c == QC - 1:
                    pool.memset(KST[2][64:96, :, :], 1.0).then_inc(kst_one, 1)
                    pool.wait_ge(kst_one, 3)
                    done(pool.memset(V32, 0.0))
            for b in range(B + 1):
                if b < B:
                    if b >= 2:
                        pool.wait_ge(pv_pe, (NH // 4) * (b - 1))
                    for m in range(LB):
                        ins = pool.tensor_copy(V32[:, b % 2, m, :, 0:HD + 1], V9[:, m, b, :, :])
                    ins.then_inc(v32_ok, 1)
                if b >= 1:
                    pool.wait_ge(tmp_ok, b)
                    pool.tensor_tensor(X[:, b - 1, :], X[:, b - 1, :], TMP, ALU.add).then_inc(x3_ok, 1)
                    root(b - 1, b)
            root(0, B)

        @block.scalar
        def _(act):
            for i, w in enumerate((wk, wv, wq, wm)):
                act.dma_start(WST[:, i, :], w).then_inc(ld_w, 16)
            half = "(a t s) -> a t s"
            for i, v in enumerate((bk, bq)):
                act.dma_start(BST[2 * i:2 * i + 1, :], v.rearrange("(a n) -> a n", a=1)).then_inc(ld_w, 16)
                src = v.rearrange(half, t=2, s=NH)
                dst = BST[2 * i + 1:2 * i + 2, :].rearrange("p (a t s) -> p a t s", t=2, s=NH)
                for t in range(2):
                    act.dma_start(dst[:, :, t, :], src[:, 1 - t, :].rearrange("(o a) s -> o a s", o=1))\
                       .then_inc(ld_w, 16)
            act.dma_start(BST[4:5, :], bv.rearrange("(a n) -> a n", a=1)).then_inc(ld_w, 16)
            act.dma_start(BST[5:6, :], bm.rearrange("(a n) -> a n", a=1)).then_inc(ld_w, 16)
            act.dma_start(BVB[:, :], bv.partition_broadcast(P)).then_inc(ld_w, 16)
            act.dma_start(GW[:, :], gate_w).then_inc(ld_w, 16)
            act.dma_start(RW[:, :, :], rw.rearrange("(k p) e -> p k e", p=P)).then_inc(ld_w, 16)
            act.dma_start(GR[:, 0:2], g_xattn.partition_broadcast(P)).then_inc(ld_g, 16)
            act.dma_start(GR[:, 2:4], g_ffn.partition_broadcast(P)).then_inc(ld_g, 16)
            for f in range(2):
                act.dma_start(ENC[:, :, f, :], enc[f, 0, 0].rearrange("(k p) d -> p k d", p=P)).then_inc(ld_enc, 16)
            act.wait_ge(ld_g, 32)
            act.activation(TGT[:, :], GR[:, :], ACT.Tanh).then_inc(act_step, 1)
            jn = [0]

            def job(dst, src):
                act.wait_ge(job_pe, jn[0] + 1)
                act.activation(dst, src, ACT.Copy).then_inc(job_act, 1)
                jn[0] += 1

            def bank(i, w=512):
                return PS[:, i, 0:w]

            def casts(parts, a, k, sem_in):
                for s in range(2):
                    act.wait_ge(cast_in, 2 * k + s + 1)
                    act.activation(parts[:, s, :], a, ACT.Copy).then_inc(cast_out, 1)

            for g in range(4):
                job(KT[:, 4 * g:4 * g + 4, :].rearrange("p k c -> p (k c)"), bank(g % 2))
            for g in range(4):
                job(QT[:, 4 * g:4 * g + 4, :].rearrange("p k c -> p (k c)"), bank(g % 2))
            job(WT[:, :, :].rearrange("p k c -> p (k c)"), bank(0))
            job(FQ[:, :, :].rearrange("p f (k n) -> p k f n", k=LB),
                PS[:, 1, :].rearrange("p (k f n) -> p k f n", k=LB, f=2))
            job(BT[:, :], PS[:, 0, 0:6])
            job(GT[:, :, :].rearrange("p k e -> p (k e)"), PS[:, 1, 0:2 * E0])
            act.wait_ge(job_act, 12)
            for i, w in enumerate((0, 2)):
                src = WT[:, w, :].rearrange("p (a t s) -> p a t s", t=2, s=NH)
                dst = PWT[:, i, :].rearrange("p (a t s) -> p a t s", t=2, s=NH)
                for t in range(2):
                    act.activation(dst[:, :, t, :], src[:, :, 1 - t, :], ACT.Copy).then_inc(f_ok, 1)
            for c in range(QC):
                casts(KR["parts"], KR["a"], c, None)
            def turn_in(base):
                for g in range(4):
                    act.wait_ge(xt_pe, base + g + 1)
                    act.activation(XNT[:, g // 2, (g % 2) * 512:(g % 2) * 512 + 512], bank(6 + g % 2), ACT.Copy)\
                        .then_inc(xt_act, 1)
            turn_in(0)

            def shared(u):
                act.wait_ge(sh_pe, u + 1)
                if u >= 2:
                    act.wait_ge(sh_act, u - 1)
                m = SHF[u % 3][1]
                act.activation(THS[0:m, u % 2, :], PS[0:m, 2 + 2 * (u % 2), :], ACT.Tanh, scale=0.5)\
                    .then_inc(sh_th, 1)

            act.wait_ge(ss_ok, 1)
            act.activation(EX, SS, ACT.Exp).then_inc(ex_ok, 1)
            for u in range(6):
                shared(u)
            for k in range(KT0):
                act.wait_ge(xb_pe, k + 1)
                if k >= 2:
                    act.wait_ge(gu_pe, k - 1)
                act.activation(XB[:, k % 2, :, :], PS[:, 1, 0:256], ACT.Copy).then_inc(xb_act, 1)
                act.wait_ge(oht_pe, k + 1)
                act.activation(OHT[:, k, :], PS[:, 6 + k % 2, :].bitcast(BF16), ACT.Copy).then_inc(oht_ok, 1)
                act.wait_ge(gu_pe, k + 1)
                if k >= 2:
                    act.wait_ge(at_ok, k - 1)
                act.activation(TH[0:HI, k % 2, :], PS[0:HI, 2 + k % 2, 0:256], ACT.Tanh, scale=0.5)\
                    .then_inc(th_ok, 1)
            for c in range(QC):
                casts(QR["parts"], QR["a"], QC + c, None)
            sc = 1.0 / float(HD) ** 0.5
            act.wait_ge(bmg_ok, 1)

            def exps(G):
                act.wait_ge(st_pe, G + 1)
                if G >= 4:
                    act.wait_ge(pv_pe, (G - 4) // 2 + 1)
                act.activation(PX[:, G % 4].rearrange("p h m n -> p (h m n)"),
                               PS[:, 2 * (G % 2):2 * (G % 2) + 2, :].rearrange("p a n -> p (a n)"),
                               ACT.Exp, scale=sc).then_inc(p_ok, 1)

            def heads4(Q):
                b, q = divmod(Q, NH // 4)
                act.wait_ge(pv_pe, Q + 1)
                if b >= 2:
                    act.wait_ge(on_pe, 2 * b - 2)
                act.activation(OTS[:, b % 2, q, :], PS[:, 6, 0:L], ACT.Copy).then_inc(ots_ok, 1)

            def turned(b):
                act.wait_ge(ont_pe, b + 1)
                if b >= 1:
                    act.wait_ge(wm_pe, b)
                act.activation(OT, PS[:, 7, 0:L], ACT.Copy).then_inc(ot_ok, 1)

            def gated(b):
                act.wait_ge(wm_pe, b + 1)
                if b >= 1:
                    act.wait_ge(x3_ok, b)
                act.activation(TMP, PS[:, 7, L:2 * L], ACT.Identity, bias=BMG[:, 0:1], scale=TGT[:, 1:2])\
                    .then_inc(tmp_ok, 1)

            def xturned(b):
                act.wait_ge(xt_pe, 4 + b + 1)
                act.activation(XNT[:, :, b * P:b * P + P], PS[:, 7, 0:L].rearrange("p (k t) -> p k t", k=LB), ACT.Copy)\
                    .then_inc(xt_act, 1)
                if b >= 1:
                    act.wait_ge(nq_ok, b)
                act.activation(SQ, XN[:, b, :], ACT.Square, accum_out=NQ[:, b:b + 1]).then_inc(nq_ok, 1)

            for b in range(B):
                for g in range(UN):
                    exps(b * UN + g)
                    if g % 2 == 0 and b * UN + g > 0:
                        heads4((b * UN + g) // 2 - 1)
                    if b >= 2 and g == 0:
                        xturned(b - 2)
                    if b >= 1 and g == 3:
                        turned(b - 1)
                    if b >= 1 and g == 4:
                        gated(b - 1)
            heads4(B * NH // 4 - 1)
            xturned(B - 2)
            turned(B - 1)
            gated(B - 1)
            xturned(B - 1)
            act.wait_ge(ss4_ok, 1)
            act.activation(EX4, LG4, ACT.Exp).then_inc(ex4_ok, 1)
            act.wait_ge(ct_pe, 1)
            act.activation(CPT[:, :], PS[0:24, 3, :].bitcast(BF16), ACT.Copy).then_inc(ct_ok, 1)
            for u in range(2 * E1):
                act.wait_ge(cb_pe, u + 1)
                if u >= 2:
                    act.wait_ge(ae_ok, u - 1)
                act.activation(CB[:, u % 2, :], bank(6 + u % 2), ACT.Copy).then_inc(cb_ok, 1)

        @block.tensor
        def _(pe):
            pe.wait_ge(const_ok, 1)
            jn = [0]

            def job(parts, waits=()):
                if jn[0] >= 2:
                    pe.wait_ge(job_act, jn[0] - 1)
                last = None
                for f in parts:
                    last = f(jn[0] % 2)
                last.then_inc(job_pe, 1)
                jn[0] += 1

            def turn(src, off, idn=IDF, m=P):
                w = src.shape[0]
                return lambda bk_: pe.transpose(PS[0:m, bk_, off:off + w], src, idn[0:w, 0:w])

            pe.wait_ge(cr_ok, 1)
            for g in range(4):
                lb, b0 = divmod(4 * g, B)
                job([turn(CR[:, b0 + i, lb, :], i * P) for i in range(4)])
            pe.wait_ge(ln_ok, 1)
            for g in range(4):
                lb, b0 = divmod(4 * g, B)
                job([turn(XN[:, b0 + i, lb * P:lb * P + P], i * P) for i in range(4)])
            pe.wait_ge(ld_w, 16 * 15)
            job([turn(WST[:, i, :], i * P) for i in range(4)])
            pe.wait_ge(enc_ok, 1)
            job([turn(EB[:, k, f, :], (k * 2 + f) * P) for k in range(LB) for f in range(2)])
            job([turn(BST, 0)])
            job([turn(GW[:, k * P:k * P + P], k * E0) for k in range(LB)])

            def conv(h):
                pe.wait_ge(kv_ready, h + 1)
                if h == 0:
                    pe.wait_ge(ld_tt, 16)
                if h >= 2:
                    pe.wait_ge(z_done, h - 1)
                b0 = 2 + 2 * (h % 2)
                pe.matmul(PS[:, b0, :], TT[:, h, 0:P], KV[:, h % 4, 0:512], start=True, stop=True)
                pe.matmul(PS[:, b0 + 1, :], TT[:, h, P:L], KV[:, h % 4, 0:512], start=True, stop=False)
                pe.matmul(PS[:, b0 + 1, :], TT[:, h, 0:P], KV[:, h % 4, 512:1024], start=False, stop=True)\
                    .then_inc(conv_done, 1)

            def rope_mm(c, w, src, sem_pe, sem_free, b0):
                if c >= 1 and sem_free is not None:
                    pe.wait_ge(sem_free, c)
                rhs = src[:, 2 * c:2 * c + 2, :].rearrange("p b n -> p (b n)")
                pe.matmul(PS[:, b0, :], WT[:, w, :], rhs, start=True, stop=True)
                pe.matmul(PS[:, b0 + 1, :], PWT[:, w // 2, :], rhs, start=True, stop=True).then_inc(sem_pe, 1)

            def vproj(g):
                lb, b0 = divmod(4 * g, B)
                fs = []
                for i in range(4):
                    fs.append(lambda bk_, i=i: pe.matmul(PS[:, bk_, i * P:i * P + P],
                                                         CTX[:, b0 + i, lb * P:lb * P + P], WT[:, 1, :],
                                                         start=True, stop=True))
                job(fs)

            for h in range(NH):
                conv(h)
                if h == 1:
                    pe.wait_ge(f_ok, 4)
                if 1 <= h and h % 3 == 1 and h // 3 < QC:
                    rope_mm(h // 3, 0, CTX, kp_pe, kp_free, 6)
                if h >= 1 and h % 3 == 2 and h // 3 < 4:
                    vproj(h // 3)
            pe.wait_ge(ol_done, NH)
            for g in range(4):
                pe.wait_ge(z_done, NH)
                for i in range(4):
                    b, lb = 2 * g + i // 2, i % 2
                    last = pe.transpose(PS[:, 2 + g, i * P:i * P + P], OL[:, lb * B + b, :], IDF[:, :])
                last.then_inc(ot_pe, 1)

            def turn_in(base, wait_free):
                for g in range(4):
                    if g >= 2:
                        pe.wait_ge(xt_act, base + g - 1)
                    for i in range(4):
                        t = (g % 2) * 4 + i
                        last = pe.transpose(PS[:, 6 + g % 2, i * P:i * P + P],
                                            XN[:, t, (g // 2) * P:(g // 2) * P + P], IDF[:, :])
                    last.then_inc(xt_pe, 1)

            pe.wait_ge(ln_ok, 2)
            pe.wait_ge(kp_free, QC)
            turn_in(0, None)
            pe.wait_ge(xt_act, 4)
            pe.wait_ge(job_act, NJ)
            for b in range(B):
                for k in range(LB):
                    last = pe.matmul(PS[:, 0, b * E0:b * E0 + E0], XNT[:, k, b * P:b * P + P], GT[:, k, :],
                                     start=(k == 0), stop=(k == 1))
            last.then_inc(lg_pe, 1)
            pe.wait_ge(ld_sh, 48)
            pe.wait_ge(ot_x, 4)

            def shared(u):
                n2, f = divmod(u, 3)
                f0, m = SHF[f]
                if u >= 2:
                    pe.wait_ge(sh_act, u - 1)
                for half in range(2):
                    for k in range(LB):
                        last = pe.matmul(PS[0:m, 2 + 2 * (u % 2) + half, :],
                                         SHW[:, k, half * SH + f0:half * SH + f0 + m],
                                         XNT[:, k, n2 * 512:n2 * 512 + 512], start=(k == 0), stop=(k == 1))
                last.then_inc(sh_pe, 1)

            shared(0)
            shared(1)
            pe.wait_ge(selb_ok, 1)
            pe.wait_ge(const_ok, 3)
            flat = SELB[:, :, :].rearrange("p b e -> p (b e)")
            pe.matmul(PS[:, 1, 0:256], UPB[:, :], flat, start=True, stop=True)
            for k in range(1, B):
                last = pe.matmul(PS[:, 1, k * E0:256], ONB[:, :], flat[:, 0:(B - k) * E0], start=False,
                                 stop=True, skip_group_check=True)
            last.then_inc(pos_pe, 1)
            for u in range(2, 6):
                shared(u)
            pe.wait_ge(oh_ok, B)
            for k in range(KT0):
                for b in range(B):
                    last = pe.matmul(PS[:, 0, k * 8:k * 8 + 8], OH[:, b, 2 * k:2 * k + 2, :].rearrange("p e c -> p (e c)"),
                                     RH[:, b, k, :], start=(b == 0), stop=(b == B - 1))
            last.then_inc(ix_pe, 1)

            def oh_turn(k):
                if k >= 2:
                    pe.wait_ge(oht_ok, k - 1)
                dst = PS[:, 6 + k % 2, :].bitcast(BF16)
                for b in range(B):
                    last = pe.transpose(dst[:, b * P:b * P + P],
                                        OH[:, b, 2 * k:2 * k + 2, :].rearrange("p e c -> p (e c)"), IDB[:, :])
                last.then_inc(oht_pe, 1)

            def xb_turn(k):
                pe.wait_ge(xg_in[k % 4], 16 * (k // 4 + 1))
                if k >= 1:
                    pe.wait_ge(xb_act, k)
                for j in range(LB):
                    last = pe.transpose(PS[:, 1, j * P:j * P + P], XG[:, k % 4, j * P:j * P + P], IDF[:, :])
                last.then_inc(xb_pe, 1)

            def up(k):
                pe.wait_ge(xb_act, k + 1)
                if k >= 2:
                    pe.wait_ge(at_ok, k - 1)
                for eo in range(2):
                    e = 2 * k + eo
                    pe.wait_ge(ld_exp[e % NRING], 32 * (e // NRING + 1))
                    for f in range(4):
                        for j in range(LB):
                            c = f * 128 + eo * SLOTC
                            last = pe.matmul(PS[0:HI, 2 + k % 2, c:c + SLOTC],
                                             WG[:, e % NRING, j, f * HI:f * HI + HI],
                                             XB[:, k % 2, j, eo * SLOTC:eo * SLOTC + SLOTC],
                                             start=(j == 0), stop=(j == 1))
                last.then_inc(gu_pe, 1)

            def down(k):
                pe.wait_ge(at_ok, k + 1)
                if k >= 2:
                    pe.wait_ge(y_ok, k - 1)
                for eo in range(2):
                    e = 2 * k + eo
                    for f in range(2):
                        last = pe.matmul(PS[eo * 64:eo * 64 + 64, 4 + k % 2, 0:256], AT[:, k % 2, f, eo, :],
                                         WD[:, e % NRING, f, :], start=(f == 0), stop=(f == 1))
                last.then_inc(y_pe, 1)

            pe.wait_ge(sh_act, 6)
            oh_turn(0)
            oh_turn(1)
            xb_turn(0)
            for k in range(KT0):
                up(k)
                if k + 1 < KT0:
                    xb_turn(k + 1)
                if k >= 1:
                    down(k - 1)
                if k + 2 < KT0:
                    oh_turn(k + 2)
            down(KT0 - 1)
            pe.wait_ge(oht_ok, KT0)
            pe.wait_ge(th_ok, KT0)
            for b in range(B):
                o = PS[:, b // 2, (b % 2) * L:(b % 2) * L + L]
                for f, (f0, m) in enumerate(SHF):
                    pe.matmul(o, SA[0:m, f, b * P:b * P + P], SHD[0:m, f, :], start=(f == 0), stop=False)
                for k in range(KT0):
                    if b == 0:
                        pe.wait_ge(y_ok, k + 1)
                    for s in range(3):
                        last = pe.matmul(o, OHT[:, k, b * P:b * P + P], Y[:, k, s, :], start=False,
                                         stop=(k == KT0 - 1 and s == 2))
                if b % 2 == 1:
                    last.then_inc(mo_pe, 1)
                    if b >= 3:
                        pe.wait_ge(ln_ok, 2 + b // 2)
                        rope_mm(b // 2 - 1, 2, XN, qp_pe, None, QBANK[b // 2 - 1])
            pe.wait_ge(ln_ok, 2 + QC)
            rope_mm(QC - 1, 2, XN, qp_pe, None, QBANK[QC - 1])

            pe.wait_ge(qp_free, QC)

            def smax(H):
                b, h = divmod(H, NH)
                if h == 0:
                    pe.wait_ge(st_in[b % 3], 16 * 6 * (b // 3 + 1))
                if H >= 2:
                    pe.wait_ge(s_max, H - 1)
                for m in range(LB):
                    last = pe.matmul(PS[:, 4 + H % 2, m * L:m * L + L], QST[b % 3][0:NT, h, m * P:m * P + P],
                                     KST[b % 3][0:NT, h, :], start=True, stop=True)
                last.then_inc(s_pe, 1)

            def maxturn(b):
                pe.wait_ge(ms_ok, b + 1)
                if b >= 2:
                    pe.wait_ge(tmp_ok, b - 1)
                pe.transpose(PS[0:96, 7, 0:64].bitcast(BF16), MS.rearrange("p s n -> p (s n)"), IDB[:, :])\
                    .then_inc(mt_pe, 1)

            def scores(G):
                b, g = divmod(G, UN)
                if g == 0:
                    pe.wait_ge(mrow_in, 48 * (b + 1))
                if G >= 2:
                    pe.wait_ge(p_ok, G - 1)
                for hh in range(2):
                    for m in range(LB):
                        last = pe.matmul(PS[:, 2 * (G % 2) + hh, m * L:m * L + L],
                                         KST[b % 3][0:SROWS, 2 * g + hh, m * P:m * P + P],
                                         QST[b % 3][0:SROWS, 2 * g + hh, :], start=True, stop=True)
                last.then_inc(st_pe, 1)

            def values(Q):
                b, q = divmod(Q, NH // 4)
                pe.wait_ge(p_ok, 2 * Q + 2)
                if q == 0:
                    pe.wait_ge(v32_ok, b + 1)
                if Q >= 1:
                    pe.wait_ge(ots_ok, Q)
                for m in range(LB):
                    for j in range(4):
                        last = pe.matmul(PS[32 * j:32 * j + 32, 6, 0:L], V32[:, b % 2, m, 4 * q + j, :],
                                         PX[:, (2 * Q + j // 2) % 4, j % 2, m, :], start=(m == 0), stop=(m == 1))
                last.then_inc(pv_pe, 1)

            def back(b, n):
                pe.wait_ge(ots_ok, (NH // 4) * (b + 1))
                if n == 1:
                    pe.wait_ge(on_ok, 2 * b + 1)
                elif b >= 1:
                    pe.wait_ge(xt_act, 4 + b)
                else:
                    pe.wait_ge(mr_ok, 2)
                for q in range(NH // 4):
                    last = pe.transpose(PS[:, 7, q * P:q * P + P], OTS[:, b % 2, q, n * P:n * P + P], IDF[:, :])
                last.then_inc(on_pe, 1)

            def outturn(b):
                pe.wait_ge(on_ok, 2 * b + 2)
                for n in range(LB):
                    last = pe.transpose(PS[:, 7, n * P:n * P + P], ON[:, n].rearrange("p d h -> p (d h)"), IDF[:, :])
                last.then_inc(ont_pe, 1)

            def project(b):
                pe.wait_ge(ot_ok, b + 1)
                pe.matmul(PS[:, 7, 256:512], WT[:, 3, :], OT, start=True, stop=True).then_inc(wm_pe, 1)

            def xturn(b):
                pe.wait_ge(ln_ok, 3 + QC + b)
                if b + 2 < B:
                    pe.wait_ge(mr_ok, b + 3)
                else:
                    pe.wait_ge(tmp_ok, b + 1)
                for k in range(LB):
                    last = pe.transpose(PS[:, 7, k * P:k * P + P], XN[:, b, k * P:k * P + P], IDF[:, :])
                last.then_inc(xt_pe, 1)

            q = list(range(B * NH))
            for _ in range(2 * LEAD):
                smax(q.pop(0))
                if q[0] == NH:
                    maxturn(0)
            for b in range(B):
                for g in range(UN):
                    G = b * UN + g
                    scores(G)
                    for _ in range(2):
                        if q:
                            smax(q.pop(0))
                    if g == 5 and b + 1 < B:
                        maxturn(b + 1)
                    if g % 2 == 0 and G > 0:
                        values(G // 2 - 1)
                    if g == 0 and b >= 2:
                        xturn(b - 2)
                    if b >= 1:
                        if g == 1:
                            back(b - 1, 0)
                        if g == 2:
                            back(b - 1, 1)
                        if g == 3:
                            outturn(b - 1)
                        if g == 4:
                            project(b - 1)
            values(B * NH // 4 - 1)
            xturn(B - 2)
            back(B - 1, 0)
            back(B - 1, 1)
            outturn(B - 1)
            project(B - 1)
            xturn(B - 1)

            pe.wait_ge(xt_act, 4 + B)
            for b in range(B):
                for k in range(LB):
                    last = pe.matmul(PS[:, 2, b * E1:b * E1 + E1], XNT[:, k, b * P:b * P + P], RW[:, k, :],
                                     start=(k == 0), stop=(k == 1))
            last.then_inc(lg_pe, 1)
            pe.wait_ge(ld_ab, 32)

            def inner(u):
                c, e = divmod(u, E1)
                if u >= 2:
                    pe.wait_ge(ae_ok, u - 1)
                for k in range(LB):
                    last = pe.matmul(PS[:, 4 + u % 2, :], WA[:, e, k, :], XNT[:, k, c * 512:c * 512 + 512],
                                     start=(k == 0), stop=(k == 1))
                last.then_inc(a_pe, 1)

            def weights(u):
                c, e = divmod(u, E1)
                if u >= 2:
                    pe.wait_ge(cb_ok, u - 1)
                pe.matmul(PS[:, 6 + u % 2, :], SELE[:, e, :], CPT[:, c * 512:c * 512 + 512], start=True,
                          stop=True).then_inc(cb_pe, 1)

            inner(0)
            inner(1)
            pe.wait_ge(c_ok, 1)
            dst = PS[0:3 * E1, 3, :].bitcast(BF16)
            for b in range(B):
                last = pe.transpose(dst[:, b * P:b * P + P], CP[:, b].rearrange("p s e -> p (s e)"), IDB[:, :])
            last.then_inc(ct_pe, 1)
            pe.wait_ge(ct_ok, 1)
            weights(0)
            weights(1)
            for u in range(2 * E1):
                c, e = divmod(u, E1)
                pe.wait_ge(ae_ok, u + 1)
                for t in range(4):
                    last = pe.matmul(PS[:, 2 * c + t // 2, (t % 2) * L:(t % 2) * L + L],
                                     AE[:, u % 2, t * P:t * P + P], WB[:, e, :],
                                     start=(e == 0 and t % 2 == 0), stop=True, skip_group_check=True)
                last.then_inc(o_pe, 1)
                if u + 2 < 2 * E1:
                    inner(u + 2)
                    weights(u + 2)

        @block.vector
        def _(dve):
            n = [0]

            def done(ins):
                n[0] += 1
                ins.then_inc(dve_step, 1)
                dve.wait_ge(dve_step, n[0])

            def bc(v, shape, axis):
                return v.unsqueeze(axis).to_broadcast(shape)

            lk = [0]

            def stats(bs):
                for b in bs:
                    ins = dve.bn_stats(STT[:, b, :], X[:, b, :])
                done(ins)
                for b in bs:
                    ins = dve.bn_aggr(MV[:, b, :], STT[:, b, :])
                done(ins)
                dve.tensor_scalar(RSA[:, bs[0]:bs[-1] + 1], MV[:, bs[0]:bs[-1] + 1, 1], EPS, None, ALU.add)\
                    .then_inc(ln_var, 1)

            def apply(bs):
                lk[0] += 1
                dve.wait_ge(ln_pow, lk[0])
                for b in bs:
                    ins = dve.tensor_scalar(XN[:, b, :], X[:, b, :], MV[:, b, 0:1], RS[:, b:b + 1],
                                            ALU.subtract, ALU.mult)
                ins.then_inc(ln_ok, 1)

            def layernorm(bs=range(B)):
                stats(bs)
                apply(bs)

            dve.wait_ge(ld_ctx, 16)
            dve.tensor_copy(CR, CTX[:, :, :].rearrange("p b (k n) -> p b k n", k=LB)[:, :, :, ::-1]).then_inc(cr_ok, 1)
            done(dve.memset(KPAD[:, 0:P], 0.0))
            dve.wait_ge(ld_ssm, 32)
            dve.tensor_tensor(KPAD[:, P:P + 1], KPAD[:, P:P + 1], DSK[:, :], ALU.add).then_inc(kpad_ok, 1)
            dve.wait_ge(ld_x, 16)
            layernorm()
            dve.wait_ge(ld_enc, 32)
            even = ENC[:, :, 1, :].rearrange("p k (a t) -> p k a t", t=2)[:, :, :, 0]
            done(dve.tensor_scalar(even, even, -1.0, None, ALU.mult))
            for k in range(LB):
                ins = dve.tensor_copy(EB[:, k].rearrange("p f (d h) -> p f d h", h=NH),
                                      bc(ENC[:, k], [P, 2, HD, NH], 3))
            ins.then_inc(enc_ok, 1)

            def two(v):
                return v.rearrange("p (b n) -> p b n", b=2)

            def rope(c, R, bias, sem_pe, sem_free, sem_parts, out_wait, cast0, b0):
                dve.wait_ge(sem_pe, c + 1)
                if out_wait:
                    out_wait()
                dve.scalar_tensor_tensor(out=two(R["a"]), in0=two(PS[:, b0, :]), scalar=BT[:, bias:bias + 1],
                                         in1=bc(FQ[:, 0, :], [P, 2, L], 1), op0=ALU.add, op1=ALU.mult)
                dve.scalar_tensor_tensor(out=two(R["b"]), in0=two(PS[:, b0 + 1, :]), scalar=BT[:, bias + 1:bias + 2],
                                         in1=bc(FQ[:, 1, :], [P, 2, L], 1), op0=ALU.add, op1=ALU.mult)\
                    .then_inc(sem_free, 1)
                dve.wait_ge(sem_free, c + 1)
                dve.tensor_tensor(R["a"], R["a"], R["b"], ALU.add).then_inc(cast_in, 1)
                dve.wait_ge(cast_out, 2 * cast0 + 1)
                dve.tensor_tensor(R["a"], R["a"], R["parts"][:, 0, :], ALU.subtract).then_inc(cast_in, 1)
                dve.wait_ge(cast_out, 2 * cast0 + 2)
                dve.tensor_tensor(R["parts"][:, 2, :], R["a"], R["parts"][:, 1, :], ALU.subtract)\
                    .then_inc(sem_parts, 1)

            def krope(c):
                if c == 0:
                    dve.wait_ge(job_act, 12)

                def w():
                    if c >= 1:
                        dve.wait_ge(kp_out, 16 * c)
                rope(c, KR, 0, kp_pe, kp_free, kp_parts, w, c, 6)

            def vout(g):
                lb, b0 = divmod(4 * g, B)
                dve.wait_ge(job_pe, 12 + g + 1)
                src = PS[:, g % 2, :].rearrange("p (b c) -> p b c", b=4)
                for i in range(4):
                    ins = dve.tensor_tensor(V9[:, lb, b0 + i, :, 0:HD].rearrange("p h d -> p d h"),
                                            src[:, i, :].rearrange("p (d h) -> p d h", h=NH),
                                            BVB[:, :].rearrange("p (d h) -> p d h", h=NH), ALU.add)
                ins.then_inc(job_act, 1)

            def zmul(h):
                dve.wait_ge(conv_done, h + 1)
                b0 = 2 + 2 * (h % 2)
                zz = Z[:, h % 2, :].rearrange("p (k j i) -> p k j i", j=HD, i=HD)
                yy = PS[:, b0:b0 + 2, :].rearrange("p a n -> p (a n)").rearrange("p (k j i) -> p k j i", j=HD, i=HD)
                dve.tensor_tensor(zz, yy, bc(QT[:, :, h * HD:h * HD + HD], [P, LB * B, HD, HD], 2), ALU.mult)\
                    .then_inc(z_done, 1)
                dve.wait_ge(z_done, h + 1)
                dve.tensor_reduce(OL[:, :, h * HD:h * HD + HD], zz, AX, ALU.add).then_inc(ol_done, 1)

            dve.wait_ge(job_act, 8)
            for h in range(NH):
                zmul(h)
                if 1 <= h and h % 3 == 1 and h // 3 < QC:
                    krope(h // 3)
                if h >= 1 and h % 3 == 2 and h // 3 < 4:
                    vout(h // 3)
            dve.wait_ge(act_step, 1)
            for g in range(4):
                dve.wait_ge(ot_pe, g + 1)
                v = X[:, 2 * g:2 * g + 2, :].rearrange("p b l -> p (b l)")
                ins = dve.scalar_tensor_tensor(out=v, in0=PS[:, 2 + g, :], scalar=TGT[:, 0:1], in1=v,
                                               op0=ALU.mult, op1=ALU.add)
                ins.then_inc(ot_x, 1)
            dve.wait_ge(ot_x, 4)
            layernorm()

            dve.wait_ge(lg_pe, 1)
            dve.wait_ge(const_ok, 10)
            done(dve.tensor_copy(LG.rearrange("p b e -> p (b e)"), PS[:, 0, 0:256]))
            done(dve.tensor_reduce(GS, LG.rearrange("p b (g k) -> p b g k", g=NG), AX, ALU.max))
            sh4 = [P, B, NG, NG]
            dve.tensor_tensor(C1, bc(GS, sh4, 2), bc(GS, sh4, 3), ALU.is_gt)
            done(dve.tensor_tensor(C2, bc(GS, sh4, 2), bc(GS, sh4, 3), ALU.is_equal))
            done(dve.tensor_tensor(C2, C2, bc(LTG[:, :, :], sh4, 1), ALU.mult))
            done(dve.tensor_tensor(C1, C1, C2, ALU.add))
            done(dve.tensor_reduce(RK, C1, AX, ALU.add))
            done(dve.tensor_scalar(RK, RK, float(TG), None, ALU.is_lt))
            g4 = "p b (g k) -> p (b g) k"
            done(dve.tensor_tensor(SC.rearrange(g4, k=GE), LG.rearrange(g4, k=GE),
                                   bc(RK.rearrange("p b g -> p (b g)"), [P, B * NG, GE], 2), ALU.mult))
            for b in range(B):
                ins = dve.max(M8[:, b, :], SC[:, b, :])
            done(ins)
            sh3 = [P, B, E0]
            dve.tensor_tensor(SS, SC, bc(M8[:, :, 0], sh3, 2), ALU.subtract).then_inc(ss_ok, 1)
            dve.tensor_tensor(EQ, SC, bc(M8[:, :, TOPK0 - 1], sh3, 2), ALU.is_equal)
            done(dve.tensor_tensor(GTR, SC, bc(M8[:, :, TOPK0 - 1], sh3, 2), ALU.is_gt))
            done(dve.tensor_reduce(CNT, GTR, AX, ALU.add))
            done(dve.tensor_scalar(CNT, CNT, -1.0, float(TOPK0), ALU.mult, ALU.add))
            fl = "p b e -> p (b e)"
            done(dve.tensor_tensor_scan(PF.rearrange(fl), RM[:, :, :].rearrange(fl), EQ.rearrange(fl), 0.0,
                                        ALU.mult, ALU.add))
            done(dve.tensor_tensor(PF, PF, bc(CNT, sh3, 2), ALU.is_le))
            done(dve.tensor_tensor(EQ, EQ, PF, ALU.mult))
            done(dve.tensor_tensor(SEL, GTR, EQ, ALU.add))
            dve.tensor_copy(SELB[:, :, :], SEL).then_inc(selb_ok, 1)
            dve.wait_ge(ex_ok, 1)
            done(dve.tensor_reduce(SE, EX, AX, ALU.add))
            done(dve.reciprocal(SE, SE))
            done(dve.tensor_tensor(EX, EX, bc(SE, sh3, 2), ALU.mult))

            def shared(u):
                n2, f = divmod(u, 3)
                m = SHF[f][1]
                b0 = 2 + 2 * (u % 2)
                dve.wait_ge(sh_th, u + 1)
                if u >= 1:
                    dve.wait_ge(sh_act, u)
                done(dve.scalar_tensor_tensor(out=A1S[0:m, :], in0=THS[0:m, u % 2, :], scalar=1.0,
                                              in1=PS[0:m, b0, :], op0=ALU.add, op1=ALU.mult))
                dve.scalar_tensor_tensor(out=SA[0:m, f, n2 * 512:n2 * 512 + 512], in0=A1S[0:m, :], scalar=0.5,
                                         in1=PS[0:m, b0 + 1, :], op0=ALU.mult, op1=ALU.mult).then_inc(sh_act, 1)

            dve.wait_ge(kp_out, 16 * QC)
            shared(0)
            dve.wait_ge(pos_pe, 1)
            pos = PS[:, 1, 0:256].rearrange("p (b e) -> p b e", b=B)
            done(dve.scalar_tensor_tensor(out=VL.rearrange(fl), in0=PS[:, 1, 0:256], scalar=float(CAP),
                                          in1=SEL.rearrange(fl), op0=ALU.is_lt, op1=ALU.mult))
            done(dve.scalar_tensor_tensor(out=PK[:, :, :].rearrange(fl), in0=PS[:, 1, 0:256], scalar=float(SLOTC),
                                          in1=VL.rearrange(fl), op0=ALU.subtract, op1=ALU.mult))
            done(dve.tensor_scalar(PK[:, :, :], PK[:, :, :], float(SLOTC), None, ALU.add))
            done(dve.scalar_tensor_tensor(out=EX.rearrange(fl), in0=EX.rearrange(fl), scalar=SCALE0,
                                          in1=VL.rearrange(fl), op0=ALU.mult, op1=ALU.mult))
            w4 = EX.rearrange("p b (k e) -> p (b k) e", e=2)

            def rh(s):
                return RH[:, :, :, 2 + 2 * s:4 + 2 * s].rearrange("p b k e -> p (b k) e")
            done(dve.tensor_copy(rh(0), w4))
            done(dve.tensor_tensor(w4, w4, rh(0), ALU.subtract))
            done(dve.tensor_copy(rh(1), w4))
            done(dve.tensor_tensor(rh(2), w4, rh(1), ALU.subtract))
            dve.wait_ge(const_ok, 11)
            for b in range(B):
                dve.tensor_tensor(OH[:, b, :, 0:CAP], bc(PK[:, b, :], [P, E0, CAP], 2),
                                  bc(IOT[:, :], [P, E0, CAP], 1), ALU.is_equal).then_inc(oh_ok, 1)
                if b < 5:
                    shared(b + 1)
            dve.wait_ge(ix_pe, 1)
            ixv = PS[:, 0, 0:KT0 * 8].rearrange("p (k c) -> p k c", c=8)
            done(dve.tensor_copy(WS[:, :], ixv[:, :, 0]))
            dve.tensor_tensor(IX[:, :], WS[:, :], ixv[:, :, 1], ALU.add).then_inc(ix_ok, 1)
            dve.wait_ge(ix_ok, 1)
            for eo in range(2):
                rows = slice(eo * 64, eo * 64 + 64)
                done(dve.tensor_reduce(WS[rows, :],
                                       ixv[rows, :, 2 + eo:8].rearrange("p k c -> p k c")[:, :, 0:5:2], AX, ALU.add))

            def silu(k):
                dve.wait_ge(th_ok, k + 1)
                if k >= 1:
                    dve.wait_ge(at_ok, k)
                if k >= 2:
                    dve.wait_ge(y_pe, k - 1)
                done(dve.scalar_tensor_tensor(out=A1[0:HI, 0:256], in0=TH[0:HI, k % 2, :], scalar=1.0,
                                              in1=PS[0:HI, 2 + k % 2, 0:256], op0=ALU.add, op1=ALU.mult))
                dve.scalar_tensor_tensor(out=AT[:, k % 2].rearrange("p f e c -> p (f e c)"), in0=A1[0:HI, 0:256],
                                         scalar=0.5, in1=PS[0:HI, 2 + k % 2, 256:512], op0=ALU.mult,
                                         op1=ALU.mult).then_inc(at_ok, 1)

            def yout(k):
                dve.wait_ge(y_pe, k + 1)
                if k >= 1:
                    dve.wait_ge(y_ok, k)
                yp = PS[:, 4 + k % 2, 0:256]
                done(dve.tensor_scalar(Y[:, k, 0, :], yp, WS[:, k:k + 1], None, ALU.mult))
                done(dve.scalar_tensor_tensor(out=YR[:, :], in0=yp, scalar=WS[:, k:k + 1], in1=Y[:, k, 0, :],
                                              op0=ALU.mult, op1=ALU.subtract))
                done(dve.tensor_copy(Y[:, k, 1, :], YR[:, :]))
                dve.tensor_tensor(Y[:, k, 2, :], YR[:, :], Y[:, k, 1, :], ALU.subtract).then_inc(y_ok, 1)

            for k in range(KT0):
                silu(k)
                if k >= 1:
                    yout(k - 1)
            yout(KT0 - 1)
            def qrope(c):
                def w():
                    if c >= 1:
                        dve.wait_ge(qp_out[c - 1], 32)
                rope(c, QR, 2, qp_pe, qp_free, qp_parts, w, QC + c, QBANK[c])

            dve.wait_ge(rows_out, 16)
            dve.tensor_scalar(BMG[:, :], BT[:, 5:6], TGT[:, 1:2], None, ALU.mult).then_inc(bmg_ok, 1)
            for g in range(QC):
                dve.wait_ge(mo_pe, g + 1)
                v = X[:, 2 * g:2 * g + 2, :].rearrange("p b l -> p (b l)")
                dve.scalar_tensor_tensor(out=v, in0=PS[:, g, :], scalar=TGT[:, 2:3], in1=v,
                                         op0=ALU.mult, op1=ALU.add).then_inc(mo_x, 1)
                dve.wait_ge(mo_x, g + 1)
                layernorm(range(2 * g, 2 * g + 2))
            for c in range(QC):
                qrope(c)

            def rowmax(H):
                dve.wait_ge(s_pe, H + 1)
                dve.tensor_reduce(MX[:, H % NH, :], PS[:, 4 + H % 2, :].rearrange("p (m n) -> p m n", m=LB),
                                  AX, ALU.max).then_inc(s_max, 1)

            def maxparts(b):
                dve.wait_ge(s_max, NH * (b + 1))
                if b >= 1:
                    dve.wait_ge(ms_ok, b)
                if b >= 1:
                    dve.wait_ge(mt_pe, b)
                m = MX.rearrange("p h m -> p (h m)")
                done(dve.tensor_scalar(MS[:, 0, :], m, -1.0, None, ALU.mult))
                done(dve.scalar_tensor_tensor(out=MXR, in0=m, scalar=-1.0, in1=MS[:, 0, :], op0=ALU.mult,
                                              op1=ALU.subtract))
                done(dve.tensor_copy(MS[:, 1, :], MXR))
                dve.tensor_tensor(MS[:, 2, :], MXR, MS[:, 1, :], ALU.subtract).then_inc(ms_ok, 1)

            def maxcopy(b):
                dve.wait_ge(mt_pe, b + 1)
                if b >= 1:
                    dve.wait_ge(mrow_in, 48 * b)
                dve.tensor_copy(MR[0:96, :], PS[0:96, 7, 0:64].bitcast(BF16)).then_inc(mr_ok, 1)

            def normal(b, m):
                dve.wait_ge(on_pe, 2 * b + m + 1)
                if b >= 1 and m == 0:
                    dve.wait_ge(ont_pe, b)
                o = PS[:, 7, :].rearrange("p (h c) -> p h c", h=NH)
                done(dve.reciprocal(RO[:, m, :], o[:, :, HD]))
                dve.tensor_tensor(ON[:, m], o[:, :, 0:HD].rearrange("p h d -> p d h"),
                                  bc(RO[:, m, :], [P, HD, NH], 1), ALU.mult).then_inc(on_ok, 1)

            q = list(range(B * NH))
            for _ in range(2 * LEAD):
                rowmax(q.pop(0))
                if q[0] == NH:
                    maxparts(0)
                    maxcopy(0)
            for b in range(B):
                for g in range(UN):
                    if g == 5 and b + 1 < B:
                        maxparts(b + 1)
                    for _ in range(2):
                        if q:
                            rowmax(q.pop(0))
                    if g == 5 and b + 1 < B:
                        maxcopy(b + 1)
                    if b >= 1:
                        if g == 1:
                            normal(b - 1, 0)
                        if g == 2:
                            normal(b - 1, 1)
                        if g == 6:
                            dve.wait_ge(x3_ok, b)
                            stats([b - 1])
                        if g == 7:
                            apply([b - 1])
            normal(B - 1, 0)
            normal(B - 1, 1)
            dve.wait_ge(x3_ok, B)
            stats([B - 1])
            apply([B - 1])

            dve.wait_ge(nq_ok, B)
            dve.wait_ge(ln_ok, 2 + QC + B)
            dve.tensor_scalar(RSA[:, :], NQ[:, :], 1e-24, None, ALU.max).then_inc(ln_var, 1)
            lk[0] += 1
            dve.wait_ge(ln_pow, lk[0])
            dve.wait_ge(lg_pe, 2)
            s8 = [P, B, E1]
            done(dve.tensor_tensor(LG4, PS[:, 2, 0:64].rearrange("p (b e) -> p b e", b=B),
                                   bc(RS[:, :], s8, 2), ALU.mult))
            for b in range(B):
                ins = dve.max(M84[:, b, :], LG4[:, b, :])
            done(ins)
            dve.tensor_tensor(EQ4, LG4, bc(M84[:, :, TOPK1 - 1], s8, 2), ALU.is_equal)
            done(dve.tensor_tensor(GT4, LG4, bc(M84[:, :, TOPK1 - 1], s8, 2), ALU.is_gt))
            dve.tensor_tensor(LG4, LG4, bc(M84[:, :, 0], s8, 2), ALU.subtract).then_inc(ss4_ok, 1)
            done(dve.tensor_reduce(C4, GT4, AX, ALU.add))
            done(dve.tensor_scalar(C4, C4, -1.0, float(TOPK1), ALU.mult, ALU.add))
            done(dve.tensor_tensor_scan(PF4.rearrange(fl), RM4[:, :, :].rearrange(fl), EQ4.rearrange(fl), 0.0,
                                        ALU.mult, ALU.add))
            done(dve.tensor_tensor(PF4, PF4, bc(C4, s8, 2), ALU.is_le))
            done(dve.tensor_tensor(EQ4, EQ4, PF4, ALU.mult))
            done(dve.tensor_tensor(GT4, GT4, EQ4, ALU.add))
            dve.wait_ge(ex4_ok, 1)
            done(dve.tensor_tensor(EX4, EX4, GT4, ALU.mult))
            done(dve.tensor_reduce(S4, EX4, AX, ALU.add))
            done(dve.reciprocal(S4, S4))
            done(dve.tensor_tensor(EX4, EX4, bc(S4, s8, 2), ALU.mult))
            done(dve.tensor_copy(CP[:, :, 0, :], EX4))
            done(dve.tensor_tensor(EX4, EX4, CP[:, :, 0, :], ALU.subtract))
            done(dve.tensor_copy(CP[:, :, 1, :], EX4))
            dve.tensor_tensor(CP[:, :, 2, :], EX4, CP[:, :, 1, :], ALU.subtract).then_inc(c_ok, 1)
            for u in range(2 * E1):
                dve.wait_ge(cb_ok, u + 1)
                dve.wait_ge(a_pe, u + 1)
                if u >= 2:
                    dve.wait_ge(o_pe, u - 1)
                dve.tensor_tensor(AE[:, u % 2, :], PS[:, 4 + u % 2, :], CB[:, u % 2, :], ALU.mult)\
                    .then_inc(ae_ok, 1)
                if u % E1 == E1 - 1:
                    c = u // E1
                    dve.wait_ge(o_pe, E1 * (c + 1))
                    for g in range(2):
                        v = X[:, 4 * c + 2 * g:4 * c + 2 * g + 2, :].rearrange("p b l -> p (b l)")
                        dve.scalar_tensor_tensor(out=v, in0=PS[:, 2 * c + g, :], scalar=TGT[:, 3:4], in1=v,
                                                 op0=ALU.mult, op1=ALU.add).then_inc(o_ok, 1)


_INS = ['x', 'ctx_2048', 'g_xattn', 'g_ffn', 'L0_xattn_ssm_kernel', 'L0_xattn_D', 'L0_ffn_gate_w',
        'L0_ffn_w_gate_up', 'L0_ffn_w_down', 'L0_ffn_ws_gate_up', 'L0_ffn_ws_down', 'L1_xattn_encoding',
        'L1_xattn_Wq', 'L1_xattn_bq', 'L1_xattn_Wk', 'L1_xattn_bk', 'L1_xattn_Wv', 'L1_xattn_bv',
        'L1_xattn_Wm', 'L1_xattn_bm', 'L1_ffn_router_w', 'L1_ffn_Wa', 'L1_ffn_Wb']
_OUTS = [((8, 128, 256), 'float32')]


def kernel(**inputs):
    import numpy as _np
    import concourse.bacc as _bacc
    from concourse import mybir as _mybir
    from concourse.bass_utils import run_bass_kernel_spmd as _run

    nc = _bacc.Bacc("TRN2", target_bir_lowering=False, num_devices=1)
    arrays, args = {}, []
    for name in _INS:
        a = _np.ascontiguousarray(inputs[name])
        arrays[f"in_{name}_dram"] = a
        args.append(nc.dram_tensor(f"in_{name}_dram", a.shape, _mybir.dt.from_np(a.dtype), kind="ExternalInput").ap())
    for i, (shape, dtype) in enumerate(_OUTS):
        dt = _mybir.dt.from_np(_np.dtype(dtype))
        args.append(nc.dram_tensor(f"out_{i}_dram", shape, dt, kind="ExternalOutput").ap())
    build(nc, *args)
    r = _run(nc, [arrays], core_ids=[0])
    return r.results[0]["out_0_dram"]
```

```python
from contextlib import ExitStack

import concourse.bass as bass
from concourse import mybir

F32 = mybir.dt.float32
BF16 = mybir.dt.bfloat16
I32 = mybir.dt.int32
ALU = mybir.AluOpType
ACT = mybir.ActivationFunctionType
AX = mybir.AxisListType.X

B, S, L = 8, 128, 256
P = 128
LB = L // P
T = B * S
NH, HD = 16, 8
E0, TOPK0, CAP, NG, TG, INTER = 32, 6, 48, 8, 3, 176
GE = E0 // NG
SCALE0 = 16.0
HI = INTER // 2
SLOTC = 64
KT0 = E0 * SLOTC // P
SH = 2 * INTER
SHF = [(0, 128), (128, 128), (256, 96)]
NPAIR = 3
NRING = 2 * NPAIR
E1, TOPK1 = 8, 2
EPS = 1e-5
NT = 9 * HD
SROWS = NT + 3
UN = NH // 2
LEAD = 12


def build(nc, x, ctx_in, g_xattn, g_ffn, ssm, dskip, gate_w, wgu, wdn, wsgu, wsdn, enc,
          wq, bq, wk, bk, wv, bv, wm, bm, rw, wa, wb, out):
    es = ExitStack()
    with es:
        def sb(name, shape, dt=F32):
            return es.enter_context(nc.sbuf_tensor(name, shape, dt))

        def sem(name):
            return es.enter_context(nc.semaphore(name))

        kpad_d = nc.dram_tensor("kpad_d", [NH, P + L], F32, kind="Internal")
        rows_d = nc.dram_tensor("rows_d", [T + 1, L], F32, kind="Internal")
        kparts_d = nc.dram_tensor("kparts_d", [3, P, T * 2], BF16, kind="Internal")
        qparts_d = nc.dram_tensor("qparts_d", [5, P, T * 2], BF16, kind="Internal")

        X = sb("X", [P, B, L])
        XN = sb("XN", [P, B, L])
        CTX = sb("CTX", [P, B, L])
        XNT = CTX[:, :, :].rearrange("p b l -> p (b l)").rearrange("p (k t) -> p k t", k=LB)
        R1 = sb("R1", [P, 8192])
        R2 = sb("R2", [P, 16384])
        V9 = sb("V9", [P, LB, B, NH, HD + 1])
        FQ = sb("FQ", [P, 2, L])
        SHW = sb("SHW", [P, LB, 2 * SH])
        SHD = sb("SHD", [P, 3, L])
        SA = sb("SA", [P, 3, T])
        WG = sb("WG", [P, NRING, LB, 2 * INTER])
        WD = sb("WD", [P, NRING, 2, L])
        IDF = sb("IDF", [P, P])
        IDB = sb("IDB", [P, P], BF16)
        UPB = sb("UPB", [P, P], BF16)
        ONB = sb("ONB", [P, P], BF16)
        WST = R1[:, 0:512].rearrange("p (w n) -> p w n", w=4)
        WT = sb("WT", [P, 4, P])
        PWT = sb("PWT", [P, 2, P])
        BST = R1[0:6, 512:640]
        BT = sb("BT", [P, 6])
        BVB = sb("BVB", [P, P])
        GW = sb("GW", [E0, L])
        GT = sb("GT", [P, LB, E0])
        RW = sb("RW", [P, LB, E1])
        GR = sb("GR", [P, 4])
        TGT = sb("TGT", [P, 4])
        STT = sb("STT", [P, B, 6])
        MV = sb("MV", [P, B, 2])
        RS = sb("RS", [P, B])
        RSA = sb("RSA", [P, B])
        RSB = sb("RSB", [P, B])
        MH = sb("MH", [P, B])
        NQ = sb("NQ", [P, B])
        BMG = sb("BMG", [P, 1])
        KPAD = R1[0:NH, 640:640 + P + L]
        DSK = sb("DSK", [NH, 1])
        ZROW = sb("ZROW", [1, L])
        ENC = sb("ENC", [P, LB, 2, HD])
        IOT = sb("IOT", [P, CAP], F32)
        RM = sb("RM", [P, B, E0])
        LTG = sb("LTG", [P, NG, NG])

        PS = es.enter_context(nc.psum_tensor("PS", [P, 8, 512], F32))

        def r2(a, n, pat=None, **kw):
            v = R2[:, a:a + n]
            return v.rearrange(pat, **kw) if pat else v

        KT = r2(0, 2048, "p (k c) -> p k c", k=LB * B)
        QT = r2(2048, 2048, "p (k c) -> p k c", k=LB * B)
        TT = r2(4096, 4096, "p (h l) -> p h l", h=NH)
        KV = r2(8192, 4096, "p (s n) -> p s n", s=4)
        Z = r2(12288, 2048, "p (s n) -> p s n", s=2)
        CR = r2(12288, 2048, "p (b k n) -> p b k n", b=B, k=LB)
        OL = r2(14336, 2048, "p (k c) -> p k c", k=LB * B)
        def rope_views(base):
            return dict(a=base[:, 0:512], b=base[:, 512:1024],
                        parts=base[:, 1024:1792].bitcast(BF16).rearrange("p (s n) -> p s n", s=3))
        KR = rope_views(SA[:, :, :].rearrange("p s n -> p (s n)")[:, 0:1024 + 768])
        EB = SA[:, 2, 0:512].rearrange("p (k f c) -> p k f c", k=LB, f=2)

        OH = R1[:, :].bitcast(BF16).rearrange("p (b e c) -> p b e c", b=B, e=E0)
        OHT = r2(0, 8192).bitcast(BF16).rearrange("p (k t) -> p k t", k=KT0)
        Y = r2(8192, 6144).bitcast(BF16).rearrange("p (k s n) -> p k s n", k=KT0, s=3)
        XG = r2(14336, 1024, "p (s n) -> p s n", s=4)
        XB = r2(15360, 512, "p (s k n) -> p s k n", s=2, k=LB)
        base = [0]

        def small(n):
            a = base[0]
            base[0] += n
            return r2(a, n)
        LG = small(256).rearrange("p (b e) -> p b e", b=B)
        GS = small(64).rearrange("p (b g) -> p b g", b=B)
        C1 = small(512).rearrange("p (b g k) -> p b g k", b=B, g=NG)
        C2 = small(512).rearrange("p (b g k) -> p b g k", b=B, g=NG)
        RK = small(64).rearrange("p (b g) -> p b g", b=B)
        SC = small(256).rearrange("p (b e) -> p b e", b=B)
        M8 = small(64).rearrange("p (b k) -> p b k", b=B)
        SS = small(256).rearrange("p (b e) -> p b e", b=B)
        EX = small(256).rearrange("p (b e) -> p b e", b=B)
        GTR = small(256).rearrange("p (b e) -> p b e", b=B)
        EQ = small(256).rearrange("p (b e) -> p b e", b=B)
        PF = small(256).rearrange("p (b e) -> p b e", b=B)
        CNT = small(8)
        SE = small(8)
        SEL = small(256).rearrange("p (b e) -> p b e", b=B)
        VL = small(256)
        PK = sb("PK", [P, B, E0])
        SELB = sb("SELB", [P, B, E0], BF16)
        RH = sb("RH", [P, B, KT0, 8], BF16)
        IX = sb("IX", [P, KT0], I32)
        WS = sb("WS", [P, KT0])
        TH = sb("TH", [P, 2, INTER])
        A1 = sb("A1", [P, INTER])
        AS = sb("AS", [P, 2, INTER])
        AT = sb("AT", [HI, 2, 2, 2, SLOTC])
        YR = sb("YR", [P, L])
        THS = R2[:, 8192:8192 + 1024].rearrange("p (s n) -> p s n", s=2)
        SGT = R2[:, 9216:9216 + 1024].rearrange("p (s n) -> p s n", s=2)
        SUP = R2[:, 10240:10240 + 1024].rearrange("p (s n) -> p s n", s=2)

        def stacks(r1, r2_):
            return [r1.bitcast(BF16)[:, i * 4096:i * 4096 + 4096].rearrange("p (h n) -> p h n", h=NH)
                    for i in range(2)] + [r2_.bitcast(BF16).rearrange("p (h n) -> p h n", h=NH)]
        KST = stacks(R1[:, 0:4096], r2(8192, 2048))
        QST = stacks(R1[:, 4096:8192], r2(10240, 2048))
        QR = rope_views(WD[:, :, :, :].rearrange("p s f n -> p (s f n)"))
        PX = r2(2048, 4096, "p (s h m n) -> p s h m n", s=4, h=2, m=LB)
        MX = sb("MX", [P, NH, LB])
        MXR = sb("MXR", [P, 32])
        MS = sb("MS", [P, 3, 32], BF16)
        MR = sb("MR", [P, P], BF16)
        RO = r2(6336, 32, "p (m h) -> p m h", m=LB)
        ON = r2(6400, 256, "p (m d h) -> p m d h", m=LB, d=HD)
        OT = r2(6656, 256)
        TMP = r2(6912, 256)
        SQ = r2(7168, 256)
        OTS = r2(12288, 2048, "p (s q n) -> p s q n", s=2, q=NH // 4)
        V32 = r2(14336, 2048, "p (s m h c) -> p s m h c", s=2, m=LB, h=NH)

        WGF = WG[:, :, :, :].rearrange("p s k f -> p (s k f)")
        WA = WGF[:, 0:2048].rearrange("p (e k r) -> p e k r", e=E1, k=LB)
        WB = WGF[:, 2048:4096].rearrange("p (e n) -> p e n", e=E1)
        CB = r2(12288, 1024, "p (s n) -> p s n", s=2)
        AE = r2(13312, 1024, "p (s n) -> p s n", s=2)
        b4 = [14592]

        def small4(n):
            a = b4[0]
            b4[0] += n
            return r2(a, n)
        LG4 = small4(64).rearrange("p (b e) -> p b e", b=B)
        M84 = small4(64).rearrange("p (b e) -> p b e", b=B)
        GT4 = small4(64).rearrange("p (b e) -> p b e", b=B)
        EQ4 = small4(64).rearrange("p (b e) -> p b e", b=B)
        PF4 = small4(64).rearrange("p (b e) -> p b e", b=B)
        EX4 = small4(64).rearrange("p (b e) -> p b e", b=B)
        C4 = small4(8)
        S4 = small4(8)
        RM4 = sb("RM4", [P, B, E1])
        CP = sb("CP", [P, B, 3, E1], BF16)
        CPT = sb("CPT", [3 * E1, T], BF16)
        SELE = sb("SELE", [3 * E1, E1, P], BF16)

        ld_ctx, ld_x, ld_ssm, ld_w, ld_enc, ld_g, ld_sh = (sem(n) for n in (
            "ld_ctx", "ld_x", "ld_ssm", "ld_w", "ld_enc", "ld_g", "ld_sh"))
        ld_up = [sem(f"ld_up{i}") for i in range(NPAIR)]
        ld_down = [sem(f"ld_down{i}") for i in range(NPAIR)]
        kpad_out, ld_tt, const_ok, kpad_ok = (sem(n) for n in ("kpad_out", "ld_tt", "const_ok", "kpad_ok"))
        cr_ok = sem("cr_ok")
        dve_step, act_step, pool_step = sem("dve_step"), sem("act_step"), sem("pool_step")
        job_pe, job_act = sem("job_pe"), sem("job_act")
        kv_ready, conv_done, z_done, ol_done = sem("kv_ready"), sem("conv_done"), sem("z_done"), sem("ol_done")
        kp_pe, kp_free, kp_parts, kp_out = sem("kp_pe"), sem("kp_free"), sem("kp_parts"), sem("kp_out")
        cast_in, cast_out, k_sum, k_rest = sem("cast_in"), sem("cast_out"), sem("k_sum"), sem("k_rest")
        enc_ok, f_ok = sem("enc_ok"), sem("f_ok")
        ln_var, ln_pow, ln_ok = sem("ln_var"), sem("ln_pow"), sem("ln_ok")
        ot_pe, ot_x = sem("ot_pe"), sem("ot_x")
        rows_out, zrow_out = sem("rows_out"), sem("zrow_out")
        xt_pe, xt_act = sem("xt_pe"), sem("xt_act")
        lg_pe, ss_ok, ex_ok, selb_ok, pos_pe = (sem(n) for n in ("lg_pe", "ss_ok", "ex_ok", "selb_ok", "pos_pe"))
        sh_pe, sh_th, sh_act = sem("sh_pe"), sem("sh_th"), sem("sh_act")
        oh_ok, oht_pe, oht_ok, ix_pe, ix_ok = (sem(n) for n in ("oh_ok", "oht_pe", "oht_ok", "ix_pe", "ix_ok"))
        xg_in = [sem(f"xg_in{i}") for i in range(4)]
        xb_pe, xb_act, gu_pe, th_ok, at_ok, y_pe, y_ok = (sem(n) for n in (
            "xb_pe", "xb_act", "gu_pe", "th_ok", "at_ok", "y_pe", "y_ok"))
        as_ok, at_pe = sem("as_ok"), sem("at_pe")
        vl_ok, rh_ok = sem("vl_ok"), sem("rh_ok")
        mo_pe, mo_x = sem("mo_pe"), sem("mo_x")
        qp_pe, qp_free, qp_parts = sem("qp_pe"), sem("qp_free"), sem("qp_parts")
        qp_out = [sem(f"qp_out{c}") for c in range(B // 2)]
        st_in = [sem(f"st_in{s}") for s in range(3)]
        kst_one = sem("kst_one")
        s_pe, s_max, ms_ok, mt_pe, mr_ok = (sem(n) for n in ("s_pe", "s_max", "ms_ok", "mt_pe", "mr_ok"))
        mrow_in, st_pe, p_ok, pv_pe = (sem(n) for n in ("mrow_in", "st_pe", "p_ok", "pv_pe"))
        on_ok, ont_pe, ot_ok, wm_pe, x3_ok = (sem(n) for n in ("on_ok", "ont_pe", "ot_ok", "wm_pe", "x3_ok"))
        ots_ok, on_pe, tmp_ok, v32_ok, nq_ok, bmg_ok = (sem(n) for n in (
            "ots_ok", "on_pe", "tmp_ok", "v32_ok", "nq_ok", "bmg_ok"))
        ld_ab, c_ok, ct_pe, ct_ok = (sem(n) for n in ("ld_ab", "c_ok", "ct_pe", "ct_ok"))
        ss4_ok, ex4_ok = sem("ss4_ok"), sem("ex4_ok")
        cb_pe, cb_ok, a_pe, ae_ok, o_pe, o_ok, out_dma = (sem(n) for n in (
            "cb_pe", "cb_ok", "a_pe", "ae_ok", "o_pe", "o_ok", "out_dma"))

        HB = B // 2
        LN2, LN3, LN4 = 2, 2 + B // 2, 2 + B
        QC = B // 2
        RISE = 4
        EARLY = 2 * LEAD - RISE
        QBANK = (6, 4, 0)
        NJ = 16

        block = es.enter_context(nc.Block())

        @block.sync
        def _(sp):
            sp.dma_start(KPAD[:, P:P + L], ssm).then_inc(ld_ssm, 16)
            sp.dma_start(DSK[:, :], dskip.rearrange("(h a) -> h a", a=1)).then_inc(ld_ssm, 16)
            sp.dma_start(CTX[:, :, :], ctx_in.rearrange("b s l -> s b l")).then_inc(ld_ctx, 16)
            sp.dma_start(X[:, :, :], x.rearrange("b s l -> s b l")).then_inc(ld_x, 16)
            sp.wait_ge(kpad_ok, 1)
            sp.dma_start(kpad_d.ap(), KPAD).then_inc(kpad_out, 16)
            sp.wait_ge(kpad_out, 16)
            tap = bass.AP(tensor=kpad_d, offset=1, ap=[[1, P], [P + L, NH], [1, L]])
            sp.dma_start(TT, tap).then_inc(ld_tt, 16)
            sp.wait_ge(ld_w, 16 * 15)

            def load_up(k):
                sp.dma_start(WG[:, 2 * (k % NPAIR):2 * (k % NPAIR) + 2, :, :],
                             wgu[2 * k:2 * k + 2].rearrange("e (k p) f -> p e k f", p=P))\
                  .then_inc(ld_up[k % NPAIR], 16)

            def load_down(k):
                sp.dma_start(WD[0:HI, 2 * (k % NPAIR):2 * (k % NPAIR) + 2, :, :],
                             wdn[2 * k:2 * k + 2].rearrange("e (k p) n -> p e k n", p=HI))\
                  .then_inc(ld_down[k % NPAIR], 16)

            for k in range(NPAIR):
                load_up(k)
                load_down(k)
            sp.dma_start(SHW[:, :, :], wsgu.rearrange("(k p) f -> p k f", p=P)).then_inc(ld_sh, 16)
            sp.dma_start(SHD[:, 0:2, :], wsdn[0:256, :].rearrange("(k p) n -> p k n", p=P)).then_inc(ld_sh, 16)
            sp.dma_start(SHD[0:96, 2, :], wsdn[256:352, :]).then_inc(ld_sh, 16)
            for c in range(QC):
                sp.wait_ge(kp_parts, c + 1)
                sp.dma_start(kparts_d.ap().rearrange("s p n -> p s n")[:, :, c * 512:c * 512 + 512],
                             KR["parts"]).then_inc(kp_out, 16)
            sp.wait_ge(ln_ok, LN3)
            sp.dma_start(rows_d.ap()[1:T + 1, :].rearrange("(b s) l -> s b l", b=B), XN[:, :, :])\
              .then_inc(rows_out, 16)
            for k in range(NPAIR, KT0 + 1):
                if k < KT0:
                    sp.wait_ge(gu_pe, k - NPAIR + 1)
                    load_up(k)
                if k > NPAIR:
                    sp.wait_ge(y_pe, k - NPAIR)
                    load_down(k - 1)
            sp.wait_ge(y_pe, KT0)
            sp.dma_start(WA, wa.rearrange("e (k p) r -> p e k r", p=P)).then_inc(ld_ab, 16)
            sp.dma_start(WB, wb.rearrange("e p n -> p e n")).then_inc(ld_ab, 16)
            def stack(b):
                if b >= 3:
                    sp.wait_ge(st_pe, UN * (b - 2))
                else:
                    sp.wait_ge(kst_one, b + 1)
                for r in range(3):
                    rows = slice(3 * HD * r, 3 * HD * r + 3 * HD)
                    for dst, src, part in ((KST, kparts_d, 0), (QST, qparts_d, r)):
                        sp.dma_start(dst[b % 3][rows, :, :],
                                     src.ap()[part:part + 3].rearrange("s (d h) (b n) -> (s d) h b n", h=NH, b=B)[:, :, b, :])\
                          .then_inc(st_in[b % 3], 16)

            def maxrow(b):
                sp.wait_ge(mr_ok, b + 1)
                for s in range(3):
                    sp.dma_start(QST[b % 3][NT + s:NT + s + 1, :, :].rearrange("p h (m n) -> p (h m) n", m=LB),
                                 MR[32 * s:32 * s + 32, :]).then_inc(mrow_in, 16)

            def qout(c):
                sp.wait_ge(qp_parts, c + 1)
                cols = slice(c * 512, c * 512 + 512)
                sp.dma_start(qparts_d.ap().rearrange("s p n -> p s n")[:, 0:3, cols], QR["parts"]).then_inc(qp_out[c], 16)
                sp.dma_start(qparts_d.ap().rearrange("s p n -> p s n")[:, 3:5, cols], QR["parts"][:, 0:2, :])\
                  .then_inc(qp_out[c], 16)

            qout(0)
            sp.wait_ge(kp_out, 16 * QC)
            sp.wait_ge(qp_out[0], 32)
            stack(0)
            stack(1)
            qout(1)
            qout(2)
            maxrow(0)
            sp.wait_ge(qp_out[1], 32)
            stack(2)
            for b in range(B):
                if b + 1 < B:
                    maxrow(b + 1)
                if b + 3 < B:
                    sp.wait_ge(qp_out[(b + 3) // 2], 32)
                    stack(b + 3)
                if b == 0:
                    qout(QC - 1)
            for c in range(2):
                sp.wait_ge(o_ok, 2 * c + 2)
                sp.dma_start(out.rearrange("b s l -> s b l")[:, 4 * c:4 * c + 4, :], X[:, 4 * c:4 * c + 4, :])\
                  .then_inc(out_dma, 16)
            sp.wait_ge(out_dma, 32)
            sp.wait_ge(zrow_out, 16)

        @block.gpsimd
        def _(pool):
            n = [0]

            def done(ins):
                n[0] += 1
                ins.then_inc(pool_step, 1)
                pool.wait_ge(pool_step, n[0])

            done(pool.memset(IDF[:, :], 0.0))
            done(pool.affine_select(out=IDF[:, :], in_=IDF[:, :], compare_op=ALU.not_equal, fill=1.0,
                                    base=0, pattern=[[-1, P]], channel_multiplier=1))
            pool.tensor_copy(IDB[:, :], IDF[:, :]).then_inc(const_ok, 1)
            pool.memset(MH[:, :], -0.5).then_inc(const_ok, 1)

            rk = [0]

            def root(a, z):
                rk[0] += 1
                pool.wait_ge(ln_var, rk[0])
                pool.wait_ge(const_ok, 2)
                r, v, t = RSB[:, a:z], RSA[:, a:z], RS[:, a:z]
                done(pool.tensor_tensor(r, v, MH[:, a:z], ALU.pow))
                done(pool.tensor_tensor(t, r, r, ALU.mult))
                done(pool.tensor_tensor(t, t, v, ALU.mult))
                done(pool.tensor_scalar(t, t, -0.5, 1.5, ALU.mult, ALU.add))
                pool.tensor_tensor(t, t, r, ALU.mult).then_inc(ln_pow, 1)
                pool.wait_ge(ln_pow, rk[0])
            root(0, HB)
            root(HB, B)

            def kpart(c, s):
                pool.wait_ge(cast_out, 2 * c + s + 1)
                if s == 1:
                    pool.wait_ge(k_rest, c + 1)
                dst = KR["a"] if s == 0 else KR["parts"][:, 2, :]
                pool.tensor_tensor(dst, KR["a"], KR["parts"][:, s, :], ALU.subtract)\
                    .then_inc(k_rest if s == 0 else kp_parts, 1)

            pool.wait_ge(job_act, 4)
            for h in range(NH):
                if h >= 4:
                    pool.wait_ge(conv_done, h - 3)
                head = KT[:, :, h * HD:h * HD + HD]
                pool.tensor_tensor(KV[:, h % 4, :].rearrange("p (k j i) -> p k j i", j=HD, i=HD),
                                   head.unsqueeze(3).to_broadcast([P, LB * B, HD, HD]),
                                   head.unsqueeze(2).to_broadcast([P, LB * B, HD, HD]),
                                   ALU.mult).then_inc(kv_ready, 1)
                if h == 3:
                    done(pool.memset(UPB[:, :], 0.0))
                    done(pool.affine_select(out=UPB[:, :], in_=UPB[:, :], compare_op=ALU.is_ge, fill=1.0,
                                            base=0, pattern=[[-1, P]], channel_multiplier=1))
                    pool.memset(ONB[:, :], 1.0).then_inc(const_ok, 1)
                    pool.iota(IOT[:, :], [[1, CAP]], base=0, channel_multiplier=0,
                              allow_small_or_imprecise_dtypes=True).then_inc(const_ok, 1)
                if h == 5:
                    done(pool.memset(RM[:, :, :], 1.0))
                    pool.memset(RM[:, :, 0:1], 0.0).then_inc(const_ok, 1)
                    done(pool.memset(RM4[:, :, :], 1.0))
                    pool.memset(RM4[:, :, 0:1], 0.0).then_inc(const_ok, 1)
                    done(pool.memset(LTG[:, :, :], 0.0))
                    pool.affine_select(out=LTG[:, :, :], in_=LTG[:, :, :], compare_op=ALU.is_ge, fill=1.0,
                                       base=0, pattern=[[-1, NG], [1, NG]], channel_multiplier=0)\
                        .then_inc(const_ok, 1)
                if h == 7:
                    pool.iota(RH[:, :, :, 0], [[P, B], [0, KT0]], base=0, channel_multiplier=0,
                              allow_small_or_imprecise_dtypes=True).then_inc(const_ok, 1)
                    pool.iota(RH[:, :, :, 1], [[0, B], [0, KT0]], base=1, channel_multiplier=1,
                              allow_small_or_imprecise_dtypes=True).then_inc(const_ok, 1)
                    pool.memset(V9[:, :, :, :, HD:HD + 1], 1.0).then_inc(const_ok, 1)
                if h >= 5 and h % 3 == 2:
                    kpart(h // 3 - 1, 0)
                if h >= 6 and h % 3 == 0:
                    kpart(h // 3 - 2, 1)
            pool.memset(OH[:, :, :, CAP:SLOTC], 0.0).then_inc(const_ok, 1)
            done(pool.memset(ZROW[:, :], 0.0))
            pool.dma_start(rows_d.ap()[0:1, :], ZROW[:, :]).then_inc(zrow_out, 16)
            done(pool.memset(SELE[:, :, :], 0.0))
            for s in range(3):
                done(pool.affine_select(out=SELE[:, :, :], in_=SELE[:, :, :], compare_op=ALU.not_equal,
                                        fill=1.0, base=-s * E1, pattern=[[-1, E1], [0, P]],
                                        channel_multiplier=1))
            for c in range(QC):
                root(2 * c, 2 * c + 2)

            pool.wait_ge(kp_out, 16 * QC)
            def shared(u):
                n2, f = divmod(u, 3)
                m = SHF[f][1]
                pool.wait_ge(sh_th, u + 1)
                done(pool.tensor_tensor(SGT[0:m, u % 2, :], SGT[0:m, u % 2, :], THS[0:m, u % 2, :], ALU.mult))
                pool.tensor_tensor(SA[0:m, f, n2 * 512:n2 * 512 + 512], SGT[0:m, u % 2, :], SUP[0:m, u % 2, :],
                                   ALU.mult).then_inc(sh_act, 1)
                pool.wait_ge(sh_act, u + 1)

            shared(0)
            shared(1)
            pool.wait_ge(vl_ok, 1)
            done(pool.tensor_tensor(EX, EX, VL.rearrange("p (b e) -> p b e", b=B), ALU.mult))
            w = EX.rearrange("p b (k e) -> p (b k) e", e=2)
            part = [RH[:, :, :, 2 + 2 * s:4 + 2 * s].rearrange("p b k e -> p (b k) e") for s in range(3)]
            done(pool.tensor_copy(part[0], w))
            done(pool.tensor_tensor(w, w, part[0], ALU.subtract))
            done(pool.tensor_copy(part[1], w))
            pool.tensor_tensor(part[2], w, part[1], ALU.subtract).then_inc(rh_ok, 1)
            pool.wait_ge(rh_ok, 1)
            shared(2)
            shared(3)
            shared(4)
            pool.wait_ge(ix_ok, 1)
            pool.wait_ge(rows_out, 16)
            pool.wait_ge(zrow_out, 16)
            for k in range(KT0):
                if k >= 4:
                    pool.wait_ge(xb_pe, k - 3)
                pool.indirect_dma_start(XG[:, k % 4, :], None, rows_d.ap(),
                                        bass.IndirectOffsetOnAxis(ap=IX[:, k:k + 1], axis=0))\
                    .then_inc(xg_in[k % 4], 16)
                if k == 3:
                    shared(5)
            pool.wait_ge(oht_pe, KT0)
            pool.wait_ge(ix_pe, 1)
            for i in range(2):
                pool.memset(KST[i][64:96, :, :], 1.0).then_inc(kst_one, 1)
                pool.wait_ge(kst_one, i + 1)

            def padded(b):
                if b >= 2:
                    pool.wait_ge(pv_pe, (NH // 4) * (b - 1))
                for m in range(LB):
                    ins = pool.tensor_copy(V32[:, b % 2, m, :, 0:HD + 1], V9[:, m, b, :, :])
                ins.then_inc(v32_ok, 1)

            root(0, 2)
            pool.wait_ge(gu_pe, KT0)
            done(pool.memset(V32, 0.0))
            root(2, 4)
            padded(0)
            padded(1)
            root(4, 6)
            pool.wait_ge(mo_pe, QC)
            pool.memset(KST[2][64:96, :, :], 1.0).then_inc(kst_one, 1)
            pool.wait_ge(kst_one, 3)
            root(6, 8)
            for b in range(B):
                pool.wait_ge(tmp_ok, b + 1)
                pool.tensor_tensor(X[:, b, :], X[:, b, :], TMP, ALU.add).then_inc(x3_ok, 1)
                if b + 2 < B:
                    padded(b + 2)
                root(b, b + 1)
                if b == B - 3:
                    root(0, HB)
            root(HB, B)

        @block.scalar
        def _(act):
            act.dma_start(GR[:, 0:2], g_xattn.partition_broadcast(P)).then_inc(ld_g, 16)
            act.dma_start(GR[:, 2:4], g_ffn.partition_broadcast(P)).then_inc(ld_g, 16)
            for i, w in enumerate((wk, wv, wq, wm)):
                act.dma_start(WST[:, i, :], w).then_inc(ld_w, 16)
            act.dma_start(GW[:, :], gate_w).then_inc(ld_w, 16)
            for f in range(2):
                act.dma_start(ENC[:, :, f, :], enc[f, 0, 0].rearrange("(k p) d -> p k d", p=P)).then_inc(ld_enc, 16)
            act.dma_start(BVB[:, :], bv.partition_broadcast(P)).then_inc(ld_w, 16)
            act.dma_start(RW[:, :, :], rw.rearrange("(k p) e -> p k e", p=P)).then_inc(ld_w, 16)
            jn = [0]

            def job(dst, src):
                act.wait_ge(job_pe, jn[0] + 1)
                act.activation(dst, src, ACT.Copy).then_inc(job_act, 1)
                jn[0] += 1

            def bank(i, w=512):
                return PS[:, i, 0:w]

            def cast(parts, a, c, s, q):
                if c >= 1 and s == 0:
                    act.wait_ge(qp_out[c - 1] if q else kp_out, 32 if q else 16 * c)
                if q:
                    act.wait_ge(cast_in, 2 * c + s + 1)
                else:
                    act.wait_ge(k_rest if s else k_sum, c + 1)
                act.activation(parts[:, s, :], a, ACT.Copy).then_inc(cast_out, 1)

            for g in range(4):
                job(KT[:, 4 * g:4 * g + 4, :].rearrange("p k c -> p (k c)"), bank(g % 2))
            half = "(a t s) -> a t s"
            for i, v in enumerate((bk, bq)):
                act.dma_start(BST[2 * i:2 * i + 1, :], v.rearrange("(a n) -> a n", a=1)).then_inc(ld_w, 16)
                src = v.rearrange(half, t=2, s=NH)
                dst = BST[2 * i + 1:2 * i + 2, :].rearrange("p (a t s) -> p a t s", t=2, s=NH)
                for t in range(2):
                    act.dma_start(dst[:, :, t, :], src[:, 1 - t, :].rearrange("(o a) s -> o a s", o=1))\
                       .then_inc(ld_w, 16)
            act.dma_start(BST[4:5, :], bv.rearrange("(a n) -> a n", a=1)).then_inc(ld_w, 16)
            act.dma_start(BST[5:6, :], bm.rearrange("(a n) -> a n", a=1)).then_inc(ld_w, 16)
            for i, g in enumerate((0, 2, 1, 3)):
                job(QT[:, 4 * g:4 * g + 4, :].rearrange("p k c -> p (k c)"), bank(i % 2))
            act.wait_ge(ld_g, 32)
            act.activation(TGT[:, :], GR[:, :], ACT.Tanh).then_inc(act_step, 1)
            job(WT[:, :, :].rearrange("p k c -> p (k c)"), bank(0))
            job(FQ[:, :, :].rearrange("p f (k n) -> p k f n", k=LB),
                PS[:, 1, :].rearrange("p (k f n) -> p k f n", k=LB, f=2))
            job(BT[:, :], PS[:, 0, 0:6])
            job(GT[:, :, :].rearrange("p k e -> p (k e)"), PS[:, 1, 0:2 * E0])
            act.wait_ge(job_act, 12)
            for i, w in enumerate((0, 2)):
                src = WT[:, w, :].rearrange("p (a t s) -> p a t s", t=2, s=NH)
                dst = PWT[:, i, :].rearrange("p (a t s) -> p a t s", t=2, s=NH)
                for t in range(2):
                    act.activation(dst[:, :, t, :], src[:, :, 1 - t, :], ACT.Copy).then_inc(f_ok, 1)
            for c in range(QC):
                for s in range(2):
                    cast(KR["parts"], KR["a"], c, s, False)
            for c in range(QC):
                act.wait_ge(xt_pe, c + 1)
                act.activation(XNT[:, :, c * 256:c * 256 + 256], bank(6 + c % 2).rearrange("p (k n) -> p k n", k=LB),
                               ACT.Copy).then_inc(xt_act, 1)

            def shared(u):
                act.wait_ge(sh_pe, u + 1)
                if u >= 2:
                    act.wait_ge(sh_act, u - 1)
                m = SHF[u % 3][1]
                b0 = 2 + 2 * (u % 2)
                act.activation(THS[0:m, u % 2, :], PS[0:m, b0, :], ACT.Tanh, scale=0.5).then_inc(act_step, 1)
                act.activation(SGT[0:m, u % 2, :], PS[0:m, b0, :], ACT.Copy, scale=0.5)
                act.activation(SUP[0:m, u % 2, :], PS[0:m, b0 + 1, :], ACT.Copy)
                act.wait_ge(act_step, u + 2)
                act.activation(THS[0:m, u % 2, :], THS[0:m, u % 2, :], ACT.Copy, bias=1.0).then_inc(sh_th, 1)

            shared(0)
            act.wait_ge(ss_ok, 1)
            act.activation(EX, SS, ACT.Exp).then_inc(ex_ok, 1)
            for u in range(1, 6):
                shared(u)
            def xbcopy(k):
                act.wait_ge(xb_pe, k + 1)
                if k >= 2:
                    act.wait_ge(gu_pe, k - 1)
                act.activation(XB[:, k % 2, :, :], PS[:, 1, 0:256], ACT.Copy).then_inc(xb_act, 1)

            def ohcopy(k):
                act.wait_ge(oht_pe, k + 1)
                act.activation(OHT[:, k, :], PS[:, 6 + k % 2, :].bitcast(BF16), ACT.Copy).then_inc(oht_ok, 1)

            def gate(k):
                act.wait_ge(gu_pe, k + 1)
                if k >= 2:
                    act.wait_ge(as_ok, k - 1)
                act.activation(TH[:, k % 2, :], PS[:, 2 + k % 2, 0:INTER], ACT.Tanh, scale=0.5).then_inc(th_ok, 1)

            def atcopy(k):
                act.wait_ge(at_pe, k + 1)
                if k >= 2:
                    act.wait_ge(y_pe, k - 1)
                act.activation(AT[:, k % 2].rearrange("p f e c -> p (f e c)"), PS[0:HI, 0, 0:256], ACT.Copy)\
                    .then_inc(at_ok, 1)

            xbcopy(0)
            ohcopy(0)
            ohcopy(1)
            for k in range(KT0):
                gate(k)
                if k >= 1:
                    atcopy(k - 1)
                if k + 1 < KT0:
                    xbcopy(k + 1)
                if k + 2 < KT0:
                    ohcopy(k + 2)
            atcopy(KT0 - 1)
            for c in range(QC - 1):
                for s in range(2):
                    cast(QR["parts"], QR["a"], c, s, True)
            sc = 1.0 / float(HD) ** 0.5
            act.wait_ge(bmg_ok, 1)

            def exps(G):
                act.wait_ge(st_pe, G + 1)
                if G >= 4:
                    act.wait_ge(pv_pe, (G - 4) // 2 + 1)
                act.activation(PX[:, G % 4].rearrange("p h m n -> p (h m n)"),
                               PS[:, 2 * (G % 2):2 * (G % 2) + 2, :].rearrange("p a n -> p (a n)"),
                               ACT.Exp, scale=sc).then_inc(p_ok, 1)

            def heads4(Q):
                b, q = divmod(Q, NH // 4)
                act.wait_ge(pv_pe, Q + 1)
                if b >= 2:
                    act.wait_ge(on_pe, 2 * b - 2)
                act.activation(OTS[:, b % 2, q, :], PS[:, 6, 0:L], ACT.Copy).then_inc(ots_ok, 1)

            def turned(b):
                act.wait_ge(ont_pe, b + 1)
                if b >= 1:
                    act.wait_ge(wm_pe, b)
                act.activation(OT, PS[:, 7, 0:L], ACT.Copy).then_inc(ot_ok, 1)

            def gated(b):
                act.wait_ge(wm_pe, b + 1)
                if b >= 1:
                    act.wait_ge(x3_ok, b)
                act.activation(TMP, PS[:, 7, L:2 * L], ACT.Identity, bias=BMG[:, 0:1], scale=TGT[:, 1:2])\
                    .then_inc(tmp_ok, 1)

            def xturned(b):
                act.wait_ge(xt_pe, 4 + b + 1)
                act.activation(XNT[:, :, b * P:b * P + P], PS[:, 3 if b == B - 1 else 7, 0:L].rearrange("p (k t) -> p k t", k=LB), ACT.Copy)\
                    .then_inc(xt_act, 1)
                if b >= 1:
                    act.wait_ge(nq_ok, b)
                act.activation(SQ, XN[:, b, :], ACT.Square, accum_out=NQ[:, b:b + 1]).then_inc(nq_ok, 1)

            for b in range(B):
                for g in range(UN):
                    exps(b * UN + g)
                    if b == 0 and g in (5, 7):
                        cast(QR["parts"], QR["a"], QC - 1, (g - 5) // 2, True)
                    if g % 2 == 1 and b * UN + g >= 3:
                        heads4((b * UN + g) // 2 - 1)
                    if b >= 1 and g == 5:
                        turned(b - 1)
                    if b >= 1 and g == 6:
                        gated(b - 1)
                    if b >= 2 and g == 7:
                        xturned(b - 2)
            def ex4(c):
                act.wait_ge(ss4_ok, c + 1)
                act.activation(EX4[:, c * HB:c * HB + HB, :], LG4[:, c * HB:c * HB + HB, :], ACT.Exp)\
                    .then_inc(ex4_ok, 1)

            def ctturned(c):
                act.wait_ge(ct_pe, c + 1)
                act.activation(CPT[:, c * 512:c * 512 + 512], PS[0:24, 3, :].bitcast(BF16)[:, c * 512:c * 512 + 512],
                               ACT.Copy).then_inc(ct_ok, 1)

            heads4(B * NH // 4 - 1)
            ex4(0)
            turned(B - 1)
            gated(B - 1)
            ctturned(0)
            xturned(B - 2)
            for u in range(2 * E1):
                act.wait_ge(cb_pe, u + 1)
                if u >= 2:
                    act.wait_ge(ae_ok, u - 1)
                act.activation(CB[:, u % 2, :], bank(6 + u % 2), ACT.Copy).then_inc(cb_ok, 1)
                if u == 2:
                    xturned(B - 1)
                if u == 3:
                    ex4(1)
                if u == 6:
                    ctturned(1)

        @block.tensor
        def _(pe):
            pe.wait_ge(const_ok, 1)
            jn = [0]

            def job(parts):
                if jn[0] >= 2:
                    pe.wait_ge(job_act, jn[0] - 1)
                last = None
                for f in parts:
                    last = f(jn[0] % 2)
                last.then_inc(job_pe, 1)
                jn[0] += 1

            def turn(src, off, idn=IDF, m=P):
                w = src.shape[0]
                return lambda bk_: pe.transpose(PS[0:m, bk_, off:off + w], src, idn[0:w, 0:w])

            pe.wait_ge(cr_ok, 1)
            for g in range(4):
                lb, b0 = divmod(4 * g, B)
                job([turn(CR[:, b0 + i, lb, :], i * P) for i in range(4)])
            for g in (0, 2, 1, 3):
                lb, b0 = divmod(4 * g, B)
                pe.wait_ge(ln_ok, 1 + b0 // HB)
                job([turn(XN[:, b0 + i, lb * P:lb * P + P], i * P) for i in range(4)])
            def tables():
                pe.wait_ge(ld_w, 16 * 15)
                job([turn(WST[:, i, :], i * P) for i in range(4)])
                pe.wait_ge(enc_ok, 1)
                job([turn(EB[:, k, f, :], (k * 2 + f) * P) for k in range(LB) for f in range(2)])
                job([turn(BST, 0)])
                job([turn(GW[:, k * P:k * P + P], k * E0) for k in range(LB)])

            def conv(h):
                pe.wait_ge(kv_ready, h + 1)
                if h == 0:
                    pe.wait_ge(ld_tt, 16)
                if h >= 2:
                    pe.wait_ge(z_done, h - 1)
                b0 = 2 + 2 * (h % 2)
                pe.matmul(PS[:, b0, :], TT[:, h, 0:P], KV[:, h % 4, 0:512], start=True, stop=True)
                pe.matmul(PS[:, b0 + 1, :], TT[:, h, P:L], KV[:, h % 4, 0:512], start=True, stop=False)
                pe.matmul(PS[:, b0 + 1, :], TT[:, h, 0:P], KV[:, h % 4, 512:1024], start=False, stop=True)\
                    .then_inc(conv_done, 1)

            def rope_mm(c, w, src, sem_pe, sem_free, b0):
                if c >= 1 and sem_free is not None:
                    pe.wait_ge(sem_free, c)
                rhs = src[:, 2 * c:2 * c + 2, :].rearrange("p b n -> p (b n)")
                pe.matmul(PS[:, b0, :], WT[:, w, :], rhs, start=True, stop=True)
                pe.matmul(PS[:, b0 + 1, :], PWT[:, w // 2, :], rhs, start=True, stop=True).then_inc(sem_pe, 1)

            def vproj(g):
                lb, b0 = divmod(4 * g, B)
                fs = []
                for i in range(4):
                    fs.append(lambda bk_, i=i: pe.matmul(PS[:, bk_, i * P:i * P + P],
                                                         CTX[:, b0 + i, lb * P:lb * P + P], WT[:, 1, :],
                                                         start=True, stop=True))
                job(fs)

            for h in range(NH):
                conv(h)
                if h == 1:
                    tables()
                    pe.wait_ge(f_ok, 4)
                if 1 <= h and h % 3 == 1 and h // 3 < QC:
                    rope_mm(h // 3, 0, CTX, kp_pe, kp_free, 6)
                if h >= 1 and h % 3 == 2 and h // 3 < 4:
                    vproj(h // 3)
            pe.wait_ge(ol_done, NH)
            for g in range(4):
                pe.wait_ge(z_done, NH)
                for i in range(4):
                    b, lb = 2 * g + i // 2, i % 2
                    last = pe.transpose(PS[:, 2 + g, i * P:i * P + P], OL[:, lb * B + b, :], IDF[:, :])
                last.then_inc(ot_pe, 1)

            def logits0(c):
                for b in (2 * c, 2 * c + 1):
                    for k in range(LB):
                        last = pe.matmul(PS[:, 0, b * E0:b * E0 + E0], XNT[:, k, b * P:b * P + P], GT[:, k, :],
                                         start=(k == 0), stop=(k == 1))
                return last

            pe.wait_ge(kp_free, QC)
            pe.wait_ge(job_act, NJ)
            for c in range(QC):
                pe.wait_ge(ln_ok, LN2 + c + 1)
                if c >= 2:
                    pe.wait_ge(xt_act, c - 1)
                for k in range(LB):
                    for i in range(2):
                        last = pe.transpose(PS[:, 6 + c % 2, (2 * k + i) * P:(2 * k + i + 1) * P],
                                            XN[:, 2 * c + i, k * P:k * P + P], IDF[:, :])
                last.then_inc(xt_pe, 1)
                if c >= 1:
                    pe.wait_ge(xt_act, c)
                    logits0(c - 1)
            pe.wait_ge(xt_act, QC)
            logits0(QC - 1).then_inc(lg_pe, 1)
            pe.wait_ge(ld_sh, 48)
            pe.wait_ge(ot_x, 4)

            def shared(u):
                n2, f = divmod(u, 3)
                f0, m = SHF[f]
                if u >= 2:
                    pe.wait_ge(sh_th, u - 1)
                for half in range(2):
                    for k in range(LB):
                        last = pe.matmul(PS[0:m, 2 + 2 * (u % 2) + half, :],
                                         SHW[:, k, half * SH + f0:half * SH + f0 + m],
                                         XNT[:, k, n2 * 512:n2 * 512 + 512], start=(k == 0), stop=(k == 1))
                last.then_inc(sh_pe, 1)

            shared(0)
            shared(1)
            pe.wait_ge(selb_ok, 1)
            pe.wait_ge(const_ok, 3)
            flat = SELB[:, :, :].rearrange("p b e -> p (b e)")
            pe.matmul(PS[:, 1, 0:256], UPB[:, :], flat, start=True, stop=True)
            for k in range(1, B):
                last = pe.matmul(PS[:, 1, k * E0:256], ONB[:, :], flat[:, 0:(B - k) * E0], start=False,
                                 stop=True, skip_group_check=True)
            last.then_inc(pos_pe, 1)
            for u in range(2, 6):
                shared(u)
            pe.wait_ge(rh_ok, 1)
            for b in range(B):
                pe.wait_ge(oh_ok, b + 1)
                for k in range(KT0):
                    last = pe.matmul(PS[:, 0, k * 8:k * 8 + 8],
                                     OH[:, b, 2 * k:2 * k + 2, :].rearrange("p e c -> p (e c)"),
                                     RH[:, b, k, :], start=(b == 0 and k == 0), stop=True, skip_group_check=True)
            last.then_inc(ix_pe, 1)

            def oh_turn(k):
                if k >= 2:
                    pe.wait_ge(oht_ok, k - 1)
                dst = PS[:, 6 + k % 2, :].bitcast(BF16)
                for b in range(B):
                    last = pe.transpose(dst[:, b * P:b * P + P],
                                        OH[:, b, 2 * k:2 * k + 2, :].rearrange("p e c -> p (e c)"), IDB[:, :])
                last.then_inc(oht_pe, 1)

            def xb_turn(k):
                pe.wait_ge(xg_in[k % 4], 16 * (k // 4 + 1))
                if k >= 1:
                    pe.wait_ge(xb_act, k)
                for j in range(LB):
                    last = pe.transpose(PS[:, 1, j * P:j * P + P], XG[:, k % 4, j * P:j * P + P], IDF[:, :])
                last.then_inc(xb_pe, 1)

            def up(k):
                pe.wait_ge(xb_act, k + 1)
                if k >= 2:
                    pe.wait_ge(as_ok, k - 1)
                pe.wait_ge(ld_up[k % NPAIR], 16 * (k // NPAIR + 1))
                for j in range(LB):
                    for eo in range(2):
                        last = pe.matmul(PS[eo * SLOTC:eo * SLOTC + SLOTC, 2 + k % 2, 0:2 * INTER],
                                         XB[:, k % 2, j, eo * SLOTC:eo * SLOTC + SLOTC],
                                         WG[:, (2 * k + eo) % NRING, j, :], start=(j == 0), stop=(j == 1))
                last.then_inc(gu_pe, 1)

            def at_turn(k):
                pe.wait_ge(as_ok, k + 1)
                if k >= 1:
                    pe.wait_ge(at_ok, k)
                for f in range(2):
                    last = pe.transpose(PS[0:HI, 0, f * P:f * P + P], AS[:, k % 2, f * HI:f * HI + HI], IDF[:, :])
                last.then_inc(at_pe, 1)

            def down(k):
                pe.wait_ge(at_ok, k + 1)
                pe.wait_ge(ld_down[k % NPAIR], 16 * (k // NPAIR + 1))
                if k >= 2:
                    pe.wait_ge(y_ok, k - 1)
                for f in range(2):
                    for eo in range(2):
                        last = pe.matmul(PS[eo * 64:eo * 64 + 64, 4 + k % 2, 0:256], AT[:, k % 2, f, eo, :],
                                         WD[0:HI, (2 * k + eo) % NRING, f, :], start=(f == 0), stop=(f == 1))
                last.then_inc(y_pe, 1)

            oh_turn(0)
            oh_turn(1)
            xb_turn(0)
            for k in range(KT0):
                up(k)
                if k >= 1:
                    at_turn(k - 1)
                if k + 1 < KT0:
                    xb_turn(k + 1)
                if k + 2 < KT0:
                    oh_turn(k + 2)
                if k >= 1:
                    down(k - 1)
            at_turn(KT0 - 1)
            down(KT0 - 1)
            def smax(H):
                b, h = divmod(H, NH)
                if H == 0:
                    pe.wait_ge(qp_free, 2)
                if h == 0:
                    pe.wait_ge(st_in[b % 3], 16 * 6 * (b // 3 + 1))
                if H >= 2:
                    pe.wait_ge(s_max, H - 1)
                for m in range(LB):
                    last = pe.matmul(PS[:, 4 + H % 2, m * L:m * L + L], QST[b % 3][0:NT, h, m * P:m * P + P],
                                     KST[b % 3][0:NT, h, :], start=True, stop=True)
                last.then_inc(s_pe, 1)

            def maxturn(b):
                pe.wait_ge(ms_ok, b + 1)
                if b >= 2:
                    pe.wait_ge(on_ok, 2 * b - 2)
                elif b == 1:
                    pe.wait_ge(qp_free, QC + 1)
                else:
                    pe.wait_ge(qp_free, 1)
                pe.transpose(PS[0:96, 7, 0:64].bitcast(BF16), MS[:, :, :].rearrange("p s n -> p (s n)"), IDB[:, :])\
                    .then_inc(mt_pe, 1)

            early = list(range(EARLY))
            pe.wait_ge(sh_act, 6)
            pe.wait_ge(oht_ok, KT0)
            pe.wait_ge(th_ok, KT0)
            for b in range(B):
                o = PS[:, b // 2, (b % 2) * L:(b % 2) * L + L]
                for f, (f0, m) in enumerate(SHF):
                    pe.matmul(o, SA[0:m, f, b * P:b * P + P], SHD[0:m, f, :], start=(f == 0), stop=False)
                for k in range(KT0):
                    if b == 0:
                        pe.wait_ge(y_ok, k + 1)
                    for s in range(3):
                        last = pe.matmul(o, OHT[:, k, b * P:b * P + P], Y[:, k, s, :], start=False,
                                         stop=(k == KT0 - 1 and s == 2))
                    if b == B - 2 and k >= KT0 // 4 or b == B - 1 and k % 2 == 1:
                        smax(early.pop(0))
                        if early and early[0] == NH + 1:
                            maxturn(0)
                if b % 2 == 1:
                    last.then_inc(mo_pe, 1)
                elif b >= 2:
                    pe.wait_ge(ln_ok, LN3 + b // 2)
                    rope_mm(b // 2 - 1, 2, XN, qp_pe, None, QBANK[b // 2 - 1])


            def scores(G):
                b, g = divmod(G, UN)
                if g == 0:
                    pe.wait_ge(mrow_in, 48 * (b + 1))
                if G == 0:
                    pe.wait_ge(qp_free, QC - 1)
                if G == 1:
                    pe.wait_ge(mo_x, QC)
                if G >= 2:
                    pe.wait_ge(p_ok, G - 1)
                for hh in range(2):
                    for m in range(LB):
                        last = pe.matmul(PS[:, 2 * (G % 2) + hh, m * L:m * L + L],
                                         KST[b % 3][0:SROWS, 2 * g + hh, m * P:m * P + P],
                                         QST[b % 3][0:SROWS, 2 * g + hh, :], start=True, stop=True)
                last.then_inc(st_pe, 1)

            def values(Q, m):
                b, q = divmod(Q, NH // 4)
                if m == 0:
                    pe.wait_ge(p_ok, 2 * Q + 2)
                    if q == 0:
                        pe.wait_ge(v32_ok, b + 1)
                    if Q >= 1:
                        pe.wait_ge(ots_ok, Q)
                for j in range(4):
                    last = pe.matmul(PS[32 * j:32 * j + 32, 6, 0:L], V32[:, b % 2, m, 4 * q + j, :],
                                     PX[:, (2 * Q + j // 2) % 4, j % 2, m, :], start=(m == 0), stop=(m == 1))
                if m == 1:
                    last.then_inc(pv_pe, 1)

            def back(b, n):
                pe.wait_ge(ots_ok, (NH // 4) * (b + 1))
                if n == 1:
                    pe.wait_ge(on_ok, 2 * b + 1)
                elif b >= 2:
                    pe.wait_ge(xt_act, 4 + b - 1)
                elif b == 1:
                    pe.wait_ge(tmp_ok, 1)
                else:
                    pe.wait_ge(mr_ok, 2)
                for q in range(NH // 4):
                    last = pe.transpose(PS[:, 7, q * P:q * P + P], OTS[:, b % 2, q, n * P:n * P + P], IDF[:, :])
                last.then_inc(on_pe, 1)

            def outturn(b):
                pe.wait_ge(on_ok, 2 * b + 2)
                if b + 2 < B:
                    pe.wait_ge(mr_ok, b + 3)
                for n in range(LB):
                    last = pe.transpose(PS[:, 7, n * P:n * P + P], ON[:, n].rearrange("p d h -> p (d h)"), IDF[:, :])
                last.then_inc(ont_pe, 1)

            def project(b):
                pe.wait_ge(ot_ok, b + 1)
                pe.matmul(PS[:, 7, 256:512], WT[:, 3, :], OT, start=True, stop=True).then_inc(wm_pe, 1)

            def xturn(b):
                pe.wait_ge(ln_ok, LN4 + b + 1)
                pe.wait_ge(tmp_ok, min(b + 2, B))
                for k in range(LB):
                    last = pe.transpose(PS[:, 3 if b == B - 1 else 7, k * P:k * P + P], XN[:, b, k * P:k * P + P], IDF[:, :])
                last.then_inc(xt_pe, 1)

            q = list(range(EARLY, B * NH))

            def qlast(i):
                if i == 0:
                    pe.wait_ge(ln_ok, LN4)
                    pe.wait_ge(mr_ok, 1)
                else:
                    pe.wait_ge(qp_free, QC)
                rhs = XN[:, B - 2:B, :].rearrange("p b n -> p (b n)")
                pe.matmul(PS[:, 7, :], PWT[:, 1, :] if i else WT[:, 2, :], rhs, start=True, stop=True)\
                    .then_inc(qp_pe, 1)

            for b in range(B):
                for g in range(UN):
                    G = b * UN + g
                    scores(G)
                    if q:
                        smax(q.pop(0))
                    if G >= 2:
                        values(G // 2 - 1, g % 2)
                    for _ in range(2 if G < RISE else 1):
                        if q:
                            smax(q.pop(0))
                    if b == 0 and g in (2, 3):
                        qlast(g - 2)
                    if g == NH - LEAD and b + 1 < B:
                        maxturn(b + 1)
                    if g == 7 and b >= 2:
                        xturn(b - 2)
                    if b >= 1:
                        if g == 2:
                            back(b - 1, 0)
                        if g == 3:
                            back(b - 1, 1)
                        if g == 5:
                            outturn(b - 1)
                        if g == 6:
                            project(b - 1)

            def logits(c):
                for b in range(c * HB, c * HB + HB):
                    pe.wait_ge(xt_act, 4 + b + 1)
                    for k in range(LB):
                        last = pe.matmul(PS[:, 2, b * E1:b * E1 + E1], XNT[:, k, b * P:b * P + P], RW[:, k, :],
                                         start=(k == 0), stop=(k == 1))
                last.then_inc(lg_pe, 1)

            def ctturn(c):
                pe.wait_ge(c_ok, c + 1)
                if c == 1:
                    pe.wait_ge(xt_act, 4 + B)
                dst = PS[0:3 * E1, 3, :].bitcast(BF16)
                for b in range(c * HB, c * HB + HB):
                    last = pe.transpose(dst[:, b * P:b * P + P], CP[:, b].rearrange("p s e -> p (s e)"), IDB[:, :])
                last.then_inc(ct_pe, 1)

            def inner(u):
                c, e = divmod(u, E1)
                if u >= 2:
                    pe.wait_ge(ae_ok, u - 1)
                for k in range(LB):
                    last = pe.matmul(PS[:, 4 + u % 2, :], WA[:, e, k, :], XNT[:, k, c * 512:c * 512 + 512],
                                     start=(k == 0), stop=(k == 1))
                last.then_inc(a_pe, 1)

            def weights(u):
                c, e = divmod(u, E1)
                if e == 0:
                    pe.wait_ge(ct_ok, c + 1)
                if u == 1:
                    pe.wait_ge(xt_act, 4 + B - 1)
                if u >= 2:
                    pe.wait_ge(cb_ok, u - 1)
                pe.matmul(PS[:, 6 + u % 2, :], SELE[:, e, :], CPT[:, c * 512:c * 512 + 512], start=True,
                          stop=True).then_inc(cb_pe, 1)

            values(B * NH // 4 - 1, 0)
            values(B * NH // 4 - 1, 1)
            pe.wait_ge(p_ok, B * UN)
            logits(0)
            back(B - 1, 0)
            pe.wait_ge(s_max, B * NH)
            pe.wait_ge(ld_ab, 32)
            inner(0)
            back(B - 1, 1)
            inner(1)
            outturn(B - 1)
            project(B - 1)
            ctturn(0)
            xturn(B - 2)
            weights(0)
            weights(1)
            for u in range(2 * E1):
                c, e = divmod(u, E1)
                pe.wait_ge(ae_ok, u + 1)
                for t in range(4):
                    last = pe.matmul(PS[:, 2 * c + t // 2, (t % 2) * L:(t % 2) * L + L],
                                     AE[:, u % 2, t * P:t * P + P], WB[:, e, :],
                                     start=(e == 0 and t % 2 == 0), stop=True, skip_group_check=True)
                last.then_inc(o_pe, 1)
                if u == 1:
                    pe.wait_ge(ct_ok, 1)
                    xturn(B - 1)
                if u == 2:
                    logits(1)
                if u == 5:
                    ctturn(1)
                if u + 2 < 2 * E1:
                    inner(u + 2)
                    weights(u + 2)

        @block.vector
        def _(dve):
            n = [0]

            def done(ins):
                n[0] += 1
                ins.then_inc(dve_step, 1)
                dve.wait_ge(dve_step, n[0])

            def bc(v, shape, axis):
                return v.unsqueeze(axis).to_broadcast(shape)

            lk = [0]

            def stats(bs):
                for b in bs:
                    ins = dve.bn_stats(STT[:, b, :], X[:, b, :])
                done(ins)
                for b in bs:
                    ins = dve.bn_aggr(MV[:, b, :], STT[:, b, :])
                done(ins)
                dve.tensor_scalar(RSA[:, bs[0]:bs[-1] + 1], MV[:, bs[0]:bs[-1] + 1, 1], EPS, None, ALU.add)\
                    .then_inc(ln_var, 1)

            def apply(bs):
                lk[0] += 1
                dve.wait_ge(ln_pow, lk[0])
                for b in bs:
                    ins = dve.tensor_scalar(XN[:, b, :], X[:, b, :], MV[:, b, 0:1], RS[:, b:b + 1],
                                            ALU.subtract, ALU.mult)
                ins.then_inc(ln_ok, 1)

            done(dve.memset(KPAD[:, 0:P], 0.0))
            dve.wait_ge(ld_ssm, 32)
            dve.tensor_tensor(KPAD[:, P:P + 1], KPAD[:, P:P + 1], DSK[:, :], ALU.add).then_inc(kpad_ok, 1)
            dve.wait_ge(ld_ctx, 16)
            dve.tensor_copy(CR, CTX[:, :, :].rearrange("p b (k n) -> p b k n", k=LB)[:, :, :, ::-1]).then_inc(cr_ok, 1)
            dve.wait_ge(ld_x, 16)
            stats(range(HB))
            stats(range(HB, B))
            apply(range(HB))
            apply(range(HB, B))
            dve.wait_ge(ld_enc, 32)
            even = ENC[:, :, 1, :].rearrange("p k (a t) -> p k a t", t=2)[:, :, :, 0]
            done(dve.tensor_scalar(even, even, -1.0, None, ALU.mult))
            for k in range(LB):
                ins = dve.tensor_copy(EB[:, k].rearrange("p f (d h) -> p f d h", h=NH),
                                      bc(ENC[:, k], [P, 2, HD, NH], 3))
            ins.then_inc(enc_ok, 1)

            def two(v):
                return v.rearrange("p (b n) -> p b n", b=2)

            def rope(c, R, bias, sem_pe, sem_free, sem_parts, cast0, b0):
                def turn_up():
                    dve.wait_ge(sem_pe, c + 1)
                    if c >= 1:
                        dve.wait_ge(sem_parts, c)
                    dve.scalar_tensor_tensor(out=two(R["a"]), in0=two(PS[:, b0, :]), scalar=BT[:, bias:bias + 1],
                                             in1=bc(FQ[:, 0, :], [P, 2, L], 1), op0=ALU.add, op1=ALU.mult)
                    dve.scalar_tensor_tensor(out=two(R["b"]), in0=two(PS[:, b0 + 1, :]),
                                             scalar=BT[:, bias + 1:bias + 2],
                                             in1=bc(FQ[:, 1, :], [P, 2, L], 1), op0=ALU.add, op1=ALU.mult)\
                        .then_inc(sem_free, 1)

                def add_up():
                    dve.wait_ge(sem_free, c + 1)
                    dve.tensor_tensor(R["a"], R["a"], R["b"], ALU.add)\
                        .then_inc(cast_in if cast0 >= QC else k_sum, 1)

                def rest():
                    dve.wait_ge(cast_out, 2 * cast0 + 1)
                    dve.tensor_tensor(R["a"], R["a"], R["parts"][:, 0, :], ALU.subtract).then_inc(cast_in, 1)

                def last():
                    dve.wait_ge(cast_out, 2 * cast0 + 2)
                    dve.tensor_tensor(R["parts"][:, 2, :], R["a"], R["parts"][:, 1, :], ALU.subtract)\
                        .then_inc(sem_parts, 1)
                return [turn_up, add_up, rest, last]

            def krope(c):
                if c == 0:
                    dve.wait_ge(job_act, 12)

                for step in rope(c, KR, 0, kp_pe, kp_free, kp_parts, c, 6)[0:2]:
                    step()

            def vout(g):
                lb, b0 = divmod(4 * g, B)
                dve.wait_ge(job_pe, 12 + g + 1)
                src = PS[:, g % 2, :].rearrange("p (b c) -> p b c", b=4)
                for i in range(4):
                    ins = dve.tensor_tensor(V9[:, lb, b0 + i, :, 0:HD].rearrange("p h d -> p d h"),
                                            src[:, i, :].rearrange("p (d h) -> p d h", h=NH),
                                            BVB[:, :].rearrange("p (d h) -> p d h", h=NH), ALU.add)
                ins.then_inc(job_act, 1)

            def zmul(h):
                dve.wait_ge(conv_done, h + 1)
                b0 = 2 + 2 * (h % 2)
                zz = Z[:, h % 2, :].rearrange("p (k j i) -> p k j i", j=HD, i=HD)
                yy = PS[:, b0:b0 + 2, :].rearrange("p a n -> p (a n)").rearrange("p (k j i) -> p k j i", j=HD, i=HD)
                dve.tensor_tensor(zz, yy, bc(QT[:, :, h * HD:h * HD + HD], [P, LB * B, HD, HD], 2), ALU.mult)\
                    .then_inc(z_done, 1)
                dve.wait_ge(z_done, h + 1)
                dve.tensor_reduce(OL[:, :, h * HD:h * HD + HD], zz, AX, ALU.add).then_inc(ol_done, 1)

            dve.wait_ge(job_act, 8)
            for h in range(NH):
                zmul(h)
                if 1 <= h and h % 3 == 1 and h // 3 < QC:
                    krope(h // 3)
                if h >= 1 and h % 3 == 2 and h // 3 < 4:
                    vout(h // 3)
            dve.wait_ge(act_step, 1)
            for g in range(4):
                dve.wait_ge(ot_pe, g + 1)
                v = X[:, 2 * g:2 * g + 2, :].rearrange("p b l -> p (b l)")
                ins = dve.scalar_tensor_tensor(out=v, in0=PS[:, 2 + g, :], scalar=TGT[:, 0:1], in1=v,
                                               op0=ALU.mult, op1=ALU.add)
                ins.then_inc(ot_x, 1)
                dve.wait_ge(ot_x, g + 1)
                stats(range(2 * g, 2 * g + 2))
                if g >= 1:
                    apply(range(2 * g - 2, 2 * g))
            apply(range(B - 2, B))

            dve.wait_ge(lg_pe, 1)
            dve.wait_ge(const_ok, 10)
            done(dve.tensor_copy(LG.rearrange("p b e -> p (b e)"), PS[:, 0, 0:256]))
            done(dve.tensor_reduce(GS, LG.rearrange("p b (g k) -> p b g k", g=NG), AX, ALU.max))
            sh4 = [P, B, NG, NG]
            dve.tensor_tensor(C1, bc(GS, sh4, 2), bc(GS, sh4, 3), ALU.is_gt)
            done(dve.tensor_tensor(C2, bc(GS, sh4, 2), bc(GS, sh4, 3), ALU.is_equal))
            done(dve.tensor_tensor(C2, C2, bc(LTG[:, :, :], sh4, 1), ALU.mult))
            done(dve.tensor_tensor(C1, C1, C2, ALU.add))
            done(dve.tensor_reduce(RK, C1, AX, ALU.add))
            done(dve.tensor_scalar(RK, RK, float(TG), None, ALU.is_lt))
            g4 = "p b (g k) -> p (b g) k"
            done(dve.tensor_tensor(SC.rearrange(g4, k=GE), LG.rearrange(g4, k=GE),
                                   bc(RK.rearrange("p b g -> p (b g)"), [P, B * NG, GE], 2), ALU.mult))
            for b in range(B):
                ins = dve.max(M8[:, b, :], SC[:, b, :])
            done(ins)
            sh3 = [P, B, E0]
            dve.tensor_tensor(SS, SC, bc(M8[:, :, 0], sh3, 2), ALU.subtract).then_inc(ss_ok, 1)
            dve.tensor_tensor(EQ, SC, bc(M8[:, :, TOPK0 - 1], sh3, 2), ALU.is_equal)
            done(dve.tensor_tensor(GTR, SC, bc(M8[:, :, TOPK0 - 1], sh3, 2), ALU.is_gt))
            done(dve.tensor_reduce(CNT, GTR, AX, ALU.add))
            done(dve.tensor_scalar(CNT, CNT, -1.0, float(TOPK0), ALU.mult, ALU.add))
            fl = "p b e -> p (b e)"
            done(dve.tensor_tensor_scan(PF.rearrange(fl), RM[:, :, :].rearrange(fl), EQ.rearrange(fl), 0.0,
                                        ALU.mult, ALU.add))
            done(dve.tensor_tensor(PF, PF, bc(CNT, sh3, 2), ALU.is_le))
            done(dve.tensor_tensor(EQ, EQ, PF, ALU.mult))
            done(dve.tensor_tensor(SEL, GTR, EQ, ALU.add))
            dve.tensor_copy(SELB[:, :, :], SEL).then_inc(selb_ok, 1)
            dve.wait_ge(ex_ok, 1)
            done(dve.tensor_reduce(SE, EX, AX, ALU.add))
            done(dve.reciprocal(SE, SE))
            done(dve.tensor_scalar(SE, SE, SCALE0, None, ALU.mult))
            done(dve.tensor_tensor(EX, EX, bc(SE, sh3, 2), ALU.mult))

            dve.wait_ge(pos_pe, 1)
            dve.scalar_tensor_tensor(out=VL, in0=PS[:, 1, 0:256], scalar=float(CAP),
                                     in1=SEL.rearrange(fl), op0=ALU.is_lt, op1=ALU.mult).then_inc(vl_ok, 1)
            dve.wait_ge(vl_ok, 1)
            done(dve.scalar_tensor_tensor(out=PK[:, :, :].rearrange(fl), in0=PS[:, 1, 0:256], scalar=float(SLOTC),
                                          in1=VL, op0=ALU.subtract, op1=ALU.mult))
            done(dve.tensor_scalar(PK[:, :, :], PK[:, :, :], float(SLOTC), None, ALU.add))
            dve.wait_ge(const_ok, 11)
            for b in range(B):
                dve.tensor_tensor(OH[:, b, :, 0:CAP], bc(PK[:, b, :], [P, E0, CAP], 2),
                                  bc(IOT[:, :], [P, E0, CAP], 1), ALU.is_equal).then_inc(oh_ok, 1)
            dve.wait_ge(ix_pe, 1)
            ixv = PS[:, 0, 0:KT0 * 8].rearrange("p (k c) -> p k c", c=8)
            done(dve.tensor_copy(WS[:, :], ixv[:, :, 0]))
            dve.tensor_tensor(IX[:, :], WS[:, :], ixv[:, :, 1], ALU.add).then_inc(ix_ok, 1)
            dve.wait_ge(ix_ok, 1)
            for eo in range(2):
                rows = slice(eo * 64, eo * 64 + 64)
                done(dve.tensor_reduce(WS[rows, :],
                                       ixv[rows, :, 2 + eo:8][:, :, 0:5:2], AX, ALU.add))

            def silu(k):
                dve.wait_ge(th_ok, k + 1)
                if k >= 1:
                    dve.wait_ge(as_ok, k)
                if k >= 2:
                    dve.wait_ge(at_pe, k - 1)
                g, u = PS[:, 2 + k % 2, 0:INTER], PS[:, 2 + k % 2, INTER:2 * INTER]
                done(dve.scalar_tensor_tensor(out=A1[:, :], in0=TH[:, k % 2, :], scalar=1.0, in1=g,
                                              op0=ALU.add, op1=ALU.mult))
                dve.scalar_tensor_tensor(out=AS[:, k % 2, :], in0=A1[:, :], scalar=0.5, in1=u,
                                         op0=ALU.mult, op1=ALU.mult).then_inc(as_ok, 1)

            def yout(k):
                dve.wait_ge(y_pe, k + 1)
                if k >= 1:
                    dve.wait_ge(y_ok, k)
                yp = PS[:, 4 + k % 2, 0:256]
                done(dve.tensor_scalar(Y[:, k, 0, :], yp, WS[:, k:k + 1], None, ALU.mult))
                done(dve.scalar_tensor_tensor(out=YR[:, :], in0=yp, scalar=WS[:, k:k + 1], in1=Y[:, k, 0, :],
                                              op0=ALU.mult, op1=ALU.subtract))
                done(dve.tensor_copy(Y[:, k, 1, :], YR[:, :]))
                dve.tensor_tensor(Y[:, k, 2, :], YR[:, :], Y[:, k, 1, :], ALU.subtract).then_inc(y_ok, 1)

            for k in range(KT0):
                silu(k)
                if k == 1:
                    dve.wait_ge(sh_act, 6)
                if k >= 1:
                    yout(k - 1)
            yout(KT0 - 1)
            def qrope(c):
                return rope(c, QR, 2, qp_pe, qp_free, qp_parts, QC + c, QBANK[c % len(QBANK)])

            dve.wait_ge(rows_out, 16)
            dve.tensor_scalar(BMG[:, :], BT[:, 5:6], TGT[:, 1:2], None, ALU.mult).then_inc(bmg_ok, 1)
            def rowmax(H):
                dve.wait_ge(s_pe, H + 1)
                dve.tensor_reduce(MX[:, H % NH, :], PS[:, 4 + H % 2, :].rearrange("p (m n) -> p m n", m=LB),
                                  AX, ALU.max).then_inc(s_max, 1)

            def maxparts(b):
                dve.wait_ge(s_max, NH * (b + 1))
                if b >= 1:
                    dve.wait_ge(ms_ok, b)
                if b >= 1:
                    dve.wait_ge(mt_pe, b)
                m = MX[:, :, :].rearrange("p h m -> p (h m)")
                done(dve.tensor_scalar(MS[:, 0, :], m, -1.0, None, ALU.mult))
                done(dve.scalar_tensor_tensor(out=MXR[:, :], in0=m, scalar=-1.0, in1=MS[:, 0, :], op0=ALU.mult,
                                              op1=ALU.subtract))
                done(dve.tensor_copy(MS[:, 1, :], MXR[:, :]))
                dve.tensor_tensor(MS[:, 2, :], MXR[:, :], MS[:, 1, :], ALU.subtract).then_inc(ms_ok, 1)

            def maxcopy(b):
                dve.wait_ge(mt_pe, b + 1)
                if b >= 1:
                    dve.wait_ge(mrow_in, 48 * b)
                dve.tensor_copy(MR[0:96, :], PS[0:96, 7, 0:64].bitcast(BF16)).then_inc(mr_ok, 1)

            for g in range(QC):
                dve.wait_ge(mo_pe, g + 1)
                v = X[:, 2 * g:2 * g + 2, :].rearrange("p b l -> p (b l)")
                dve.scalar_tensor_tensor(out=v, in0=PS[:, g, :], scalar=TGT[:, 2:3], in1=v,
                                         op0=ALU.mult, op1=ALU.add).then_inc(mo_x, 1)
                if g < QC - 1:
                    dve.wait_ge(mo_x, g + 1)
                    stats(range(2 * g, 2 * g + 2))
                    apply(range(2 * g, 2 * g + 2))
                    steps = qrope(g)
                    if g < QC - 2:
                        for step in steps:
                            step()
                    else:
                        for H in range(EARLY):
                            rowmax(H)
                            if H >= 11 and steps:
                                steps.pop(0)()
                            if H == NH - 1:
                                maxparts(0)
                            if H == NH:
                                maxcopy(0)

            def normal(b, m):
                dve.wait_ge(on_pe, 2 * b + m + 1)
                if b >= 1 and m == 0:
                    dve.wait_ge(ont_pe, b)
                o = PS[:, 7, :].rearrange("p (h c) -> p h c", h=NH)
                done(dve.reciprocal(RO[:, m, :], o[:, :, HD]))
                dve.tensor_tensor(ON[:, m], o[:, :, 0:HD].rearrange("p h d -> p d h"),
                                  bc(RO[:, m, :], [P, HD, NH], 1), ALU.mult).then_inc(on_ok, 1)

            q = list(range(EARLY, B * NH))
            def asknorm(c):
                dve.wait_ge(nq_ok, HB * (c + 1))
                dve.tensor_scalar(RSA[:, c * HB:c * HB + HB], NQ[:, c * HB:c * HB + HB], 1e-24, None, ALU.max)\
                    .then_inc(ln_var, 1)

            last2 = range(B - 2, B)

            def qlast(i):
                dve.wait_ge(qp_pe, QC + i)
                if i == 0:
                    dve.wait_ge(qp_parts, QC - 1)
                dve.scalar_tensor_tensor(out=two(QR["b" if i else "a"]), in0=two(PS[:, 7, :]),
                                         scalar=BT[:, 2 + i:3 + i], in1=bc(FQ[:, i, :], [P, 2, L], 1),
                                         op0=ALU.add, op1=ALU.mult).then_inc(qp_free, 1)

            def qlastsum():
                dve.wait_ge(qp_free, QC + 1)
                dve.tensor_tensor(QR["a"], QR["a"], QR["b"], ALU.add).then_inc(cast_in, 1)

            late = [lambda: (dve.wait_ge(mo_x, QC), stats(last2)), lambda: apply(last2), lambda: qlast(0),
                    lambda: qlast(1), qlastsum, lambda: None, qrope(QC - 1)[2], lambda: None, qrope(QC - 1)[3]]
            for b in range(B):
                for g in range(UN):
                    if b >= 2 and g == 0:
                        dve.wait_ge(x3_ok, b - 1)
                        stats([b - 2])
                    if g == NH - LEAD and b + 1 < B:
                        maxparts(b + 1)
                    for _ in range(3 if b * UN + g < RISE else 2):
                        if q:
                            rowmax(q.pop(0))
                    if late:
                        late.pop(0)()
                    if g == NH - LEAD and b + 1 < B:
                        maxcopy(b + 1)
                    if b >= 2 and g == 1:
                        apply([b - 2])
                    if b == B - 1 and g == 2:
                        asknorm(0)
                    if b >= 1:
                        if g == 2:
                            normal(b - 1, 0)
                        if g == 3:
                            normal(b - 1, 1)
            def route(c):
                half = slice(c * HB, c * HB + HB)
                lg, m8, gt, eq, pf, ex = (v[:, half, :] for v in (LG4, M84, GT4, EQ4, PF4, EX4))
                c4, s4, cp, rm = C4[:, half], S4[:, half], CP[:, half], RM4[:, half, :]
                s8 = [P, HB, E1]

                def first():
                    if c == 1:
                        lk[0] += 1
                        dve.wait_ge(ln_pow, lk[0])
                    dve.wait_ge(lg_pe, 2 + c)
                    done(dve.tensor_tensor(lg, PS[:, 2, c * HB * E1:(c + 1) * HB * E1]
                                           .rearrange("p (b e) -> p b e", b=HB), bc(RS[:, half], s8, 2), ALU.mult))
                    for b in range(HB):
                        ins = dve.max(m8[:, b, :], lg[:, b, :])
                    done(ins)
                    dve.tensor_tensor(eq, lg, bc(m8[:, :, TOPK1 - 1], s8, 2), ALU.is_equal)
                    done(dve.tensor_tensor(gt, lg, bc(m8[:, :, TOPK1 - 1], s8, 2), ALU.is_gt))
                    dve.tensor_tensor(lg, lg, bc(m8[:, :, 0], s8, 2), ALU.subtract).then_inc(ss4_ok, 1)

                def second():
                    done(dve.tensor_reduce(c4, gt, AX, ALU.add))
                    done(dve.tensor_scalar(c4, c4, -1.0, float(TOPK1), ALU.mult, ALU.add))
                    done(dve.tensor_tensor_scan(pf.rearrange(fl), rm.rearrange(fl), eq.rearrange(fl), 0.0,
                                                ALU.mult, ALU.add))
                    done(dve.tensor_tensor(pf, pf, bc(c4, s8, 2), ALU.is_le))
                    done(dve.tensor_tensor(eq, eq, pf, ALU.mult))
                    done(dve.tensor_tensor(gt, gt, eq, ALU.add))

                def third():
                    dve.wait_ge(ex4_ok, c + 1)
                    done(dve.tensor_tensor(ex, ex, gt, ALU.mult))
                    done(dve.tensor_reduce(s4, ex, AX, ALU.add))
                    done(dve.reciprocal(s4, s4))
                    done(dve.tensor_tensor(ex, ex, bc(s4, s8, 2), ALU.mult))
                    done(dve.tensor_copy(cp[:, :, 0, :], ex))
                    done(dve.tensor_tensor(ex, ex, cp[:, :, 0, :], ALU.subtract))
                    done(dve.tensor_copy(cp[:, :, 1, :], ex))
                    dve.tensor_tensor(cp[:, :, 2, :], ex, cp[:, :, 1, :], ALU.subtract).then_inc(c_ok, 1)
                return [first, second, third]

            lk[0] += 1
            dve.wait_ge(ln_pow, lk[0])
            dve.wait_ge(x3_ok, B - 1)
            stats([B - 2])
            apply([B - 2])
            steps = route(0)
            steps.pop(0)()
            normal(B - 1, 0)
            steps.pop(0)()
            normal(B - 1, 1)
            steps.pop(0)()
            dve.wait_ge(x3_ok, B)
            stats([B - 1])
            for u in range(2 * E1):
                dve.wait_ge(cb_ok, u + 1)
                dve.wait_ge(a_pe, u + 1)
                if u >= 2:
                    dve.wait_ge(o_pe, u - 1)
                dve.tensor_tensor(AE[:, u % 2, :], PS[:, 4 + u % 2, :], CB[:, u % 2, :], ALU.mult)\
                    .then_inc(ae_ok, 1)
                if u == 0:
                    apply([B - 1])
                if u == 2:
                    asknorm(1)
                    steps = route(1)
                if 3 <= u < 6:
                    steps.pop(0)()
                if u % E1 == E1 - 1:
                    c = u // E1
                    dve.wait_ge(o_pe, E1 * (c + 1))
                    for g in range(2):
                        v = X[:, 4 * c + 2 * g:4 * c + 2 * g + 2, :].rearrange("p b l -> p (b l)")
                        dve.scalar_tensor_tensor(out=v, in0=PS[:, 2 * c + g, :], scalar=TGT[:, 3:4], in1=v,
                                                 op0=ALU.mult, op1=ALU.add).then_inc(o_ok, 1)


_INS = ['x', 'ctx_2048', 'g_xattn', 'g_ffn', 'L0_xattn_ssm_kernel', 'L0_xattn_D', 'L0_ffn_gate_w',
        'L0_ffn_w_gate_up', 'L0_ffn_w_down', 'L0_ffn_ws_gate_up', 'L0_ffn_ws_down', 'L1_xattn_encoding',
        'L1_xattn_Wq', 'L1_xattn_bq', 'L1_xattn_Wk', 'L1_xattn_bk', 'L1_xattn_Wv', 'L1_xattn_bv',
        'L1_xattn_Wm', 'L1_xattn_bm', 'L1_ffn_router_w', 'L1_ffn_Wa', 'L1_ffn_Wb']
_OUTS = [((8, 128, 256), 'float32')]


def kernel(**inputs):
    import numpy as _np
    import concourse.bacc as _bacc
    from concourse import mybir as _mybir
    from concourse.bass_utils import run_bass_kernel_spmd as _run

    nc = _bacc.Bacc("TRN2", target_bir_lowering=False, num_devices=1)
    arrays, args = {}, []
    for name in _INS:
        a = _np.ascontiguousarray(inputs[name])
        arrays[f"in_{name}_dram"] = a
        args.append(nc.dram_tensor(f"in_{name}_dram", a.shape, _mybir.dt.from_np(a.dtype), kind="ExternalInput").ap())
    for i, (shape, dtype) in enumerate(_OUTS):
        dt = _mybir.dt.from_np(_np.dtype(dtype))
        args.append(nc.dram_tensor(f"out_{i}_dram", shape, dt, kind="ExternalOutput").ap())
    build(nc, *args)
    r = _run(nc, [arrays], core_ids=[0])
    return r.results[0]["out_0_dram"]
```
